# Optimizing a Trainium2 kernel written in Bass

```python
import numpy as np
import jax
import jax.numpy as jnp

def _softmax(x, axis=-1):
    return jax.nn.softmax(x, axis=axis)

def _gelu(x):
    return jax.nn.gelu(x, approximate=True)

def _silu(x):
    return jax.nn.silu(x)

def _sigmoid(x):
    return jax.nn.sigmoid(x)

def _layernorm(x, axis=-1, eps=1e-05):
    m = jnp.mean(x, axis=axis, keepdims=True)
    v = jnp.var(x, axis=axis, keepdims=True)
    return (x - m) / jnp.sqrt(v + eps)

def _scatter_add(tgt, idx, src, axis=0):
    return tgt.at[idx].add(src)

def _segment_sum(src, seg, n):
    return jax.ops.segment_sum(src, seg, n)
kernel_name = 'mk_perceiver_d2_seqx_r4_5a7609'

def setup_inputs(seed: int=0):
    np.random.seed(seed)
    _w = jnp.asarray

    def _rec_inputs():
        import jax
        import jax.numpy as jnp
        _rk = jax.random.key(seed)
        x = -0.0002928 + 1 * jax.random.normal(jax.random.fold_in(_rk, 1), (8, 64, 256), jnp.float32)
        _lenS = 64 - jax.random.randint(jax.random.fold_in(_rk, 7), (8,), 0, max(1, 64 // 4) + 1, jnp.int32)
        _lenS2 = 1601 - jax.random.randint(jax.random.fold_in(_rk, 8), (8,), 0, max(1, 1601 // 4) + 1, jnp.int32)
        _ctx_1024P = jax.random.normal(jax.random.fold_in(_rk, 11), (8, 16, 256), jnp.float32)
        _ctx_1024c = jax.random.dirichlet(jax.random.fold_in(_rk, 511), 0.3 * jnp.ones((16,), jnp.float32), (8, 1601))
        _ctx_1024t = jnp.einsum('bsk,bkd->bsd', _ctx_1024c, _ctx_1024P)
        _ctx_1024t = _ctx_1024t * jax.lax.rsqrt(jnp.mean(jnp.square(_ctx_1024t)) + 1e-12) * 0.953939
        ctx_1024 = -1.52775e-05 + 0.999936 * (_ctx_1024t + 0.3 * jax.random.normal(jax.random.fold_in(_rk, 611), (8, 1601, 256), jnp.float32))
        return (x, ctx_1024)
    x, ctx_1024 = _rec_inputs()

    def _L0_xattn_setup():
        import jax, jax.numpy as jnp
        import numpy as np
        DIM = 256
        NUM_HEADS = 8
        HEAD_DIM = 64
        INNER = NUM_HEADS * HEAD_DIM
        key = jax.random.key(seed)
        ks = jax.random.split(key, 7)
        B, N, M = (8, 128, 1024)
        x = jax.random.normal(ks[0], (B, N, DIM), dtype=jnp.float32)
        context = jax.random.normal(ks[1], (B, M, DIM), dtype=jnp.float32)
        s_in = 1.0 / np.sqrt(DIM)
        s_inner = 1.0 / np.sqrt(INNER)
        Wq = jax.random.normal(ks[2], (DIM, INNER), dtype=jnp.float32) * s_in
        Wk = jax.random.normal(ks[3], (DIM, INNER), dtype=jnp.float32) * s_in
        Wv = jax.random.normal(ks[4], (DIM, INNER), dtype=jnp.float32) * s_in
        Wo = jax.random.normal(ks[5], (INNER, DIM), dtype=jnp.float32) * s_inner
        bo = jax.random.normal(ks[6], (DIM,), dtype=jnp.float32) * 0.01
        return {'x': x, 'context': context, 'Wq': Wq, 'Wk': Wk, 'Wv': Wv, 'Wo': Wo, 'bo': bo}
    _L0_xattn_all = _L0_xattn_setup()
    _L0_xattn_in = {k: v for k, v in _L0_xattn_all.items() if k in ('Wq', 'Wk', 'Wv', 'Wo', 'bo')}
    del _L0_xattn_all

    def _L0_attn_setup():
        import jax, jax.numpy as jnp
        import numpy as np
        B, S, D, H = (2, 256, 256, 16)
        DH = D // H
        BW = 128
        K = 4
        _EPS = 1e-06

        def _rmsnorm(x, w):
            return x * jax.lax.rsqrt(jnp.mean(x * x, axis=-1, keepdims=True) + _EPS) * w

        def _l2norm(x):
            return x * jax.lax.rsqrt(jnp.sum(x * x, axis=-1, keepdims=True) + _EPS)

        def _causal_dwconv_silu(x, w):
            k = w.shape[1]
            xp = jnp.pad(x, ((0, 0), (k - 1, 0), (0, 0)))
            mixed = sum((xp[:, i:i + x.shape[1], :] * w[:, i] for i in range(k)))
            return jax.nn.silu(mixed)

        def _forward(hidden, cond_in_W, rot_theta, cond_norm_w, delta_W, qkv_ramp_logit, beta_ramp_logit, ctrl_W, ctrl_b, q_conv_w, k_conv_w, v_conv_w, out_norm_w, out_proj_W, out_proj_b):
            b, s, d = hidden.shape
            h = beta_ramp_logit.shape[0]
            dh = d // h
            p = hidden @ cond_in_W
            bw = p.shape[-1]
            p2 = jnp.moveaxis(p.reshape(b, s, bw // 2, 2), 1, 0)
            c, sn = (jnp.cos(rot_theta), jnp.sin(rot_theta))

            def rot_step(carry, xt):
                s0, s1 = (carry[..., 0], carry[..., 1])
                new = jnp.stack([c * s0 - sn * s1 + xt[..., 0], sn * s0 + c * s1 + xt[..., 1]], axis=-1)
                return (new, new)
            init = jnp.zeros((b, bw // 2, 2), hidden.dtype)
            _, states = jax.lax.scan(rot_step, init, p2)
            cond = _rmsnorm(jnp.moveaxis(states, 0, 1).reshape(b, s, bw), cond_norm_w)
            deltas = cond @ delta_W
            qd, kd, vd, bd = jnp.split(deltas, [d, 2 * d, 3 * d], axis=-1)
            ramp = jax.nn.sigmoid(qkv_ramp_logit)
            qd = qd * ramp[0]
            kd = kd * ramp[1]
            vd = vd * ramp[2]
            bd = bd * jax.nn.sigmoid(beta_ramp_logit)
            ctrl = hidden @ ctrl_W + ctrl_b
            q_l, k_l, v_l, dec_l, bet_l, gate_l = jnp.split(ctrl, [d, 2 * d, 3 * d, 3 * d + h, 3 * d + 2 * h], axis=-1)
            q = _causal_dwconv_silu(q_l + qd, q_conv_w).reshape(b, s, h, dh)
            k = _causal_dwconv_silu(k_l + kd, k_conv_w).reshape(b, s, h, dh)
            v = _causal_dwconv_silu(v_l + vd, v_conv_w).reshape(b, s, h, dh)
            q, k = (_l2norm(q), _l2norm(k))
            beta = jax.nn.sigmoid(bet_l + bd)
            g = jax.nn.sigmoid(dec_l)

            def step(Sst, inp):
                qt, kt, vt, bt, gt = inp
                Sd = gt[..., None, None] * Sst
                kS = jnp.einsum('bhk,bhkv->bhv', kt, Sd)
                Snew = Sd + jnp.einsum('bhk,bhv->bhkv', kt, bt[..., None] * (vt - kS))
                ot = jnp.einsum('bhk,bhkv->bhv', qt, Snew)
                return (Snew, ot)
            xs = tuple((jnp.moveaxis(a, 1, 0) for a in (q, k, v, beta, g)))
            S0 = jnp.zeros((b, h, dh, dh), hidden.dtype)
            _, o = jax.lax.scan(step, S0, xs)
            o = jnp.moveaxis(o, 0, 1)
            gate = gate_l.reshape(b, s, h, dh)
            o = _rmsnorm(o, out_norm_w) * jax.nn.silu(gate)
            return o.reshape(b, s, d) @ out_proj_W.T + out_proj_b
        key = jax.random.key(seed)
        ks = jax.random.split(key, 12)
        n = lambda k, shp, s=0.02: jax.random.normal(k, shp, jnp.float32) * s
        logit001 = float(np.log(0.01 / 0.99))
        ctrl_b = np.zeros(3 * D + 2 * H + D, np.float32)
        ctrl_b[3 * D:3 * D + H] = 1.5
        ctrl_b[3 * D + H:3 * D + 2 * H] = -2.0
        ctrl_b[3 * D + 2 * H:] = -1.5
        conv_base = np.zeros((D, K), np.float32)
        conv_base[:, -1] = 1.0
        return {'hidden': jax.random.normal(ks[0], (B, S, D), jnp.float32), 'cond_in_W': n(ks[1], (D, BW)), 'rot_theta': jax.random.uniform(ks[2], (BW // 2,), jnp.float32, 0.0, 0.5), 'cond_norm_w': jnp.ones((BW,), jnp.float32), 'delta_W': n(ks[3], (BW, 3 * D + H)), 'qkv_ramp_logit': jnp.full((3, D), logit001, jnp.float32), 'beta_ramp_logit': jnp.full((H,), logit001, jnp.float32), 'ctrl_W': n(ks[4], (D, 3 * D + 2 * H + D)), 'ctrl_b': jnp.asarray(ctrl_b), 'q_conv_w': jnp.asarray(conv_base) + n(ks[5], (D, K), 0.05), 'k_conv_w': jnp.asarray(conv_base) + n(ks[6], (D, K), 0.05), 'v_conv_w': jnp.asarray(conv_base) + n(ks[7], (D, K), 0.05), 'out_norm_w': jnp.ones((DH,), jnp.float32), 'out_proj_W': n(ks[8], (D, D)), 'out_proj_b': jnp.zeros((D,), jnp.float32)}
    _L0_attn_all = _L0_attn_setup()
    _L0_attn_in = {k: v for k, v in _L0_attn_all.items() if k in ('cond_in_W', 'rot_theta', 'cond_norm_w', 'delta_W', 'qkv_ramp_logit', 'beta_ramp_logit', 'ctrl_W', 'ctrl_b', 'q_conv_w', 'k_conv_w', 'v_conv_w', 'out_norm_w', 'out_proj_W', 'out_proj_b')}
    del _L0_attn_all

    def _L0_ffn_setup():
        import jax, jax.numpy as jnp
        import numpy as np
        B, F, D, H, E, K = (4, 512, 256, 512, 8, 2)
        key = jax.random.key(seed)
        ks = jax.random.split(key, 9)
        sc = lambda k, shape, fan_in: jax.random.normal(k, shape, jnp.float32) * fan_in ** (-0.5)
        return {'x': jax.random.normal(ks[0], (B, F, D), jnp.float32), 'rw1': sc(ks[1], (D, D), D), 'rb1': jnp.zeros((D,), jnp.float32), 'rw2': sc(ks[2], (D, E), D), 'rb2': jnp.zeros((E,), jnp.float32), 'ew1': sc(ks[3], (E, D, H), D), 'eb1': jnp.zeros((E, H), jnp.float32), 'ew2': sc(ks[4], (E, H, D), H), 'eb2': jnp.zeros((E, D), jnp.float32)}
    _L0_ffn_all = _L0_ffn_setup()
    _L0_ffn_in = {k: v for k, v in _L0_ffn_all.items() if k in ('rw1', 'rb1', 'rw2', 'rb2', 'ew1', 'eb1', 'ew2', 'eb2')}
    del _L0_ffn_all

    def _L1_xattn_setup():
        import jax, jax.numpy as jnp
        import numpy as np
        DIM = 256
        N_HEADS = 16
        HEAD_DIM = DIM // N_HEADS
        GAMMA = 10.0

        def larope_cos_sin(seq_len, gamma, head_dim):
            inv_freq = 1.0 / 10000.0 ** (jnp.arange(0, head_dim, 2, dtype=jnp.float32) / head_dim)
            t = jnp.arange(seq_len, dtype=jnp.float32)
            freqs = jnp.outer(gamma * (t / seq_len), inv_freq)
            emb = jnp.concatenate([freqs, freqs], axis=-1)
            return (jnp.cos(emb), jnp.sin(emb))

        def apply_rope(x, cos, sin):
            d = x.shape[-1] // 2
            x1, x2 = (x[..., :d], x[..., d:])
            c = cos[None, None, :, :d]
            s = sin[None, None, :, :d]
            return jnp.concatenate([x1 * c - x2 * s, x1 * s + x2 * c], axis=-1)
        key = jax.random.key(seed)
        ks = jax.random.split(key, 11)
        B, Lq, Lk = (4, 512, 256)
        std = 1.0 / np.sqrt(DIM)
        inp = {'query': jax.random.normal(ks[0], (B, Lq, DIM), dtype=jnp.float32), 'key': jax.random.normal(ks[1], (B, Lk, DIM), dtype=jnp.float32), 'value': jax.random.normal(ks[2], (B, Lk, DIM), dtype=jnp.float32), 'Wq': jax.random.normal(ks[3], (DIM, DIM), dtype=jnp.float32) * std, 'bq': jnp.zeros((DIM,), dtype=jnp.float32), 'Wk': jax.random.normal(ks[4], (DIM, DIM), dtype=jnp.float32) * std, 'bk': jnp.zeros((DIM,), dtype=jnp.float32), 'Wv': jax.random.normal(ks[5], (DIM, DIM), dtype=jnp.float32) * std, 'bv': jnp.zeros((DIM,), dtype=jnp.float32), 'Wo': jax.random.normal(ks[6], (DIM, DIM), dtype=jnp.float32) * std, 'bo': jnp.zeros((DIM,), dtype=jnp.float32)}
        return inp
    _L1_xattn_all = _L1_xattn_setup()
    _L1_xattn_in = {k: v for k, v in _L1_xattn_all.items() if k in ('Wq', 'bq', 'Wk', 'bk', 'Wv', 'bv', 'Wo', 'bo')}
    del _L1_xattn_all

    def _L1_attn_setup():
        import jax, jax.numpy as jnp
        import numpy as np
        B, N, E, H = (2, 512, 256, 8)
        HID = 256
        D = HID // H
        EPS = 1e-08

        def rms_norm(x, scale):
            rms = jnp.linalg.norm(x, axis=-1, keepdims=True) * x.shape[-1] ** (-0.5)
            return scale * (x / (rms + EPS))
        key = jax.random.key(seed)
        ks = jax.random.split(key, 12)
        s = 0.02
        return {'x': jax.random.normal(ks[0], (B, N, E), jnp.float32), 'Wq': jax.random.normal(ks[1], (HID, E), jnp.float32) * s, 'bq': jnp.zeros((HID,), jnp.float32), 'Wk': jax.random.normal(ks[2], (HID, E), jnp.float32) * s, 'bk': jnp.zeros((HID,), jnp.float32), 'Wv': jax.random.normal(ks[3], (HID, E), jnp.float32) * s, 'bv': jnp.zeros((HID,), jnp.float32), 'Wu': jax.random.normal(ks[4], (HID, E), jnp.float32) * s, 'bu': jnp.zeros((HID,), jnp.float32), 'Wo': jax.random.normal(ks[5], (E, HID), jnp.float32) * s, 'bo': jnp.zeros((E,), jnp.float32), 'scale': jnp.ones((HID,), jnp.float32)}
    _L1_attn_all = _L1_attn_setup()
    _L1_attn_in = {k: v for k, v in _L1_attn_all.items() if k in ('Wq', 'bq', 'Wk', 'bk', 'Wv', 'bv', 'Wu', 'bu', 'Wo', 'bo', 'scale')}
    del _L1_attn_all

    def _L1_ffn_setup():
        import jax, jax.numpy as jnp
        import numpy as np
        H, I, E_ROUTED, TOP_K = (256, 704, 7, 2)
        B, S = (4, 512)

        def _expert(h, g, u, d):
            return jnp.einsum('...i,hi->...h', jax.nn.silu(h @ g.T) * (h @ u.T), d)
        key = jax.random.key(seed)
        ks = jax.random.split(key, 10)
        sc = 0.02
        return {'x': jax.random.normal(ks[0], (B, S, H), dtype=jnp.float32), 'sg': jax.random.normal(ks[1], (I, H), dtype=jnp.float32) * sc, 'su': jax.random.normal(ks[2], (I, H), dtype=jnp.float32) * sc, 'sd': jax.random.normal(ks[3], (H, I), dtype=jnp.float32) * sc, 'rg': jax.random.normal(ks[4], (E_ROUTED, I, H), dtype=jnp.float32) * sc, 'ru': jax.random.normal(ks[5], (E_ROUTED, I, H), dtype=jnp.float32) * sc, 'rd': jax.random.normal(ks[6], (E_ROUTED, H, I), dtype=jnp.float32) * sc, 'wr': jax.random.normal(ks[7], (E_ROUTED, H), dtype=jnp.float32) * sc, 'rb': jnp.zeros((E_ROUTED,), dtype=jnp.float32)}
    _L1_ffn_all = _L1_ffn_setup()
    _L1_ffn_in = {k: v for k, v in _L1_ffn_all.items() if k in ('sg', 'su', 'sd', 'rg', 'ru', 'rd', 'wr', 'rb')}
    del _L1_ffn_all
    return {'x': x, 'ctx_1024': ctx_1024, 'L0_xattn_Wq': _L0_xattn_in['Wq'], 'L0_xattn_Wk': _L0_xattn_in['Wk'], 'L0_xattn_Wv': _L0_xattn_in['Wv'], 'L0_xattn_Wo': _L0_xattn_in['Wo'], 'L0_xattn_bo': _L0_xattn_in['bo'], 'L0_attn_cond_in_W': _L0_attn_in['cond_in_W'], 'L0_attn_rot_theta': _L0_attn_in['rot_theta'], 'L0_attn_cond_norm_w': _L0_attn_in['cond_norm_w'], 'L0_attn_delta_W': _L0_attn_in['delta_W'], 'L0_attn_qkv_ramp_logit': _L0_attn_in['qkv_ramp_logit'], 'L0_attn_beta_ramp_logit': _L0_attn_in['beta_ramp_logit'], 'L0_attn_ctrl_W': _L0_attn_in['ctrl_W'], 'L0_attn_ctrl_b': _L0_attn_in['ctrl_b'], 'L0_attn_q_conv_w': _L0_attn_in['q_conv_w'], 'L0_attn_k_conv_w': _L0_attn_in['k_conv_w'], 'L0_attn_v_conv_w': _L0_attn_in['v_conv_w'], 'L0_attn_out_norm_w': _L0_attn_in['out_norm_w'], 'L0_attn_out_proj_W': _L0_attn_in['out_proj_W'], 'L0_attn_out_proj_b': _L0_attn_in['out_proj_b'], 'L0_ffn_rw1': _L0_ffn_in['rw1'], 'L0_ffn_rb1': _L0_ffn_in['rb1'], 'L0_ffn_rw2': _L0_ffn_in['rw2'], 'L0_ffn_rb2': _L0_ffn_in['rb2'], 'L0_ffn_ew1': _L0_ffn_in['ew1'], 'L0_ffn_eb1': _L0_ffn_in['eb1'], 'L0_ffn_ew2': _L0_ffn_in['ew2'], 'L0_ffn_eb2': _L0_ffn_in['eb2'], 'L1_xattn_Wq': _L1_xattn_in['Wq'], 'L1_xattn_bq': _L1_xattn_in['bq'], 'L1_xattn_Wk': _L1_xattn_in['Wk'], 'L1_xattn_bk': _L1_xattn_in['bk'], 'L1_xattn_Wv': _L1_xattn_in['Wv'], 'L1_xattn_bv': _L1_xattn_in['bv'], 'L1_xattn_Wo': _L1_xattn_in['Wo'], 'L1_xattn_bo': _L1_xattn_in['bo'], 'L1_attn_Wq': _L1_attn_in['Wq'], 'L1_attn_bq': _L1_attn_in['bq'], 'L1_attn_Wk': _L1_attn_in['Wk'], 'L1_attn_bk': _L1_attn_in['bk'], 'L1_attn_Wv': _L1_attn_in['Wv'], 'L1_attn_bv': _L1_attn_in['bv'], 'L1_attn_Wu': _L1_attn_in['Wu'], 'L1_attn_bu': _L1_attn_in['bu'], 'L1_attn_Wo': _L1_attn_in['Wo'], 'L1_attn_bo': _L1_attn_in['bo'], 'L1_attn_scale': _L1_attn_in['scale'], 'L1_ffn_sg': _L1_ffn_in['sg'], 'L1_ffn_su': _L1_ffn_in['su'], 'L1_ffn_sd': _L1_ffn_in['sd'], 'L1_ffn_rg': _L1_ffn_in['rg'], 'L1_ffn_ru': _L1_ffn_in['ru'], 'L1_ffn_rd': _L1_ffn_in['rd'], 'L1_ffn_wr': _L1_ffn_in['wr'], 'L1_ffn_rb': _L1_ffn_in['rb']}

def reference(x, ctx_1024, L0_xattn_Wq, L0_xattn_Wk, L0_xattn_Wv, L0_xattn_Wo, L0_xattn_bo, L0_attn_cond_in_W, L0_attn_rot_theta, L0_attn_cond_norm_w, L0_attn_delta_W, L0_attn_qkv_ramp_logit, L0_attn_beta_ramp_logit, L0_attn_ctrl_W, L0_attn_ctrl_b, L0_attn_q_conv_w, L0_attn_k_conv_w, L0_attn_v_conv_w, L0_attn_out_norm_w, L0_attn_out_proj_W, L0_attn_out_proj_b, L0_ffn_rw1, L0_ffn_rb1, L0_ffn_rw2, L0_ffn_rb2, L0_ffn_ew1, L0_ffn_eb1, L0_ffn_ew2, L0_ffn_eb2, L1_xattn_Wq, L1_xattn_bq, L1_xattn_Wk, L1_xattn_bk, L1_xattn_Wv, L1_xattn_bv, L1_xattn_Wo, L1_xattn_bo, L1_attn_Wq, L1_attn_bq, L1_attn_Wk, L1_attn_bk, L1_attn_Wv, L1_attn_bv, L1_attn_Wu, L1_attn_bu, L1_attn_Wo, L1_attn_bo, L1_attn_scale, L1_ffn_sg, L1_ffn_su, L1_ffn_sd, L1_ffn_rg, L1_ffn_ru, L1_ffn_rd, L1_ffn_wr, L1_ffn_rb):
    import jax
    import jax.numpy as jnp

    def _L0_xattn_ref(x, context, Wq, Wk, Wv, Wo, bo):
        import jax, jax.numpy as jnp
        import numpy as np
        DIM = 256
        NUM_HEADS = 8
        HEAD_DIM = 64
        INNER = NUM_HEADS * HEAD_DIM
        B, N, _ = x.shape
        M = context.shape[1]
        scale = HEAD_DIM ** (-0.5)
        q = (x @ Wq).reshape(B, N, NUM_HEADS, HEAD_DIM).transpose(0, 2, 1, 3)
        k = (context @ Wk).reshape(B, M, NUM_HEADS, HEAD_DIM).transpose(0, 2, 1, 3)
        v = (context @ Wv).reshape(B, M, NUM_HEADS, HEAD_DIM).transpose(0, 2, 1, 3)
        attn = jax.nn.softmax(jnp.einsum('bhnd,bhmd->bhnm', q, k) * scale, axis=-1)
        out = jnp.einsum('bhnm,bhmd->bhnd', attn, v)
        out = out.transpose(0, 2, 1, 3).reshape(B, N, INNER)
        return out @ Wo + bo

    def _L0_attn_ref(hidden, cond_in_W, rot_theta, cond_norm_w, delta_W, qkv_ramp_logit, beta_ramp_logit, ctrl_W, ctrl_b, q_conv_w, k_conv_w, v_conv_w, out_norm_w, out_proj_W, out_proj_b):
        import jax, jax.numpy as jnp
        import numpy as np
        B, S, D, H = (2, 256, 256, 16)
        DH = D // H
        BW = 128
        K = 4
        _EPS = 1e-06

        def _rmsnorm(x, w):
            return x * jax.lax.rsqrt(jnp.mean(x * x, axis=-1, keepdims=True) + _EPS) * w

        def _l2norm(x):
            return x * jax.lax.rsqrt(jnp.sum(x * x, axis=-1, keepdims=True) + _EPS)

        def _causal_dwconv_silu(x, w):
            k = w.shape[1]
            xp = jnp.pad(x, ((0, 0), (k - 1, 0), (0, 0)))
            mixed = sum((xp[:, i:i + x.shape[1], :] * w[:, i] for i in range(k)))
            return jax.nn.silu(mixed)

        def _forward(hidden, cond_in_W, rot_theta, cond_norm_w, delta_W, qkv_ramp_logit, beta_ramp_logit, ctrl_W, ctrl_b, q_conv_w, k_conv_w, v_conv_w, out_norm_w, out_proj_W, out_proj_b):
            b, s, d = hidden.shape
            h = beta_ramp_logit.shape[0]
            dh = d // h
            p = hidden @ cond_in_W
            bw = p.shape[-1]
            p2 = jnp.moveaxis(p.reshape(b, s, bw // 2, 2), 1, 0)
            c, sn = (jnp.cos(rot_theta), jnp.sin(rot_theta))

            def rot_step(carry, xt):
                s0, s1 = (carry[..., 0], carry[..., 1])
                new = jnp.stack([c * s0 - sn * s1 + xt[..., 0], sn * s0 + c * s1 + xt[..., 1]], axis=-1)
                return (new, new)
            init = jnp.zeros((b, bw // 2, 2), hidden.dtype)
            _, states = jax.lax.scan(rot_step, init, p2)
            cond = _rmsnorm(jnp.moveaxis(states, 0, 1).reshape(b, s, bw), cond_norm_w)
            deltas = cond @ delta_W
            qd, kd, vd, bd = jnp.split(deltas, [d, 2 * d, 3 * d], axis=-1)
            ramp = jax.nn.sigmoid(qkv_ramp_logit)
            qd = qd * ramp[0]
            kd = kd * ramp[1]
            vd = vd * ramp[2]
            bd = bd * jax.nn.sigmoid(beta_ramp_logit)
            ctrl = hidden @ ctrl_W + ctrl_b
            q_l, k_l, v_l, dec_l, bet_l, gate_l = jnp.split(ctrl, [d, 2 * d, 3 * d, 3 * d + h, 3 * d + 2 * h], axis=-1)
            q = _causal_dwconv_silu(q_l + qd, q_conv_w).reshape(b, s, h, dh)
            k = _causal_dwconv_silu(k_l + kd, k_conv_w).reshape(b, s, h, dh)
            v = _causal_dwconv_silu(v_l + vd, v_conv_w).reshape(b, s, h, dh)
            q, k = (_l2norm(q), _l2norm(k))
            beta = jax.nn.sigmoid(bet_l + bd)
            g = jax.nn.sigmoid(dec_l)

            def step(Sst, inp):
                qt, kt, vt, bt, gt = inp
                Sd = gt[..., None, None] * Sst
                kS = jnp.einsum('bhk,bhkv->bhv', kt, Sd)
                Snew = Sd + jnp.einsum('bhk,bhv->bhkv', kt, bt[..., None] * (vt - kS))
                ot = jnp.einsum('bhk,bhkv->bhv', qt, Snew)
                return (Snew, ot)
            xs = tuple((jnp.moveaxis(a, 1, 0) for a in (q, k, v, beta, g)))
            S0 = jnp.zeros((b, h, dh, dh), hidden.dtype)
            _, o = jax.lax.scan(step, S0, xs)
            o = jnp.moveaxis(o, 0, 1)
            gate = gate_l.reshape(b, s, h, dh)
            o = _rmsnorm(o, out_norm_w) * jax.nn.silu(gate)
            return o.reshape(b, s, d) @ out_proj_W.T + out_proj_b
        return _forward(hidden, cond_in_W, rot_theta, cond_norm_w, delta_W, qkv_ramp_logit, beta_ramp_logit, ctrl_W, ctrl_b, q_conv_w, k_conv_w, v_conv_w, out_norm_w, out_proj_W, out_proj_b)

    def _L0_ffn_ref(x, rw1, rb1, rw2, rb2, ew1, eb1, ew2, eb2):
        import jax, jax.numpy as jnp
        import numpy as np
        B, F, D, H, E, K = (4, 512, 256, 512, 8, 2)
        b, f, d = x.shape
        t = x.reshape(b * f, d)
        logits = jax.nn.silu(t @ rw1 + rb1) @ rw2 + rb2
        vals, idx = jax.lax.top_k(logits, K)
        rows = jnp.arange(t.shape[0])[:, None]
        masked = jnp.full_like(logits, -jnp.inf).at[rows, idx].set(vals)
        w = jax.nn.softmax(masked, axis=1)
        eh = jax.nn.silu(jnp.einsum('td,edh->teh', t, ew1) + eb1[None])
        eo = jnp.einsum('teh,ehd->ted', eh, ew2) + eb2[None]
        y = t + jnp.einsum('te,ted->td', w, eo)
        return y.reshape(b, f, d)

    def _L1_xattn_ref(query, key, value, Wq, bq, Wk, bk, Wv, bv, Wo, bo):
        import jax, jax.numpy as jnp
        import numpy as np
        DIM = 256
        N_HEADS = 16
        HEAD_DIM = DIM // N_HEADS
        GAMMA = 10.0

        def larope_cos_sin(seq_len, gamma, head_dim):
            inv_freq = 1.0 / 10000.0 ** (jnp.arange(0, head_dim, 2, dtype=jnp.float32) / head_dim)
            t = jnp.arange(seq_len, dtype=jnp.float32)
            freqs = jnp.outer(gamma * (t / seq_len), inv_freq)
            emb = jnp.concatenate([freqs, freqs], axis=-1)
            return (jnp.cos(emb), jnp.sin(emb))

        def apply_rope(x, cos, sin):
            d = x.shape[-1] // 2
            x1, x2 = (x[..., :d], x[..., d:])
            c = cos[None, None, :, :d]
            s = sin[None, None, :, :d]
            return jnp.concatenate([x1 * c - x2 * s, x1 * s + x2 * c], axis=-1)
        B, Lq, _ = query.shape
        Lk = key.shape[1]
        scale = HEAD_DIM ** (-0.5)

        def proj(x, W, b, L):
            y = x @ W.T + b
            return y.reshape(B, L, N_HEADS, HEAD_DIM).transpose(0, 2, 1, 3)
        q = proj(query, Wq, bq, Lq)
        k = proj(key, Wk, bk, Lk)
        v = proj(value, Wv, bv, Lk)
        q_cos, q_sin = larope_cos_sin(Lq, GAMMA, HEAD_DIM)
        k_cos, k_sin = larope_cos_sin(Lk, GAMMA, HEAD_DIM)
        q = apply_rope(q, q_cos, q_sin)
        k = apply_rope(k, k_cos, k_sin)
        scores = jnp.einsum('bhqd,bhkd->bhqk', q, k) * scale
        attn = jax.nn.softmax(scores, axis=-1)
        out = jnp.einsum('bhqk,bhkd->bhqd', attn, v)
        out = out.transpose(0, 2, 1, 3).reshape(B, Lq, DIM)
        return out @ Wo.T + bo

    def _L1_attn_ref(x, Wq, bq, Wk, bk, Wv, bv, Wu, bu, Wo, bo, scale):
        import jax, jax.numpy as jnp
        import numpy as np
        B, N, E, H = (2, 512, 256, 8)
        HID = 256
        D = HID // H
        EPS = 1e-08

        def rms_norm(x, scale):
            rms = jnp.linalg.norm(x, axis=-1, keepdims=True) * x.shape[-1] ** (-0.5)
            return scale * (x / (rms + EPS))
        n = x.shape[-2]
        q = x @ Wq.T + bq
        u = x @ Wu.T + bu
        k = x @ Wk.T + bk
        v = x @ Wv.T + bv
        u = jax.nn.silu(u)
        v = jax.nn.silu(v)
        to_heads = lambda t: t.reshape(*t.shape[:-1], H, D).swapaxes(-3, -2)
        q, k, v = map(to_heads, (q, k, v))
        q = jax.nn.elu(q)
        k = jax.nn.elu(k)
        mask = jnp.tril(jnp.ones((n, n), q.dtype))
        energy = jnp.einsum('bhnd,bhmd->bhnm', q, k) * mask
        out = jnp.einsum('bhnm,bhmd->bhnd', energy, v)
        out = out.swapaxes(-3, -2).reshape(*x.shape[:-1], HID)
        out = rms_norm(out, scale)
        out = u * out
        return out @ Wo.T + bo

    def _L1_ffn_ref(x, sg, su, sd, rg, ru, rd, wr, rb):
        import jax, jax.numpy as jnp
        import numpy as np
        H, I, E_ROUTED, TOP_K = (256, 704, 7, 2)
        B, S = (4, 512)

        def _expert(h, g, u, d):
            return jnp.einsum('...i,hi->...h', jax.nn.silu(h @ g.T) * (h @ u.T), d)
        shared_out = _expert(x, sg, su, sd)
        logits = x @ wr.T + rb
        probs = jax.nn.softmax(logits, axis=-1)
        scores, idx = jax.lax.top_k(probs, TOP_K)
        scores = scores / scores.sum(axis=-1, keepdims=True)
        w = jnp.sum(scores[..., None] * jax.nn.one_hot(idx, E_ROUTED, dtype=x.dtype), axis=-2)
        out = shared_out
        for e in range(E_ROUTED):
            out = out + w[..., e:e + 1] * _expert(x, rg[e], ru[e], rd[e])
        return out
    x = x + _L0_xattn_ref(_layernorm(x, axis=-1), ctx_1024, L0_xattn_Wq, L0_xattn_Wk, L0_xattn_Wv, L0_xattn_Wo, L0_xattn_bo)
    x = x + _L0_attn_ref(_layernorm(x, axis=-1), L0_attn_cond_in_W, L0_attn_rot_theta, L0_attn_cond_norm_w, L0_attn_delta_W, L0_attn_qkv_ramp_logit, L0_attn_beta_ramp_logit, L0_attn_ctrl_W, L0_attn_ctrl_b, L0_attn_q_conv_w, L0_attn_k_conv_w, L0_attn_v_conv_w, L0_attn_out_norm_w, L0_attn_out_proj_W, L0_attn_out_proj_b)
    x = x + _L0_ffn_ref(_layernorm(x, axis=-1), L0_ffn_rw1, L0_ffn_rb1, L0_ffn_rw2, L0_ffn_rb2, L0_ffn_ew1, L0_ffn_eb1, L0_ffn_ew2, L0_ffn_eb2)
    x = x + _L1_xattn_ref(_layernorm(x, axis=-1), ctx_1024, ctx_1024, L1_xattn_Wq, L1_xattn_bq, L1_xattn_Wk, L1_xattn_bk, L1_xattn_Wv, L1_xattn_bv, L1_xattn_Wo, L1_xattn_bo)
    x = x + _L1_attn_ref(_layernorm(x, axis=-1), L1_attn_Wq, L1_attn_bq, L1_attn_Wk, L1_attn_bk, L1_attn_Wv, L1_attn_bv, L1_attn_Wu, L1_attn_bu, L1_attn_Wo, L1_attn_bo, L1_attn_scale)
    x = x + _L1_ffn_ref(_layernorm(x, axis=-1), L1_ffn_sg, L1_ffn_su, L1_ffn_sd, L1_ffn_rg, L1_ffn_ru, L1_ffn_rd, L1_ffn_wr, L1_ffn_rb)
    return x

_drawn_inputs = setup_inputs


def setup_inputs(seed=0):
    import zlib

    import numpy as np

    out = dict(_drawn_inputs(seed))
    spreads = {'L0_attn_cond_norm_w': (1.0, 0.6),
     'L0_attn_qkv_ramp_logit': (-4.595119953155518, 0.6),
     'L0_attn_beta_ramp_logit': (-4.595119953155518, 0.6),
     'L0_attn_out_norm_w': (1.0, 0.2),
     'L0_attn_out_proj_b': (0.0, 0.1),
     'L0_ffn_rb1': (0.0, 0.1),
     'L0_ffn_rb2': (0.0, 0.1),
     'L0_ffn_eb1': (0.0, 0.404),
     'L0_ffn_eb2': (0.0, 0.1),
     'L1_xattn_bq': (0.0, 0.8),
     'L1_xattn_bk': (0.0, 0.8),
     'L1_xattn_bv': (0.0, 0.1),
     'L1_xattn_bo': (0.0, 0.1),
     'L1_attn_bq': (0.0, 0.8),
     'L1_attn_bk': (0.0, 0.621),
     'L1_attn_bv': (0.0, 0.636),
     'L1_attn_bu': (0.0, 0.8),
     'L1_attn_bo': (0.0, 0.1),
     'L1_attn_scale': (1.0, 0.6),
     'L1_ffn_rb': (0.0, 0.8)}
    factors = {'L0_xattn_bo': 3.547,
     'L0_attn_cond_in_W': 8.0,
     'L0_attn_rot_theta': 8.0,
     'L0_attn_delta_W': 8.0,
     'L1_ffn_sg': 3.833,
     'L1_ffn_su': 3.407,
     'L1_ffn_sd': 3.332,
     'L1_ffn_rg': 6.431,
     'L1_ffn_ru': 6.329,
     'L1_ffn_rd': 6.322,
     'L1_ffn_wr': 7.758}
    for name, (base, spread) in spreads.items():
        noise = np.random.default_rng([zlib.crc32(name.encode()), seed]).standard_normal(out[name].shape)
        drawn = base * np.exp(spread * noise) if base else spread * noise
        out[name] = jnp.asarray(drawn.astype(out[name].dtype))
    for name, factor in factors.items():
        out[name] = (out[name] * factor).astype(out[name].dtype)
    return out
```

```python
from contextlib import ExitStack

import concourse.bass as bass
from concourse import mybir

F32 = mybir.dt.float32
U32 = mybir.dt.uint32
ALU = mybir.AluOpType
ACT = mybir.ActivationFunctionType
AX = mybir.AxisListType
ds = bass.ds

P = 128
B = 8
S = 64
D = 256
T = B * S
NT = T // P
FC = D // P
M = 1601
MC = -(-M // P)
ML = M - (MC - 1) * P
BANK = 512
KB = [(k, min(BANK, M - k)) for k in range(0, M, BANK)]
QUADS = [list(range(q, min(q + 4, MC))) for q in range(0, MC, 4)]
EPS_LN = 1e-5


class Count:

    def __init__(self, sem):
        self.sem, self.base, self.k = sem, 0, 0

    def restart(self, base):
        self.base, self.k = base, 0

    def up(self, instruction):
        instruction.then_inc(self.sem, 1)
        self.k += 1

    def now(self, back=0):
        return self.base + (self.k - back)


def keys(c):
    return P if c < MC - 1 else ML


class Kit:
    pass


def build(nc, a, out):
    k = Kit()
    k.nc, k.a, k.out = nc, a, out
    with ExitStack() as ctx:
        k.sem = lambda name: ctx.enter_context(nc.semaphore(name))
        k.sb = lambda name, shape, dt=F32, where=ctx: where.enter_context(nc.sbuf_tensor(name, shape, dt))
        k.ps_s = ctx.enter_context(nc.psum_tensor("ps_s", [P, 4 * BANK], F32))
        k.ps_t = ctx.enter_context(nc.psum_tensor("ps_t", [P, 2, BANK], F32))
        k.ps_o = ctx.enter_context(nc.psum_tensor("ps_o", [P, BANK], F32))
        k.ps_m = ctx.enter_context(nc.psum_tensor("ps_m", [P, BANK], F32))
        k.x = k.sb("x", [P, NT, D])
        k.xn = k.sb("xn", [P, NT, D])
        k.xnT = k.sb("xnT", [P, FC, T])
        k.ident = k.sb("ident", [P, P])
        k.stats = k.sb("stats", [P, NT, 6])
        k.mean_var = k.sb("mean_var", [P, NT, 2])
        k.var_eps = k.sb("var_eps", [P, NT])
        k.rstd = k.sb("rstd", [P, NT])
        k.minus_half = k.sb("minus_half", [P, 2 * NT])
        k.x_in = k.sem("x_in")
        k.out_sent = k.sem("out_sent")
        k.consts = k.sem("consts")
        k.dve_order = k.sem("dve_order")
        k.ln_var = k.sem("ln_var")
        k.ln_rstd = k.sem("ln_rstd")
        k.ln_xn = k.sem("ln_xn")
        k.ln_turned = k.sem("ln_turned")
        k.ln_xT_act = k.sem("ln_xT_act")
        k.ln_xT_dve = k.sem("ln_xT_dve")
        k.passed = k.sem("passed")
        k.y_full = k.sem("y_full")
        k.x_done = k.sem("x_done")
        k.order = Count(k.dve_order)

        k.shared, k.rounds, k.units = {}, 0, 0
        parts = [StageA, StageB, StageC, StageD, StageE, StageF]
        parts = [p(k, n) for n, p in enumerate(parts)]
        block = ctx.enter_context(nc.Block())

        @block.sync
        def _(sp):
            sp.dma_start(k.x[:, :, :], a["x"].rearrange("(t b) s d -> (b s) t d", t=NT)).then_inc(k.x_in, 16)
            for p in parts:
                p.sync(sp)
            sp.wait_ge(k.x_done, len(parts))
            sp.dma_start(out.rearrange("(t b) s d -> (b s) t d", t=NT), k.x[:, :, :]).then_inc(k.out_sent, 16)
            sp.wait_ge(k.out_sent, 16)

        @block.gpsimd
        def _(pool):
            nc.gpsimd.memset(k.ident[:, :], 0.0).then_inc(k.consts, 1)
            nc.gpsimd.memset(k.minus_half[:, :], -0.5).then_inc(k.consts, 1)
            pool.wait_ge(k.consts, 2)
            nc.gpsimd.affine_select(out=k.ident[:, :], in_=k.ident[:, :], compare_op=ALU.not_equal, fill=1.0,
                                    base=0, pattern=[[-1, P]], channel_multiplier=1).then_inc(k.consts, 1)
            for p in parts:
                p.gpsimd(pool)

        @block.scalar
        def _(act):
            for p in parts:
                p.scalar(act)

        @block.vector
        def _(dve):
            dve.wait_ge(k.x_in, 16)
            for p in parts:
                p.vector(dve)

        @block.tensor
        def _(pe):
            pe.wait_ge(k.consts, 3)
            for p in parts:
                p.tensor(pe)


def link(k, dve, instruction):
    k.order.up(instruction)
    dve.wait_ge(k.dve_order, k.order.now())


def stand(k, eng, sem, value):
    eng.wait_ge(sem, value)
    if not isinstance(value, int):
        eng.nop().then_inc(k.passed, 1)


def norm_vector(k, dve, n):
    nc = k.nc
    for t in range(NT):
        last = nc.vector.bn_stats(k.stats[:, t, :], k.x[:, t, :])
    link(k, dve, last)
    for t in range(NT):
        last = nc.vector.bn_aggr(k.mean_var[:, t, :], k.stats[:, t, :])
    link(k, dve, last)
    nc.vector.tensor_scalar(k.var_eps[:, :], k.mean_var[:, :, 1], EPS_LN, None, ALU.add).then_inc(k.ln_var, 1)
    dve.wait_ge(k.ln_rstd, n + 1)
    for t in range(NT):
        nc.vector.tensor_scalar(k.xn[:, t, :], k.x[:, t, :], k.mean_var[:, t, 0:1], k.rstd[:, t:t + 1],
                                ALU.subtract, ALU.mult).then_inc(k.ln_xn, 1)
    dve.wait_ge(k.ln_turned, 2 * n + 2)
    nc.vector.tensor_copy(k.xnT[:, 1, :], k.ps_t[:, 1, :]).then_inc(k.ln_xT_dve, 1)


def norm_pool(k, pool, n):
    pool.wait_ge(k.ln_var, n + 1)
    k.nc.gpsimd.tensor_tensor(k.rstd[:, :], k.var_eps[:, :], k.minus_half[:, 0:NT], ALU.pow).then_inc(k.ln_rstd, 1)


def norm_tensor(k, pe, n):
    for f in range(FC):
        for t in range(NT):
            if f == 0:
                pe.wait_ge(k.ln_xn, NT * n + t + 1)
            last = k.nc.tensor.transpose(k.ps_t[:, f, t * P:(t + 1) * P], k.xn[:, t, f * P:(f + 1) * P], k.ident[:, :])
        last.then_inc(k.ln_turned, 1)


def norm_scalar(k, act, n):
    act.wait_ge(k.ln_turned, 2 * n + 1)
    k.nc.scalar.activation(k.xnT[:, 0, :], k.ps_t[:, 0, :], ACT.Copy).then_inc(k.ln_xT_act, 1)


def wait_norm(k, eng, n):
    eng.wait_ge(k.ln_xT_act, n + 1)
    eng.wait_ge(k.ln_xT_dve, n + 1)


class Attention:

    G = None
    WIDTH = None
    FOLDED = False

    def attention_memory(self, k, st):
        name = self.name
        self.p = k.sb(name + "p", [P, 2, M], F32, st)
        self.pT = k.sb(name + "pT", [P, MC, P], F32, st)
        self.neg_max = k.sb(name + "neg_max", [P, 2], F32, st)
        self.sums = k.sb(name + "sums", [P, 2], F32, st)
        self.inv = k.sb(name + "inv", [P, 2], F32, st)
        sem = k.sem
        self.scored = sem(name + "scored")
        self.maxed = sem(name + "maxed")
        self.exped = sem(name + "exped")
        self.turned = sem(name + "turned")
        self.moved_dve = sem(name + "moved_dve")
        self.moved_act = sem(name + "moved_act")
        self.valued = sem(name + "valued")
        self.inverted = sem(name + "inverted")
        self.scaled = sem(name + "scaled")
        self.misc_full = sem(name + "misc_full")
        self.misc_read = sem(name + "misc_read")

    def bodies(self, eng, body):
        body(0, True, False)
        with eng.Fori(1, B // 2 - 1) as i:
            body(i, False, False)
        body(B // 2 - 1, False, True)

    def dve_extra(self, k, dve, i, s, first, last):
        pass

    def pe_turn(self, k, pe, n, s, q):
        if q >= 2:
            pe.wait_ge(self.moved_act if q % 2 else self.moved_dve, 2 * n + 1)
        elif not (isinstance(n, int) and n == 0):
            pe.wait_ge(self.moved_act if q % 2 else self.moved_dve, 2 * n)
        for j, c in enumerate(QUADS[q]):
            last = k.nc.tensor.transpose(k.ps_t[0:keys(c), q % 2, j * P:(j + 1) * P],
                                         self.p[:, s % 2, c * P:c * P + keys(c)], k.ident[:, :])
        last.then_inc(self.turned, 1)

    def pe_value(self, k, pe, n, s, q):
        pe.wait_ge(self.moved_act if q % 2 else self.moved_dve, 2 * n + 1 + q // 2)
        for c in QUADS[q]:
            last = k.nc.tensor.matmul(k.ps_o[:, 0:self.WIDTH], self.pT[0:keys(c), c, :],
                                      self.values(s, c), start=(c == 0), stop=(c == MC - 1))
        return last

    def tensor_loop(self, k, pe):
        G = self.G
        misc = Count(self.misc_full)

        def fill(*what):
            if not (isinstance(misc.base, int) and misc.now() == 0):
                stand(k, pe, self.misc_read, misc.now())
            misc.up(self.pe_misc(k, pe, *what))

        self.pe_before(k, pe, fill)
        pre = misc.k
        self.pe_scores(k, pe, 0, 0, KB).then_inc(self.scored, 1)

        def body(i, first, last):
            if not first:
                misc.restart(self.first_fills + self.fills * (i - 1))
            for s in range(2 * G):
                n = 2 * G * i + s
                end = last and s == 2 * G - 1
                pe.wait_ge(self.exped, n + 1)
                self.pe_turn(k, pe, n, s, 0)
                self.pe_turn(k, pe, n, s, 1)
                if self.FOLDED and not (first and s == 0):
                    self.pe_fold(k, pe, n - 1)
                if not end:
                    s1 = (s + 1) % (2 * G)
                    i1 = i if s1 else i + 1
                    self.pe_ready(k, pe, i1, s1, misc)
                    self.pe_scores(k, pe, i1, s1, KB[0:2])
                self.pe_turn(k, pe, n, s, 2)
                self.pe_turn(k, pe, n, s, 3)
                if not end:
                    self.pe_scores(k, pe, i1, s1, KB[2:]).then_inc(self.scored, 1)
                for what in self.fills_before(s, first, last):
                    fill(i, *what)
                if not (first and s == 0):
                    pe.wait_ge(self.scaled, n)
                for q in range(3):
                    self.pe_value(k, pe, n, s, q)
                self.pe_value(k, pe, n, s, 3).then_inc(self.parted if self.FOLDED else self.valued, 1)
                for what in self.fills_after(s, first, last):
                    fill(i, *what)
            if first:
                assert misc.k == self.first_fills, misc.k
            elif not last:
                assert misc.k == self.fills, misc.k

        self.bodies(pe, body)
        misc.restart(self.first_fills + self.fills * (B // 2 - 2) + misc.k)
        self.pe_after(k, pe, fill, misc)

    def vector_loop(self, k, dve):
        G = self.G

        def maximum(n, s):
            dve.wait_ge(self.scored, n + 1)
            k.nc.vector.tensor_reduce(self.neg_max[:, s % 2:s % 2 + 1], k.ps_s[:, 0:M], AX.X, ALU.max,
                                      negate=True).then_inc(self.maxed, 1)

        def move(n, q):
            dve.wait_ge(self.turned, 4 * n + q + 1)
            w, c = len(QUADS[q]), QUADS[q][0]
            k.nc.vector.tensor_copy(self.pT[:, c:c + w, :], k.ps_t[:, q % 2, 0:w * P]
                                    .rearrange("p (c r) -> p c r", r=P)).then_inc(self.moved_dve, 1)

        def scale_folded(n, s):
            dve.wait_ge(self.inverted, n + 1)
            dve.wait_ge(self.valued, n + 1)
            self.dve_scale(k, dve, s % (2 * G)).then_inc(self.scaled, 1)

        maximum(0, 0)

        def body(i, first, last):
            for s in range(2 * G):
                n = 2 * G * i + s
                move(n, 0)
                if self.FOLDED and not (first and s == 0):
                    scale_folded(n - 1, s - 1)
                move(n, 2)
                if not (last and s == 2 * G - 1):
                    maximum(n + 1, s + 1)
                dve.wait_ge(self.exped, n + 1)
                k.nc.vector.reciprocal(self.inv[:, s % 2:s % 2 + 1], self.sums[:, s % 2:s % 2 + 1])\
                    .then_inc(self.inverted, 1)
                if self.FOLDED:
                    dve.wait_ge(self.parted, n + 1)
                    self.dve_unfold(k, dve)
                    if last and s == 2 * G - 1:
                        scale_folded(n, s)
                else:
                    dve.wait_ge(self.inverted, n + 1)
                    dve.wait_ge(self.valued, n + 1)
                    self.dve_scale(k, dve, s).then_inc(self.scaled, 1)
                self.dve_extra(k, dve, i, s, first, last)

        self.bodies(dve, body)

    def scalar_loop(self, k, act):
        G = self.G
        misc = Count(self.misc_read)

        def read(*what):
            act.wait_ge(self.misc_full, misc.now() + 1)
            misc.up(self.act_misc(k, act, *what))

        def exponential(n, s):
            act.wait_ge(self.maxed, n + 1)
            k.nc.scalar.activation(self.p[:, s % 2, :], k.ps_s[:, 0:M], ACT.Exp, bias=self.neg_max[:, s % 2:s % 2 + 1],
                                   accum_out=self.sums[:, s % 2:s % 2 + 1]).then_inc(self.exped, 1)

        def move(n, q):
            act.wait_ge(self.turned, 4 * n + q + 1)
            w, c = len(QUADS[q]), QUADS[q][0]
            r = keys(c)
            k.nc.scalar.activation(self.pT[0:r, c:c + w, :], k.ps_t[0:r, q % 2, 0:w * P]
                                   .rearrange("p (c r) -> p c r", r=P), ACT.Copy).then_inc(self.moved_act, 1)

        self.act_before(k, act, read)
        exponential(0, 0)

        def body(i, first, last):
            if not first:
                misc.restart(self.first_fills + self.fills * (i - 1))
            for s in range(2 * G):
                n = 2 * G * i + s
                move(n, 1)
                move(n, 3)
                for what in self.fills_before(s, first, last):
                    read(i, *what)
                if not (last and s == 2 * G - 1):
                    exponential(n + 1, s + 1)
                for what in self.fills_after(s, first, last):
                    read(i, *what)

        self.bodies(act, body)
        misc.restart(self.first_fills + self.fills * (B // 2 - 2) + misc.k)
        self.act_after(k, act, read)


class StageA(Attention):

    name = "a_"
    H, DH = 8, 64
    G = 4
    WIDTH = D

    def __init__(self, k, n):
        self.n, self.k = n, k
        sem = k.sem
        with ExitStack() as st:
            sb = lambda name, shape, dt=F32: k.sb("a_" + name, shape, dt, st)
            self.wq = sb("wq", [P, FC, 512])
            self.wkT = sb("wkT", [64, 8, D])
            self.wv = sb("wv", [P, FC, 512])
            self.wo = sb("wo", [P, 4, D])
            self.bo = sb("bo", [P, D])
            self.qT = sb("qT", [64, 8, T])
            self.ctx = sb("ctx", [P, 2, MC, D])
            self.ctxT = sb("ctxT", [P, 2, FC, M])
            self.qk = sb("qk", [P, 2, FC, 8 * S])
            self.mixed = sb("mixed", [P, 2, D])
            self.mixedT = sb("mixedT", [P, 2, FC, 8 * S])
            self.oT = sb("oT", [P, 4, T])
            self.attention_memory(k, st)
            self.w_in = sem("a_w_in")
            self.late_in = sem("a_late_in")
            self.ctx_in = [sem("a_ctx_in0"), sem("a_ctx_in1")]
            self.ctxT_in = [sem("a_ctxT_in0"), sem("a_ctxT_in1")]
            self.q_full = sem("a_q_full")
            self.q_read = sem("a_q_read")
        self.first_fills = 2 + 8 - 1 + 1 + 4
        self.fills = 8 + 2 + 4

    def pe_ready(self, k, pe, i, s1, misc):
        if s1 % 4 == 0:
            stand(k, pe, self.misc_read, misc.now())

    def fills_before(self, s, first, last):
        return [] if first and s == 0 else [("turn", (s - 1) % 8)]

    def fills_after(self, s, first, last):
        g = s % 4
        out = []
        if g == 0 and not (first and s == 0):
            out.append(("out", (s - 1) % 8 // 4))
        if g in (1, 2) and not (last and s >= 4):
            out.append(("qk", 1 - s // 4, g - 1, 1 + s // 4))
        return out

    def values(self, s, c):
        return self.ctx[0:keys(c), s // 4, c, :]

    def sync(self, sp):
        k, a = self.k, self.k.a
        sp.dma_start(self.wq[:, :, :], a["a_wq"]).then_inc(self.w_in, 16)
        sp.dma_start(self.wkT[:, :, :], a["a_wkT"]).then_inc(self.w_in, 16)

        def load(b, p):
            at = b if isinstance(b, int) else ds(b, 1)
            tT, t = a["ctxT"], a["ctx_1024"]
            srcT = tT[b] if isinstance(b, int) else tT[ds(b, 1)].rearrange("a p f m -> (a p) f m")
            src = t[b] if isinstance(b, int) else t[ds(b, 1)].rearrange("a m d -> (a m) d")
            if not (isinstance(b, int) and b < 2):
                sp.wait_ge(self.scored, 4 * (b - 2) + 4)
            sp.dma_start(self.ctxT[:, p, :, :], srcT).then_inc(self.ctxT_in[p], 16)
            if not (isinstance(b, int) and b < 2):
                sp.wait_ge(self.valued, 4 * (b - 2) + 4)
            sp.dma_start(self.ctx[:, p, 0:MC - 1, :],
                         src[0:(MC - 1) * P, :].rearrange("(c p) d -> p c d", p=P)).then_inc(self.ctx_in[p], 16)
            sp.dma_start(self.ctx[0:ML, p, MC - 1, :], src[(MC - 1) * P:M, :]).then_inc(self.ctx_in[p], 16)

        load(0, 0)
        load(1, 1)
        sp.dma_start(self.wv[:, :, :], a["a_wv"]).then_inc(self.late_in, 16)
        sp.dma_start(self.wo[:, :, :], a["a_wo"]).then_inc(self.late_in, 16)
        sp.dma_start(self.bo[:, :], a["a_bo"].partition_broadcast(P)).then_inc(self.late_in, 16)
        with sp.Fori(1, B // 2) as i:
            load(2 * i, 0)
            load(2 * i + 1, 1)

    def gpsimd(self, pool):
        norm_pool(self.k, pool, self.n)

    def tensor(self, pe):
        norm_tensor(self.k, pe, self.n)
        self.tensor_loop(self.k, pe)

    def pe_before(self, k, pe, fill):
        nc = k.nc
        wait_norm(k, pe, self.n)
        pe.wait_ge(self.w_in, 32)
        for h in range(8):
            if h >= 2:
                pe.wait_ge(self.q_read, h - 1)
            for f in range(FC):
                last = nc.tensor.matmul(k.ps_s[0:64, (h % 2) * BANK:(h % 2 + 1) * BANK],
                                        self.wq[:, f, h * 64:(h + 1) * 64], k.xnT[:, f, :],
                                        start=(f == 0), stop=(f == FC - 1))
            last.then_inc(self.q_full, 1)
        pe.wait_ge(self.q_read, 8)
        fill(0, "qk", 0, 0, 0)
        fill(0, "qk", 0, 1, 0)
        pe.wait_ge(self.misc_read, 2)

    def pe_scores(self, k, pe, i, s, blocks):
        p, g = s // 4, s % 4
        if g == 0 and blocks[0][0] == 0:
            pe.wait_ge(self.ctxT_in[p], 16 * (i + 1))
        for c, w in blocks:
            for f in range(FC):
                last = k.nc.tensor.matmul(k.ps_s[:, c:c + w], self.qk[:, p, f, g * P:(g + 1) * P],
                                          self.ctxT[:, p, f, c:c + w], start=(f == 0), stop=(f == FC - 1))
        return last

    def pe_value(self, k, pe, n, s, q):
        if s % 4 == 0 and q == 0:
            pe.wait_ge(self.ctx_in[s // 4], 32 * (self.pe_i + 1))
        return Attention.pe_value(self, k, pe, n, s, q)

    def pe_misc(self, k, pe, i, kind, *which):
        nc = k.nc
        if kind == "turn":
            s = which[0]
            n = 8 * i + s if s < 7 else 8 * i - 1
            pe.wait_ge(self.scaled, n + 1)
            for f in range(FC):
                last = nc.tensor.transpose(k.ps_m[:, f * P:(f + 1) * P], self.mixed[:, s % 2, f * P:(f + 1) * P],
                                           k.ident[:, :])
        elif kind == "out":
            p = which[0]
            if isinstance(i, int) and i == 0:
                pe.wait_ge(self.late_in, 48)
            for h in range(8):
                for f in range(FC):
                    last = nc.tensor.matmul(k.ps_m[64 * (h % 2):64 * (h % 2) + 64, h // 2 * S:(h // 2 + 1) * S],
                                            self.wv[:, f, h * 64:(h + 1) * 64],
                                            self.mixedT[:, p, f, h * S:(h + 1) * S],
                                            start=(f == 0), stop=(f == FC - 1))
        else:
            p, f, ahead = which
            b = 2 * i + ahead
            for h in range(8):
                rhs = self.qT[:, h, b * S:(b + 1) * S] if isinstance(b, int) else self.qT[:, h, ds(b * S, S)]
                last = nc.tensor.matmul(k.ps_m[:, h * S:(h + 1) * S], self.wkT[:, h, f * P:(f + 1) * P], rhs,
                                        start=True, stop=True)
        return last

    def bodies(self, eng, body):
        def noted(i, first, last):
            self.pe_i = i
            body(i, first, last)
        Attention.bodies(self, eng, noted)

    def pe_after(self, k, pe, fill, misc):
        nc = k.nc
        misc_last = B // 2
        fill(misc_last, "turn", 7)
        fill(misc_last, "out", 1)
        pe.wait_ge(self.misc_read, misc.now())
        pe.wait_ge(self.late_in, 48)
        for t in range(NT):
            for c in range(4):
                last = nc.tensor.matmul(k.ps_s[:, t * BANK:t * BANK + D], self.oT[:, c, t * P:(t + 1) * P],
                                        self.wo[:, c, :], start=(c == 0), stop=(c == 3))
            last.then_inc(k.y_full, 1)

    def scalar(self, act):
        norm_scalar(self.k, act, self.n)
        self.scalar_loop(self.k, act)

    def act_before(self, k, act, read):
        for h in range(8):
            act.wait_ge(self.q_full, h + 1)
            k.nc.scalar.activation(self.qT[:, h, :], k.ps_s[0:64, (h % 2) * BANK:(h % 2 + 1) * BANK],
                                   ACT.Copy).then_inc(self.q_read, 1)
        read(0, "qk", 0, 0, 0)
        read(0, "qk", 0, 1, 0)

    def act_misc(self, k, act, i, kind, *which):
        nc = k.nc
        if kind == "turn":
            s = which[0]
            return nc.scalar.activation(self.mixedT[:, s // 4, :, s % 4 * P:(s % 4 + 1) * P],
                                        k.ps_m[:, 0:FC * P].rearrange("p (f r) -> p f r", r=P), ACT.Copy)
        if kind == "out":
            b = 2 * i + which[0] if which[0] == 0 else 2 * i - 1
            at = slice(b * S, (b + 1) * S) if isinstance(b, int) else ds(b * S, S)
            return nc.scalar.activation(self.oT[:, :, at], k.ps_m[:, 0:4 * S].rearrange("p (c s) -> p c s", s=S), ACT.Copy)
        p, f, _ = which
        return nc.scalar.activation(self.qk[:, p, f, :], k.ps_m[:, :], ACT.Copy, scale=self.DH ** -0.5)

    def act_after(self, k, act, read):
        read(B // 2, "turn", 7)
        read(B // 2, "out", 1)

    def dve_scale(self, k, dve, s):
        return k.nc.vector.tensor_scalar(self.mixed[:, s % 2, :], k.ps_o[:, 0:D], self.inv[:, s % 2:s % 2 + 1], None,
                                         ALU.mult)

    def vector(self, dve):
        k = self.k
        norm_vector(k, dve, self.n)
        self.vector_loop(k, dve)
        dve.wait_ge(self.late_in, 48)
        finish(k, dve, lambda t: self.bo[:, :], lambda t: k.ps_s[:, t * BANK:t * BANK + D], self.n)


class StageB:

    H, DH = 16, 16
    RUN = 50
    W = H * RUN + D
    RING = 8

    def __init__(self, k, n):
        self.k, self.n = k, n
        sem = k.sem
        with ExitStack() as st:
            sb = lambda name, shape, dt=F32: k.sb("b_" + name, shape, dt, st)
            self.cin = sb("cin", [P, FC, P])
            self.ctl = sb("ctl", [P, FC, self.W])
            self.ctl_b = sb("ctl_b", [P, self.W])
            self.delta = sb("delta", [P, 16, self.RUN])
            self.ramp = sb("ramp", [P, 16, self.RUN - 1])
            self.theta = sb("theta", [64, 1])
            self.turn_work = sb("turn_work", [64, 8])
            self.cos_sin = sb("cos_sin", [64, 6, 3])
            self.norm_w = sb("norm_w", [64, 2])
            self.state = sb("state", [64, 2, 2, T])
            self.part = sb("part", [64, 2, T])
            self.rms = sb("rms", [P, NT])
            self.rms_inv = sb("rms_inv", [P, NT])
            self.ones = sb("ones", [64, 1])
            self.spread = sb("spread", [64, T])
            self.condT = sb("condT", [P, T])
            self.mix = sb("mix", [P, NT, self.W])
            self.rows = sb("rows", [P, 3 + S, self.RUN])
            self.conv_w = sb("conv_w", [P, 4, 48])
            self.conv = sb("conv", [P, S, 48])
            self.prod = sb("prod", [P, S, 48])
            self.act = sb("act", [P, S, 48])
            self.gates = sb("gates", [P, S, 2])
            self.neg_gb = sb("neg_gb", [P, S])
            self.ssq = sb("ssq", [P, 2, S])
            self.ssq_inv = sb("ssq_inv", [P, 2, S])
            self.kv = sb("kv", [P, S, 2, 16])
            self.qn = sb("qn", [P, S, 16])
            self.hist = sb("hist", [P, self.RING, 16, 16])
            self.tmp = sb("tmp", [P, 16, 16])
            self.outer = sb("outer", [P, 16, 16])
            self.past = sb("past", [P, 16])
            self.begun = sb("begun", [P, 16])
            self.coef = sb("coef", [P, S, 2])
            self.u = sb("u", [P, 16])
            self.qs = sb("qs", [P, self.RING, 16, 16])
            self.o = sb("o", [P, S, 16])
            self.o_sq = sb("o_sq", [P, S, 16])
            self.o_w = sb("o_w", [P, 16])
            self.o_tok = sb("o_tok", [P, NT, D])
            self.gate = sb("gate", [P, NT, D])
            self.oT = sb("oT", [P, FC, T])
            self.wo = sb("wo", [P, FC, D])
            self.bo = sb("bo", [P, D])
        self.mix_dram = k.nc.dram_tensor("b_mix_dram", (T, 800), F32, kind="Internal").ap()
        self.o_dram = k.nc.dram_tensor("b_o_dram", (P, S * 16), F32, kind="Internal").ap()
        self.w_in = sem("b_w_in")
        self.small_in = sem("b_small_in")
        self.cleared = sem("b_cleared")
        self.ramped = sem("b_ramped")
        self.delta_ready = sem("b_delta_ready")
        self.angle = sem("b_angle")
        self.sines = sem("b_sines")
        self.cosines = sem("b_cosines")
        self.p_full = sem("b_p_full")
        self.p_read = sem("b_p_read")
        self.squared = sem("b_squared")
        self.ms_full = sem("b_ms_full")
        self.ms_eps = sem("b_ms_eps")
        self.ms_inv = sem("b_ms_inv")
        self.spread_full = sem("b_spread_full")
        self.cond = sem("b_cond")
        self.mix_full = sem("b_mix_full")
        self.mix_ready = sem("b_mix_ready")
        self.mix_sent = sem("b_mix_sent")
        self.rows_in = sem("b_rows_in")
        self.q_prod = sem("b_q_prod")
        self.q_conv = sem("b_q_conv")
        self.conved = sem("b_conved")
        self.silued = sem("b_silued")
        self.gated = sem("b_gated")
        self.squares = sem("b_squares")
        self.rooted = sem("b_rooted")
        self.eps_in = sem("b_eps_in")
        self.roots = sem("b_roots")
        self.ready = sem("b_ready")
        self.state_done = sem("b_state_done")
        self.qs_done = sem("b_qs_done")
        self.qs_read = sem("b_qs_read")
        self.step = sem("b_step")
        self.o_ready = sem("b_o_ready")
        self.o_squared = sem("b_o_squared")
        self.o_ms = sem("b_o_ms")
        self.o_root = sem("b_o_root")
        self.o_normed = sem("b_o_normed")
        self.o_sent = sem("b_o_sent")
        self.o_back = sem("b_o_back")
        self.gate_silu = sem("b_gate_silu")
        self.gated_out = sem("b_gated_out")
        self.turned_o = sem("b_turned_o")
        self.oT_act = sem("b_oT_act")

    def sync(self, sp):
        k, a = self.k, self.k.a
        sp.wait_ge(k.x_done, self.n)
        for name, tile in (("theta", self.theta), ("norm_w", self.norm_w), ("conv_w", self.conv_w)):
            sp.dma_start(tile[...], a["b_" + name]).then_inc(self.small_in, 16)
        sp.dma_start(self.o_w[:, :], a["b_o_w"].partition_broadcast(P)).then_inc(self.small_in, 16)
        sp.dma_start(self.ramp[:, :, :], a["b_ramp"].partition_broadcast(P)).then_inc(self.small_in, 16)
        sp.dma_start(self.cin[:, :, :], a["b_cin"]).then_inc(self.w_in, 16)
        sp.wait_ge(self.cleared, 1)
        sp.dma_start(self.delta[:, :, 0:self.RUN - 1], a["b_delta"]).then_inc(self.w_in, 16)
        sp.dma_start(self.ctl[:, :, :], a["b_ctl"]).then_inc(self.w_in, 16)
        sp.dma_start(self.ctl_b[:, :], a["b_ctl_b"].partition_broadcast(P)).then_inc(self.w_in, 16)
        sp.dma_start(self.wo[:, :, :], a["b_wo"]).then_inc(self.w_in, 16)
        sp.dma_start(self.bo[:, :], a["b_bo"].partition_broadcast(P)).then_inc(self.w_in, 16)
        for t in range(NT):
            sp.wait_ge(self.mix_ready, t + 1)
            sp.dma_start(self.mix_dram[t * P:(t + 1) * P, :], self.mix[:, t, 0:800]).then_inc(self.mix_sent, 16)
        sp.wait_ge(self.cleared, 2)
        for b in range(B):
            if b % 2 == 0:
                sp.wait_ge(self.mix_sent, 16 * NT)
            sp.dma_start(self.rows[16 * b:16 * b + 16, 3:3 + S, :],
                         self.mix_dram[b * S:(b + 1) * S, :].rearrange("s (h c) -> h s c", h=16))\
                .then_inc(self.rows_in, 16)
        sp.wait_ge(self.o_normed, 1)
        sp.dma_start(self.o_dram[:, :], self.o_sq[:, :, :].rearrange("p s d -> p (s d)")).then_inc(self.o_sent, 16)
        sp.wait_ge(self.o_sent, 16)
        for b in range(B):
            sp.dma_start(self.o_tok[64 * (b % 2):64 * (b % 2) + 64, b // 2, :].rearrange("s (h d) -> s h d", h=16),
                         self.o_dram[16 * b:16 * b + 16, :].rearrange("h (s d) -> s h d", s=S))\
                .then_inc(self.o_back, 16)

    def gpsimd(self, pool):
        k, nc = self.k, self.k.nc
        pool.wait_ge(k.x_done, self.n)
        nc.gpsimd.memset(self.delta[:, :, :], 0.0).then_inc(self.cleared, 1)
        nc.gpsimd.memset(self.ones[:, :], 1.0).then_inc(self.consts_(), 1)
        nc.gpsimd.memset(self.rows[:, 0:3, :], 0.0).then_inc(self.cleared, 1)
        norm_pool(k, pool, self.n)
        pool.wait_ge(self.ramped, 1)
        pool.wait_ge(self.w_in, 96)
        nc.gpsimd.tensor_tensor(self.delta[:, :, 0:self.RUN - 1], self.delta[:, :, 0:self.RUN - 1], self.ramp[:, :, :],
                                ALU.mult).then_inc(self.delta_ready, 1)
        pool.wait_ge(self.ms_eps, 1)
        nc.gpsimd.tensor_tensor(self.rms_inv[:, :], self.rms[:, :], k.minus_half[:, 0:NT], ALU.pow)\
            .then_inc(self.ms_inv, 1)
        pool.wait_ge(self.rows_in, 16 * B)
        pool.wait_ge(self.small_in, 80)
        order = 0
        for j in range(4):
            dst = self.conv if j == 0 else self.prod
            nc.gpsimd.tensor_tensor(dst[:, :, 0:16], self.rows[:, j:j + S, 0:16],
                                    self.conv_w[:, j:j + 1, 0:16].to_broadcast([P, S, 16]), ALU.mult)\
                .then_inc(self.q_prod, 1)
            order += 1
            pool.wait_ge(self.q_prod, order)
            if j:
                nc.gpsimd.tensor_tensor(self.conv[:, :, 0:16], self.conv[:, :, 0:16], self.prod[:, :, 0:16], ALU.add)\
                    .then_inc(self.q_prod, 1)
                order += 1
                pool.wait_ge(self.q_prod, order)
        nc.gpsimd.nop().then_inc(self.q_conv, 1)
        pool.wait_ge(self.ready, 1)
        H = self.RING // 2

        def products(i, start, end):
            for j in range(self.RING):
                stand(k, pool, self.state_done, i * self.RING + (j + 1))
                if j % H == 0 and not start:
                    stand(k, pool, self.qs_read, 2 * i + (j // H - 1))
                q = self.qn[:, ds(i * self.RING + j, 1), :].to_broadcast([P, 16, 16])
                nc.gpsimd.tensor_tensor(self.qs[:, j, :, :], self.hist[:, j, :, :], q, ALU.mult).then_inc(self.qs_done, 1)

        self.rounds(pool, products)

    def rounds(self, eng, body):
        body(0, True, False)
        with eng.Fori(1, S // self.RING - 1) as i:
            body(i, False, False)
        body(S // self.RING - 1, False, True)

    def consts_(self):
        return self.eps_in

    def tensor(self, pe):
        k, nc = self.k, self.k.nc
        norm_tensor(k, pe, self.n)
        wait_norm(k, pe, self.n)
        pe.wait_ge(self.w_in, 96)
        for c in range(2):
            for f in range(FC):
                last = nc.tensor.matmul(k.ps_s[0:64, c * BANK:(c + 1) * BANK], self.cin[:, f, c * 64:(c + 1) * 64],
                                        k.xnT[:, f, :], start=(f == 0), stop=(f == FC - 1))
            last.then_inc(self.p_full, 1)
        pe.wait_ge(self.squared, 1)
        pe.wait_ge(self.eps_in, 1)
        for t in range(NT):
            for c in range(2):
                last = nc.tensor.matmul(k.ps_m[:, t:t + 1], self.part[:, c, t * P:(t + 1) * P], self.ones[:, :],
                                        start=(c == 0), stop=(c == 1))
        last.then_inc(self.ms_full, 1)
        pe.wait_ge(self.ms_inv, 1)
        for t in range(NT):
            last = nc.tensor.matmul(k.ps_o[0:64, t * P:(t + 1) * P], self.rms_inv[:, t:t + 1].to_broadcast([P, 64]),
                                    k.ident[:, :], start=True, stop=True)
        last.then_inc(self.spread_full, 1)
        pe.wait_ge(self.cond, 2)
        pe.wait_ge(self.delta_ready, 1)
        dw = self.delta[:, :, :].rearrange("p h c -> p (h c)")
        for t in range(NT):
            if t:
                pe.wait_ge(self.mix_ready, t)
            tok = slice(t * P, (t + 1) * P)
            for lo in range(0, self.W, BANK):
                hi = min(lo + BANK, self.W)
                nc.tensor.matmul(k.ps_s[:, lo:hi], k.xnT[:, 0, tok], self.ctl[:, 0, lo:hi], start=True, stop=False)
                if lo < 800:
                    top = min(hi, 800)
                    nc.tensor.matmul(k.ps_s[:, lo:top], self.condT[:, tok], dw[:, lo:top], start=False, stop=False)
                last = nc.tensor.matmul(k.ps_s[:, lo:hi], k.xnT[:, 1, tok], self.ctl[:, 1, lo:hi], start=False, stop=True)
            last.then_inc(self.mix_full, 1)
        for f in range(FC):
            for t in range(NT):
                if f == 0:
                    pe.wait_ge(self.gated_out, t + 1)
                last = nc.tensor.transpose(k.ps_t[:, f, t * P:(t + 1) * P], self.o_tok[:, t, f * P:(f + 1) * P],
                                           k.ident[:, :])
            last.then_inc(self.turned_o, 1)
        pe.wait_ge(self.oT_act, 2)
        for t in range(NT):
            for f in range(FC):
                last = nc.tensor.matmul(k.ps_s[:, t * BANK:t * BANK + D], self.oT[:, f, t * P:(t + 1) * P],
                                        self.wo[:, f, :], start=(f == 0), stop=(f == FC - 1))
            last.then_inc(k.y_full, 1)

    def scalar(self, act):
        k, nc = self.k, self.k.nc
        act.wait_ge(self.small_in, 80)
        nc.scalar.activation(self.ramp[:, :, :], self.ramp[:, :, :], ACT.Sigmoid).then_inc(self.ramped, 1)
        act.wait_ge(self.angle, 1)
        nc.scalar.activation(self.turn_work[:, 2:3], self.turn_work[:, 1:2], ACT.Sin).then_inc(self.sines, 1)
        nc.scalar.activation(self.turn_work[:, 3:4], self.turn_work[:, 1:2], ACT.Sin, scale=0.5).then_inc(self.sines, 1)
        norm_scalar(k, act, self.n)
        for c in range(2):
            act.wait_ge(self.p_full, c + 1)
            nc.scalar.activation(self.state[:, 0, c, :], k.ps_s[0:64, c * BANK:(c + 1) * BANK], ACT.Copy)\
                .then_inc(self.p_read, 1)
        act.wait_ge(self.spread_full, 1)
        nc.scalar.activation(self.spread[:, :], k.ps_o[0:64, :], ACT.Copy).then_inc(self.cosines, 1)
        act.wait_ge(self.q_conv, 1)
        act.wait_ge(self.q_prod, 7)
        act.wait_ge(self.conved, 1)
        nc.scalar.activation(self.act[:, :, :], self.conv[:, :, :], ACT.Silu).then_inc(self.silued, 1)
        nc.scalar.activation(self.gates[:, :, :], self.rows[:, 3:3 + S, 48:50], ACT.Sigmoid).then_inc(self.gated, 1)
        act.wait_ge(self.silued, 1)
        nc.scalar.activation(self.prod[:, :, 0:32], self.act[:, :, 0:32], ACT.Square).then_inc(self.squares, 1)
        act.wait_ge(self.mix_ready, NT)
        for t in range(NT):
            nc.scalar.activation(self.gate[:, t, :], self.mix[:, t, 800:self.W], ACT.Silu).then_inc(self.gate_silu, 1)
        act.wait_ge(self.rooted, 1)
        nc.scalar.activation(self.ssq[:, :, :], self.ssq[:, :, :], ACT.Sqrt).then_inc(self.roots, 1)
        act.wait_ge(self.o_ms, 1)
        nc.scalar.activation(self.ssq[:, 0, :], self.ssq[:, 0, :], ACT.Sqrt).then_inc(self.o_root, 1)
        for f in range(FC):
            act.wait_ge(self.turned_o, f + 1)
            nc.scalar.activation(self.oT[:, f, :], k.ps_t[:, f, :], ACT.Copy).then_inc(self.oT_act, 1)

    def vector(self, dve):
        k, nc = self.k, self.k.nc
        v = nc.vector
        chain = lambda ins: link(k, dve, ins)
        dve.wait_ge(self.small_in, 80)
        w = self.turn_work
        TWO_PI_HI, TWO_PI_LO, MAGIC = 6.28125, 0.0019353071795864769, 12582912.0
        chain(v.tensor_scalar(w[:, 0:1], self.theta[:, :], 0.15915494309189535, MAGIC, ALU.mult, ALU.add))
        chain(v.tensor_scalar(w[:, 0:1], w[:, 0:1], MAGIC, None, ALU.subtract))
        chain(v.scalar_tensor_tensor(w[:, 1:2], w[:, 0:1], -TWO_PI_HI, self.theta[:, :], ALU.mult, ALU.add))
        chain(v.scalar_tensor_tensor(w[:, 1:2], w[:, 0:1], -TWO_PI_LO, w[:, 1:2], ALU.mult, ALU.add))
        v.tensor_scalar(w[:, 1:2], w[:, 1:2], 3.1415925, -3.1415925, ALU.min, ALU.max).then_inc(self.angle, 1)
        dve.wait_ge(self.sines, 2)
        cs = self.cos_sin
        v.tensor_copy(cs[:, 0, 1:2], w[:, 2:3])
        chain(v.tensor_tensor(w[:, 4:5], w[:, 3:4], w[:, 3:4], ALU.mult))
        chain(v.tensor_scalar(cs[:, 0, 0:1], w[:, 4:5], -2.0, 1.0, ALU.mult, ALU.add))
        for j in range(1, 6):
            c, s_ = cs[:, j - 1, 0:1], cs[:, j - 1, 1:2]
            chain(v.tensor_tensor(w[:, 5:6], s_, s_, ALU.mult))
            v.tensor_scalar(cs[:, j, 0:1], w[:, 5:6], -2.0, 1.0, ALU.mult, ALU.add)
            chain(v.tensor_scalar(cs[:, j, 1:2], s_, c, 2.0, ALU.mult, ALU.mult))
        chain(v.tensor_scalar(cs[:, :, 2], cs[:, :, 1], -1.0, None, ALU.mult))
        norm_vector(k, dve, self.n)
        dve.wait_ge(self.p_read, 2)
        part = self.part[:, :, :].rearrange("p c (b s) -> p c b s", s=S)
        for j in range(6):
            d = 1 << j
            old = self.state[:, j % 2, :, :].rearrange("p c (b s) -> p c b s", s=S)
            new = self.state[:, 1 - j % 2, :, :].rearrange("p c (b s) -> p c b s", s=S)
            c, s_, ms = (cs[:, j, q:q + 1] for q in range(3))
            for q in range(2):
                v.scalar_tensor_tensor(part[:, q, :, d:S], old[:, q, :, 0:S - d], c, old[:, q, :, d:S], ALU.mult, ALU.add)
            chain(v.tensor_copy(self.state[:, 1 - j % 2, :, :].rearrange("p c (b s) -> p (c b) s", s=S)[:, :, 0:d],
                                self.state[:, j % 2, :, :].rearrange("p c (b s) -> p (c b) s", s=S)[:, :, 0:d]))
            v.scalar_tensor_tensor(new[:, 0, :, d:S], old[:, 1, :, 0:S - d], ms, part[:, 0, :, d:S], ALU.mult, ALU.add)
            chain(v.scalar_tensor_tensor(new[:, 1, :, d:S], old[:, 0, :, 0:S - d], s_, part[:, 1, :, d:S],
                                         ALU.mult, ALU.add))
        st = self.state[:, 0, :, :]
        v.tensor_tensor(self.part[:, :, :], st, st, ALU.mult).then_inc(self.squared, 1)
        dve.wait_ge(self.ms_full, 1)
        v.tensor_scalar(self.rms[:, :], k.ps_m[:, 0:NT], 1.0 / P, 1e-6, ALU.mult, ALU.add).then_inc(self.ms_eps, 1)
        dve.wait_ge(self.cosines, 1)
        for q in range(2):
            v.scalar_tensor_tensor(self.condT[64 * q:64 * q + 64, :], self.state[:, 0, q, :], self.norm_w[:, q:q + 1],
                                   self.spread[:, :], ALU.mult, ALU.mult).then_inc(self.cond, 1)
        for t in range(NT):
            dve.wait_ge(self.mix_full, t + 1)
            v.tensor_tensor(self.mix[:, t, :], k.ps_s[:, 0:self.W], self.ctl_b[:, :], ALU.add).then_inc(self.mix_ready, 1)
        dve.wait_ge(self.rows_in, 16 * B)
        for j in range(4):
            dst = self.conv if j == 0 else self.prod
            chain(v.tensor_tensor(dst[:, :, 16:48], self.rows[:, j:j + S, 16:48],
                                  self.conv_w[:, j:j + 1, 16:48].to_broadcast([P, S, 32]), ALU.mult))
            if j:
                last = v.tensor_tensor(self.conv[:, :, 16:48], self.conv[:, :, 16:48], self.prod[:, :, 16:48], ALU.add)
                if j < 3:
                    chain(last)
        last.then_inc(self.conved, 1)
        dve.wait_ge(self.squares, 1)
        for q in range(2):
            last = v.tensor_reduce(self.ssq[:, q, :], self.prod[:, :, 16 * q:16 * q + 16], AX.X, ALU.add)
        chain(last)
        v.tensor_scalar(self.ssq[:, :, :], self.ssq[:, :, :], 1e-6, None, ALU.add).then_inc(self.rooted, 1)
        dve.wait_ge(self.gated, 1)
        beta, g = self.gates[:, :, 0], self.gates[:, :, 1]
        v.scalar_tensor_tensor(self.neg_gb[:, :], beta, -1.0, g, ALU.mult, ALU.mult)
        v.tensor_tensor(self.kv[:, :, 0, :], self.act[:, :, 32:48],
                        self.gates[:, :, 0:1].to_broadcast([P, S, 16]), ALU.mult)
        dve.wait_ge(self.roots, 1)
        chain(v.reciprocal(self.ssq_inv[:, :, :], self.ssq[:, :, :]))
        v.memset(self.tmp[:, :, :], 0.0)
        v.memset(self.hist[:, self.RING - 1, :, :], 0.0)
        inv = self.ssq_inv[:, :, :]
        v.tensor_tensor(self.kv[:, :, 1, :], self.act[:, :, 16:32],
                        inv[:, 1, :].rearrange("p (s o) -> p s o", o=1).to_broadcast([P, S, 16]), ALU.mult)
        last = v.tensor_tensor(self.qn[:, :, :], self.act[:, :, 0:16],
                               inv[:, 0, :].rearrange("p (s o) -> p s o", o=1).to_broadcast([P, S, 16]), ALU.mult)
        chain(last)
        v.nop().then_inc(self.ready, 1)
        last = v.tensor_tensor(self.prod[:, 1:S, 0:16], self.kv[:, 1:S, 1, :], self.kv[:, 0:S - 1, 1, :], ALU.mult)
        v.memset(self.past[:, :], 0.0)
        v.memset(self.u[:, :], 0.0)
        v.memset(self.coef[:, 0:1, :], 0.0)
        v.tensor_tensor(self.coef[:, 1:S, 0], self.neg_gb[:, 1:S], self.gates[:, 0:S - 1, 1], ALU.mult)
        chain(last)
        chain(v.tensor_reduce(self.ssq[:, 0, 1:S], self.prod[:, 1:S, 0:16], AX.X, ALU.add))
        chain(v.tensor_tensor(self.coef[:, 1:S, 1], self.neg_gb[:, 1:S], self.ssq[:, 0, 1:S], ALU.mult))
        R, H = self.RING, self.RING // 2
        col = lambda tile, at: tile[:, ds(at, 1)] if not isinstance(at, int) else tile[:, at:at + 1]

        def keys_at(t):
            return self.kv[:, ds(t, 1), 1, :].to_broadcast([P, 16, 16])

        def outputs(half):
            stand(k, dve, self.qs_done, half * H + H)
            lo = H * (half % 2) if isinstance(half, int) else H * self.half_slot
            v.tensor_reduce(self.o[:, ds(half * H, H), :].rearrange("p s d -> p (s d)"),
                            self.qs[:, lo:lo + H, :, :].rearrange("p s v k -> p (s v) k"), AX.X, ALU.add)\
                .then_inc(self.qs_read, 1)

        def recur(i, start, end):
            for j in range(R):
                t = i * R + j
                prev = self.hist[:, (j - 1) % R, :, :]
                done = 5 * R * i + 5 * j
                if not (start and j == 0):
                    stand(k, dve, self.step, done)
                v.scalar_tensor_tensor(self.begun[:, :], self.past[:, :], self.coef[:, ds(t, 1), 0],
                                       self.kv[:, ds(t, 1), 0, :].rearrange("p a d -> p (a d)"), ALU.mult, ALU.add)\
                    .then_inc(self.step, 1)
                if not (start and j == 0):
                    stand(k, dve, self.state_done, t)
                ahead = not (end and j == R - 1)
                if ahead:
                    v.tensor_tensor(self.tmp[:, :, :], prev, keys_at(t + 1), ALU.mult).then_inc(self.step, 1)
                stand(k, dve, self.step, done + 1)
                v.scalar_tensor_tensor(self.u[:, :], self.u[:, :], self.coef[:, ds(t, 1), 1], self.begun[:, :],
                                       ALU.mult, ALU.add).then_inc(self.step, 1)
                stand(k, dve, self.step, done + 2 + ahead)
                v.tensor_tensor(self.outer[:, :, :], self.u[:, :].rearrange("p (v o) -> p v o", o=1)
                                .to_broadcast([P, 16, 16]), keys_at(t), ALU.mult).then_inc(self.step, 1)
                if ahead:
                    v.tensor_reduce(self.past[:, :], self.tmp[:, :, :], AX.X, ALU.add).then_inc(self.step, 1)
                stand(k, dve, self.step, done + 3 + ahead)
                v.scalar_tensor_tensor(self.hist[:, j, :, :], prev, self.gates[:, ds(t, 1), 1], self.outer[:, :, :],
                                       ALU.mult, ALU.add).then_inc(self.state_done, 1)
                if j % H == 1 and not (start and j < H):
                    self.half_slot = 1 - j // H
                    outputs(2 * i + j // H - 1)

        self.rounds(dve, recur)
        outputs(S // H - 1)
        dve.wait_ge(self.qs_read, S // H)
        chain(v.tensor_tensor(self.o_sq[:, :, :], self.o[:, :, :], self.o[:, :, :], ALU.mult))
        chain(v.tensor_reduce(self.ssq[:, 0, :], self.o_sq[:, :, :], AX.X, ALU.add))
        v.tensor_scalar(self.ssq[:, 0, :], self.ssq[:, 0, :], 1.0 / 16, 1e-6, ALU.mult, ALU.add).then_inc(self.o_ms, 1)
        dve.wait_ge(self.o_root, 1)
        chain(v.reciprocal(self.ssq_inv[:, 0, :], self.ssq[:, 0, :]))
        chain(v.tensor_tensor(self.o[:, :, :], self.o[:, :, :],
                              inv[:, 0, :].rearrange("p (s o) -> p s o", o=1).to_broadcast([P, S, 16]), ALU.mult))
        v.tensor_tensor(self.o_sq[:, :, :], self.o[:, :, :],
                        self.o_w[:, :].rearrange("p (o d) -> p o d", o=1).to_broadcast([P, S, 16]), ALU.mult)\
            .then_inc(self.o_normed, 1)
        dve.wait_ge(self.gate_silu, NT)
        dve.wait_ge(self.o_back, 16 * B)
        for t in range(NT):
            v.tensor_tensor(self.o_tok[:, t, :], self.o_tok[:, t, :], self.gate[:, t, :], ALU.mult)\
                .then_inc(self.gated_out, 1)
        finish(k, dve, lambda t: self.bo[:, :], lambda t: k.ps_s[:, t * BANK:t * BANK + D], self.n)


class Experts:

    E = 8
    HC = None
    LAG = None
    RING = None
    LOADS = None

    def experts_memory(self, k, sb, name):
        sem = k.sem
        self.logits = sb("logits", [P, NT, 8])
        self.top = sb("top", [P, NT, 8])
        self.top_i = sb("top_i", [P, NT, 8], U32)
        self.top_f = sb("top_f", [P, NT, 8])
        self.gap = sb("gap", [P, NT])
        self.second = sb("second", [P, NT])
        self.total = sb("total", [P, NT])
        self.p1 = sb("p1", [P, NT])
        self.p2 = sb("p2", [P, NT])
        self.index_i = sb("index_i", [P, 8], U32)
        self.index = sb("index", [P, 8])
        self.pick = sb("pick", [P, NT, 8])
        self.w = sb("w", [P, NT, 8])
        self.wT = sb("wT", [8, T])
        self.wide = sb("wide", [P, 8, T])
        self.hid = sb("hid", [P, 4, T])
        self.yT = sb("yT", [P, FC, T])
        self.R, self.U = k.rounds, k.units
        k.rounds, k.units = k.rounds + 1, k.units + self.E * self.HC
        self.router_in = sem(name + "router_in")

        def shared(n):
            if n not in k.shared:
                k.shared[n] = sem("experts_" + n)
            return k.shared[n]

        self.w_counted = shared("w_counted")
        self.logits_full = shared("logits_full")
        self.gapped = shared("gapped")
        self.second_done = shared("second_done")
        self.w_ready = shared("w_ready")
        self.wT_full = shared("wT_full")
        self.wT_done = shared("wT_done")
        self.wide_full = shared("wide_full")
        self.wide_done = shared("wide_done")
        self.hid_full = shared("hid_full")
        self.hid_act = shared("hid_act")
        self.hid_done = shared("hid_done")
        self.y_unit = shared("y_unit")
        self.yT_act = shared("yT_act")
        self.yT_dve = shared("yT_dve")
        self.e_in = [sem(name + "e_in0"), sem(name + "e_in1")]

    def bodies(self, eng, body):
        body(0, True, False)
        with eng.Fori(1, self.E // 2 - 1) as i:
            body(i, False, False)
        body(self.E // 2 - 1, False, True)

    def sync_experts(self, k, sp):
        for e in range(2):
            self.load(sp, e, e)
        with sp.Fori(1, self.E // 2) as i:
            for p in range(2):
                sp.wait_ge(self.y_unit, self.U + self.HC * (2 * (i - 1) + p + 1))
                self.load(sp, 2 * i + p, p)

    def gpsimd(self, pool):
        k = self.k
        pool.wait_ge(k.x_done, self.n)
        k.nc.gpsimd.iota(self.index_i[:, :], pattern=[[1, 8]], base=0, channel_multiplier=0).then_inc(self.w_counted, 1)
        norm_pool(k, pool, self.n)

    def choose(self, k, dve, bias):
        v = k.nc.vector
        chain = lambda ins: link(k, dve, ins)
        dve.wait_ge(self.w_counted, self.R + 1)
        v.tensor_copy(self.index[:, :], self.index_i[:, :])
        dve.wait_ge(self.logits_full, self.R + 1)
        E = self.ROUTED
        if E < 8:
            v.memset(self.logits[:, :, E:8], -3.0e38)
        chain(v.tensor_tensor(self.logits[:, :, 0:E], k.ps_m[:, 0:NT * 8].rearrange("p (t e) -> p t e", e=8)[:, :, 0:E],
                              bias.to_broadcast([P, NT, E]), ALU.add))
        for t in range(NT):
            last = v.max(self.top[:, t, :], self.logits[:, t, :])
        chain(last)
        for t in range(NT):
            v.max_index(self.top_i[:, t, :], self.top[:, t, :], self.logits[:, t, :])
        v.tensor_tensor(self.gap[:, :], self.top[:, :, 1], self.top[:, :, 0], ALU.subtract).then_inc(self.gapped, 1)
        chain(v.tensor_copy(self.index[:, :], self.index_i[:, :]))
        dve.wait_ge(self.second_done, self.R + 1)
        chain(v.tensor_copy(self.top_f[:, :, :], self.top_i[:, :, :]))
        chain(v.tensor_scalar(self.total[:, :], self.second[:, :], 1.0, None, ALU.add))
        chain(v.reciprocal(self.p1[:, :], self.total[:, :]))
        chain(v.tensor_tensor(self.p2[:, :], self.second[:, :], self.p1[:, :], ALU.mult))
        for t in range(NT):
            v.tensor_scalar(self.w[:, t, :], self.index[:, :], self.top_f[:, t, 0:1], self.p1[:, t:t + 1],
                            ALU.is_equal, ALU.mult)
            last = v.tensor_scalar(self.pick[:, t, :], self.index[:, :], self.top_f[:, t, 1:2], self.p2[:, t:t + 1],
                                   ALU.is_equal, ALU.mult)
        chain(last)
        last = v.tensor_tensor(self.w[:, :, :], self.w[:, :, :], self.pick[:, :, :], ALU.add)
        if E < 8:
            chain(last)
            last = v.memset(self.w[:, :, E:8], 1.0)
        last.then_inc(self.w_ready, 1)
        dve.wait_ge(self.wT_full, self.R + 1)
        v.tensor_copy(self.wT[:, :], k.ps_o[0:8, :]).then_inc(self.wT_done, 1)

    def spread(self, k, pe):
        nc = k.nc
        pe.wait_ge(self.w_ready, self.R + 1)
        for t in range(NT):
            last = nc.tensor.matmul(k.ps_o[0:8, t * P:(t + 1) * P], self.w[:, t, :], k.ident[:, :], start=True, stop=True)
        last.then_inc(self.wT_full, 1)
        pe.wait_ge(self.wT_done, self.R + 1)
        for e in range(self.E):
            if e >= 2:
                pe.wait_ge(self.wide_done, self.E * self.R + e - 1)
            nc.tensor.matmul(k.ps_t[:, e % 2, :], k.ident[0:8, e:e + 1].to_broadcast([8, P]), self.wT[:, :],
                             start=True, stop=True).then_inc(self.wide_full, 1)
        pe.wait_ge(self.wide_done, self.E * (self.R + 1))

    def act_spread(self, k, act):
        for e in range(self.E):
            act.wait_ge(self.wide_full, self.E * self.R + e + 1)
            k.nc.scalar.activation(self.wide[:, e, :], k.ps_t[:, e % 2, :], ACT.Copy).then_inc(self.wide_done, 1)

    def tensor_experts(self, k, pe, begun):
        HC, L = self.HC, self.LAG

        def first(i, u):
            e, c = u // HC % 2, u % HC
            if c == 0:
                stand(k, pe, self.e_in[e], 16 * self.LOADS * ((i + u // (2 * HC)) + 1))
            n = 2 * HC * i + u
            if not (isinstance(n, int) and n < self.RING):
                stand(k, pe, self.hid_done, n + (self.U - self.RING + 1))
            self.pe_first(k, pe, e, c, u % self.RING).then_inc(self.hid_full, 1)

        for u in range(L):
            first(0, u)

        def body(i, start, end):
            for u in range(2 * HC):
                if not (end and u + L >= 2 * HC):
                    first(i, u + L)
                stand(k, pe, self.hid_done, 2 * HC * i + (self.U + u + 1))
                e, c = u // HC, u % HC
                for f in range(FC):
                    lhsT, rhs = self.second_operands(e, c, f, u % 4)
                    last = k.nc.tensor.matmul(k.ps_t[:, f, :], lhsT, rhs, start=(start and u == 0 and not begun),
                                              stop=(end and u == 2 * HC - 1))
                last.then_inc(self.y_unit, 1)

        self.bodies(pe, body)
        pe.wait_ge(self.yT_act, self.R + 1)
        pe.wait_ge(self.yT_dve, self.R + 1)
        for t in range(NT):
            for f in range(FC):
                last = k.nc.tensor.transpose(k.ps_s[:, t * BANK + f * P:t * BANK + (f + 1) * P],
                                             self.yT[:, f, t * P:(t + 1) * P], k.ident[:, :])
            last.then_inc(k.y_full, 1)

    def scalar_experts(self, k, act):
        HC = self.HC

        def body(i, start, end):
            for u in range(2 * HC):
                stand(k, act, self.hid_full, 2 * HC * i + (self.U + u + 1))
                self.act_unit(k, act, 2 * i + u // HC, u % HC, u % self.RING).then_inc(self.hid_act, 1)

        self.bodies(act, body)
        act.wait_ge(self.y_unit, self.U + self.E * HC)
        k.nc.scalar.activation(self.yT[:, 0, :], k.ps_t[:, 0, :], ACT.Copy).then_inc(self.yT_act, 1)

    def vector_experts(self, k, dve):
        HC = self.HC

        def body(i, start, end):
            for u in range(2 * HC):
                n = 2 * HC * i + u
                stand(k, dve, self.hid_act, n + (self.U + 1))
                self.dve_unit(k, dve, 2 * i + u // HC, u % HC, u, n).then_inc(self.hid_done, 1)

        self.bodies(dve, body)
        dve.wait_ge(self.y_unit, self.U + self.E * HC)
        k.nc.vector.tensor_copy(self.yT[:, 1, :], k.ps_t[:, 1, :]).then_inc(self.yT_dve, 1)


class StageC(Experts):

    HC, LAG, RING, LOADS = 4, 2, 4, 2
    ROUTED = 8

    def __init__(self, k, n):
        self.k, self.n = k, n
        with ExitStack() as st:
            sb = lambda name, shape, dt=F32: k.sb("c_" + name, shape, dt, st)
            self.experts_memory(k, sb, "c_")
            self.rw1 = sb("rw1", [P, FC, D])
            self.rb1 = sb("rb1", [P, FC])
            self.rw2 = sb("rw2", [P, FC, 8])
            self.rb2 = sb("rb2", [P, 1, 8])
            self.b1 = sb("b1", [P, 8, 4])
            self.b2 = sb("b2", [8, D])
            self.w1 = sb("w1", [P, 2, FC, 512])
            self.w2 = sb("w2", [P, 2, 4, D])
            self.rh = sb("rh", [P, FC, T])
            self.sg = sb("sg", [P, 4, T])
            self.rh_full = k.sem("c_rh_full")
            self.rh_done = k.sem("c_rh_done")

    def load(self, sp, e, p):
        a = self.k.a
        for src, dst in (("c_w1", self.w1), ("c_w2", self.w2)):
            at = a[src][e] if isinstance(e, int) else a[src][ds(e, 1)].rearrange("a p f m -> (a p) f m")
            sp.dma_start(dst[:, p, :, :], at).then_inc(self.e_in[p], 16)

    def sync(self, sp):
        k, a = self.k, self.k.a
        sp.wait_ge(k.x_done, self.n)
        for name, tile in (("rw1", self.rw1), ("rb1", self.rb1), ("rw2", self.rw2), ("b1", self.b1), ("b2", self.b2)):
            sp.dma_start(tile[...], a["c_" + name]).then_inc(self.router_in, 16)
        sp.dma_start(self.rb2[:, 0, :], a["c_rb2"].partition_broadcast(P)).then_inc(self.router_in, 16)
        self.sync_experts(k, sp)

    def tensor(self, pe):
        k, nc = self.k, self.k.nc
        norm_tensor(k, pe, self.n)
        wait_norm(k, pe, self.n)
        pe.wait_ge(self.router_in, 96)
        for m in range(FC):
            for f in range(FC):
                last = nc.tensor.matmul(k.ps_s[:, m * BANK:(m + 1) * BANK], self.rw1[:, f, m * P:(m + 1) * P],
                                        k.xnT[:, f, :], start=(f == 0), stop=(f == FC - 1))
            last.then_inc(self.rh_full, 1)
        pe.wait_ge(self.rh_done, 2)
        for t in range(NT):
            for f in range(FC):
                last = nc.tensor.matmul(k.ps_m[:, t * 8:(t + 1) * 8], self.rh[:, f, t * P:(t + 1) * P], self.rw2[:, f, :],
                                        start=(f == 0), stop=(f == FC - 1))
        last.then_inc(self.logits_full, 1)
        self.spread(k, pe)
        for f in range(FC):
            nc.tensor.matmul(k.ps_t[:, f, :], self.b2[:, f * P:(f + 1) * P], self.wT[:, :], start=True, stop=False)
        self.tensor_experts(k, pe, True)

    def pe_first(self, k, pe, e, c, r):
        for f in range(FC):
            last = k.nc.tensor.matmul(k.ps_s[:, r * BANK:(r + 1) * BANK], self.w1[:, e, f, c * P:(c + 1) * P],
                                      k.xnT[:, f, :], start=(f == 0), stop=(f == FC - 1))
        return last

    def second_operands(self, e, c, f, h):
        return self.w2[:, e, c, f * P:(f + 1) * P], self.hid[:, h, :]

    def scalar(self, act):
        k, nc = self.k, self.k.nc
        norm_scalar(k, act, self.n)
        act.wait_ge(self.router_in, 96)
        for m in range(FC):
            act.wait_ge(self.rh_full, m + 1)
            nc.scalar.activation(self.rh[:, m, :], k.ps_s[:, m * BANK:(m + 1) * BANK], ACT.Silu,
                                 bias=self.rb1[:, m:m + 1]).then_inc(self.rh_done, 1)
        act.wait_ge(self.gapped, self.R + 1)
        nc.scalar.activation(self.second[:, :], self.gap[:, :], ACT.Exp).then_inc(self.second_done, 1)
        self.act_spread(k, act)
        self.scalar_experts(k, act)

    def act_unit(self, k, act, e, c, r):
        b = self.b1[:, e, c:c + 1] if isinstance(e, int) else self.b1[:, ds(e, 1), c]
        return k.nc.scalar.activation(self.sg[:, r, :], k.ps_s[:, r * BANK:(r + 1) * BANK], ACT.Silu, bias=b)

    def dve_unit(self, k, dve, e, c, u, n):
        w = self.wide[:, e, :] if isinstance(e, int) else self.wide[:, ds(e, 1), :].rearrange("p a t -> p (a t)")
        return k.nc.vector.tensor_tensor(self.hid[:, u % 4, :], self.sg[:, u % 4, :], w, ALU.mult)

    def vector(self, dve):
        k = self.k
        norm_vector(k, dve, self.n)
        dve.wait_ge(self.router_in, 96)
        self.choose(k, dve, self.rb2[:, :, :])
        self.vector_experts(k, dve)
        finish(k, dve, lambda t: k.xn[:, t, :], lambda t: k.ps_s[:, t * BANK:t * BANK + D], self.n)


class StageD(Attention):

    name = "d_"
    G = 8
    FOLDED = True
    SCALE = 0.25

    def __init__(self, k, n):
        self.n, self.k = n, k
        sem = k.sem
        with ExitStack() as st:
            sb = lambda name, shape, dt=F32: k.sb("d_" + name, shape, dt, st)
            self.wq = sb("wq", [P, FC, D])
            self.wk = sb("wk", [P, FC, D])
            self.wv = sb("wv", [P, FC, D])
            self.wo = sb("wo", [P, 2, D])
            self.bq = sb("bq", [P, FC])
            self.bk = sb("bk", [P, FC])
            self.bv = sb("bv", [P, 2])
            self.bo = sb("bo", [P, D])
            self.k_rot = sb("k_rot", [P, 2, M])
            self.q_rot = sb("q_rot", [P, 2, S])
            self.head_of = sb("head_of", [P, 8])
            self.ctxT = sb("ctxT", [P, 2, FC, M])
            self.kT = sb("kT", [P, 2, FC, M])
            self.v = sb("v", [P, 2, MC, D])
            self.k_raw = sb("k_raw", [P, 2, BANK])
            self.k_swap = sb("k_swap", [P, 2, BANK])
            self.q_raw = sb("q_raw", [P, FC, T])
            self.q_swap = sb("q_swap", [P, FC, T])
            self.qm = sb("qm", [P, 2, FC, 8, S])
            self.o = sb("o", [P, 2, 8, 16])
            self.oT = sb("oT", [P, 2, T])
            self.parts = sb("parts", [P, P])
            self.fold = sb("fold", [P, 32])
            self.attention_memory(k, st)
        self.parted = sem("d_parted")
        self.unfolded = sem("d_unfolded")
        self.w_in = sem("d_w_in")
        self.late_in = sem("d_late_in")
        self.q_full = sem("d_q_full")
        self.q_read = sem("d_q_read")
        self.q_ready = sem("d_q_ready")
        self.qm_ready = sem("d_qm_ready")
        self.k_swapped = sem("d_k_swapped")
        self.k_part = sem("d_k_part")
        self.k_roped = sem("d_k_roped")
        self.ctxT_in = [sem("d_ctxT_in0"), sem("d_ctxT_in1")]
        self.first_fills = 15 + 15 + 16
        self.fills = 32

    def fills_before(self, s, first, last):
        g = s % 8
        if g == 0:
            return [] if first and s == 0 else [("o", 1 - s // 8)]
        return [] if last and s >= 8 else [("k", 1 - s // 8, g, 1 + s // 8)]

    def fills_after(self, s, first, last):
        g = s % 8
        if last and s >= 8:
            return []
        return [("k", 1 - s // 8, 0, 1 + s // 8)] if g == 0 else [("v", 1 - s // 8, g - 1, 1 + s // 8)]

    def values(self, s, c):
        g = s % 8
        return self.v[0:keys(c), s // 8, c, g * 32:(g + 1) * 32]

    def pe_value(self, k, pe, n, s, q):
        pe.wait_ge(self.moved_act if q % 2 else self.moved_dve, 2 * n + 1 + q // 2)
        for j, c in enumerate(QUADS[q]):
            last = k.nc.tensor.matmul(k.ps_o[32 * j:32 * j + 32, 0:P], self.values(s, c), self.pT[0:keys(c), c, :],
                                      start=(c < 4), stop=(c + 4 >= MC))
        return last

    def pe_fold(self, k, pe, n):
        stand(k, pe, self.unfolded, n + 1)
        k.nc.tensor.matmul(k.ps_o[:, P:P + 32], self.parts[:, :], self.fold[:, :], start=True, stop=True)\
            .then_inc(self.valued, 1)

    def dve_unfold(self, k, dve):
        k.nc.vector.tensor_copy(self.parts[:, :], k.ps_o[:, 0:P]).then_inc(self.unfolded, 1)

    def sync(self, sp):
        k, a = self.k, self.k.a
        sp.wait_ge(k.x_done, self.n)

        def load(b, p):
            srcT = a["ctxT"][b] if isinstance(b, int) else a["ctxT"][ds(b, 1)].rearrange("a p f m -> (a p) f m")
            if not (isinstance(b, int) and b < 2):
                sp.wait_ge(self.scored, 8 * (b - 2) + 2)
            sp.dma_start(self.ctxT[:, p, :, :], srcT).then_inc(self.ctxT_in[p], 16)

        for name, tile in (("wq", self.wq), ("bq", self.bq), ("q_rot", self.q_rot), ("head_of", self.head_of),
                           ("fold", self.fold),
                           ("wk", self.wk), ("bk", self.bk), ("wv", self.wv)):
            sp.dma_start(tile[...], a["d_" + name]).then_inc(self.w_in, 16)
        load(0, 0)
        sp.dma_start(self.k_rot[:, :, :], a["d_k_rot"]).then_inc(self.w_in, 16)
        load(1, 1)
        sp.dma_start(self.wo[:, :, :], a["d_wo"]).then_inc(self.late_in, 16)
        sp.dma_start(self.bv[:, :], a["d_bv"]).then_inc(self.late_in, 16)
        sp.dma_start(self.bo[:, :], a["d_bo"].partition_broadcast(P)).then_inc(self.late_in, 16)
        with sp.Fori(1, B // 2) as i:
            load(2 * i, 0)
            load(2 * i + 1, 1)

    def gpsimd(self, pool):
        k = self.k
        norm_pool(k, pool, self.n)
        pool.wait_ge(self.w_in, 144)
        part = Count(self.k_part)

        def rope(r, g):
            c, w = KB[g % 4]
            raw, swap = self.k_raw[:, g % 2, 0:w], self.k_swap[:, g % 2, 0:w]
            stand(k, pool, self.k_swapped, r + 1)
            part.up(k.nc.gpsimd.tensor_tensor(raw, raw, self.k_rot[:, 0, c:c + w], ALU.mult))
            part.up(k.nc.gpsimd.tensor_tensor(swap, swap, self.k_rot[:, 1, c:c + w], ALU.mult))
            stand(k, pool, self.k_part, part.now())
            return k.nc.gpsimd.tensor_tensor(self.kT[:, self.rope_p, g // 4, c:c + w], raw, swap, ALU.add)

        self.rope_p = 0
        for g in range(8):
            rope(g, g).then_inc(self.k_roped, 1)
        with pool.Fori(0, B // 2 - 1) as i:
            part.restart(16 + 32 * i)
            for p in range(2):
                self.rope_p = 1 - p
                for g in range(8):
                    rope(16 * i + 8 * p + 8 + g, g).then_inc(self.k_roped, 1)
        part.restart(16 * (B - 1))
        self.rope_p = 1
        for g in range(8):
            rope(8 * (B - 1) + g, g).then_inc(self.k_roped, 1)

    def tensor(self, pe):
        norm_tensor(self.k, pe, self.n)
        self.tensor_loop(self.k, pe)

    def pe_before(self, k, pe, fill):
        nc = k.nc
        wait_norm(k, pe, self.n)
        pe.wait_ge(self.w_in, 144)
        for m in range(FC):
            for f in range(FC):
                last = nc.tensor.matmul(k.ps_s[:, m * BANK:(m + 1) * BANK], self.wq[:, f, m * P:(m + 1) * P],
                                        k.xnT[:, f, :], start=(f == 0), stop=(f == FC - 1))
            last.then_inc(self.q_full, 1)
        for g in range(8):
            fill(0, "k", 0, g, 0)
        for g in range(7):
            fill(0, "v", 0, g, 0)
        pe.wait_ge(self.q_read, 2)
        pe.wait_ge(self.misc_read, 15)
        pe.wait_ge(self.qm_ready, 1)
        pe.wait_ge(self.k_roped, 4)

    def pe_ready(self, k, pe, i, s1, misc):
        b8 = 16 * i + 8 * (s1 // 8)
        if s1 % 8 == 0:
            stand(k, pe, self.qm_ready, 2 * i + s1 // 8 + 1)
            stand(k, pe, self.k_roped, b8 + 4)
        elif s1 % 8 == 4:
            stand(k, pe, self.k_roped, b8 + 8)

    def pe_scores(self, k, pe, i, s, blocks):
        p, f, j = s // 8, s % 8 // 4, 2 * (s % 4)
        for c, w in blocks:
            last = k.nc.tensor.matmul(k.ps_s[:, c:c + w], self.qm[:, p, f, j:j + 2, :].rearrange("p j s -> p (j s)"),
                                      self.kT[:, p, f, c:c + w], start=True, stop=True)
        return last

    def pe_misc(self, k, pe, i, kind, *which):
        nc = k.nc
        if kind == "o":
            p = which[0]
            stand(k, pe, self.scaled, 16 * i + (8 if p == 0 else 0))
            return nc.tensor.transpose(k.ps_m[:, 0:P], self.o[:, p, :, :].rearrange("p j d -> p (j d)"), k.ident[:, :])
        p, g, ahead = which
        if kind == "k":
            if g == 0:
                stand(k, pe, self.ctxT_in[p], 16 * (i + ahead // 2 + 1))
            c, w = KB[g % 4]
            m = g // 4
            for f in range(FC):
                last = nc.tensor.matmul(k.ps_m[:, 0:w], self.wk[:, f, m * P:(m + 1) * P], self.ctxT[:, p, f, c:c + w],
                                        start=(f == 0), stop=(f == FC - 1))
            return last
        for j, c in enumerate(range(2 * g, min(2 * g + 2, MC))):
            for f in range(FC):
                last = nc.tensor.matmul(k.ps_m[0:keys(c), j * D:(j + 1) * D], self.ctxT[:, p, f, c * P:c * P + keys(c)],
                                        self.wv[:, f, :], start=(f == 0), stop=(f == FC - 1))
        return last

    def pe_after(self, k, pe, fill, misc):
        nc = k.nc
        self.pe_fold(k, pe, self.G * B - 1)
        fill(B // 2, "o", 1)
        pe.wait_ge(self.misc_read, misc.now())
        pe.wait_ge(self.late_in, 48)
        for t in range(NT):
            for p in range(2):
                last = nc.tensor.matmul(k.ps_s[:, t * BANK:t * BANK + D], self.oT[:, p, t * P:(t + 1) * P],
                                        self.wo[:, p, :], start=(p == 0), stop=(p == 1))
            last.then_inc(k.y_full, 1)

    def scalar(self, act):
        norm_scalar(self.k, act, self.n)
        self.scalar_loop(self.k, act)

    def act_before(self, k, act, read):
        act.wait_ge(self.w_in, 144)
        for m in range(FC):
            act.wait_ge(self.q_full, m + 1)
            k.nc.scalar.activation(self.q_raw[:, m, :], k.ps_s[:, m * BANK:(m + 1) * BANK], ACT.Identity,
                                   bias=self.bq[:, m:m + 1]).then_inc(self.q_read, 1)
        for g in range(8):
            read(0, "k", 0, g, 0)
        for g in range(7):
            read(0, "v", 0, g, 0)

    def act_misc(self, k, act, i, kind, *which):
        nc = k.nc
        if kind == "o":
            b = 2 * i if which[0] == 0 else 2 * i - 1
            if isinstance(i, int):
                act.wait_ge(self.late_in, 48)
            for par in range(2):
                dst = self.oT[:, par, b * S:(b + 1) * S] if isinstance(b, int) else self.oT[:, par, ds(b * S, S)]
                last = nc.scalar.activation(dst, k.ps_m[:, par * S:(par + 1) * S], ACT.Identity,
                                            bias=self.bv[:, par:par + 1])
            return last
        p, g, ahead = which
        if kind == "k":
            c, w = KB[g % 4]
            r = 16 * i + 8 * ahead + g
            if not (isinstance(r, int) and r < 2):
                stand(k, act, self.k_roped, r - 1)
            return nc.scalar.activation(self.k_raw[:, g % 2, 0:w], k.ps_m[:, 0:w], ACT.Identity,
                                        bias=self.bk[:, g // 4:g // 4 + 1])
        n = min(2, MC - 2 * g)
        r = keys(2 * g)
        return nc.scalar.activation(self.v[0:r, p, 2 * g:2 * g + n, :],
                                    k.ps_m[0:r, 0:n * D].rearrange("p (c d) -> p c d", d=D), ACT.Copy)

    def act_after(self, k, act, read):
        read(B // 2, "o", 1)

    def swap(self, k, dve, r, g, index):
        c, w = KB[g % 4]
        stand(k, dve, self.misc_read, index + 1)
        if not (isinstance(r, int) and r < 2):
            stand(k, dve, self.k_roped, r - 1)
        k.nc.vector.stream_shuffle(self.k_swap[:, g % 2, 0:w], self.k_raw[:, g % 2, 0:w], [j ^ 8 for j in range(32)])\
            .then_inc(self.k_swapped, 1)

    def separate(self, k, dve, b, p):
        at = slice(b * S, (b + 1) * S) if isinstance(b, int) else ds(b * S, S)
        for j in range(8):
            last = k.nc.vector.tensor_scalar(self.qm[:, p, :, j, :], self.q_raw[:, :, at], self.head_of[:, j:j + 1],
                                             None, ALU.mult)
        last.then_inc(self.qm_ready, 1)

    def dve_extra(self, k, dve, i, s, first, last):
        if last and s >= 8:
            return
        g, ahead = s % 8, 1 + s // 8
        if g == 0:
            self.separate(k, dve, 2 * i + ahead, 1 - s // 8)
        b16 = 32 * i + 16 * (s // 8)
        self.swap(k, dve, 16 * i + 8 * ahead + g, g, b16 + (15 if g == 0 else 14 + 2 * g))

    def dve_scale(self, k, dve, s):
        p, j = s // 8, s % 8
        for par in range(2):
            rows = slice(64 * par, 64 * par + 64)
            last_ = k.nc.vector.tensor_scalar(self.o[rows, p, j, :], k.ps_o[rows, P + 16 * par:P + 16 * par + 16],
                                              self.inv[rows, s % 2:s % 2 + 1], None, ALU.mult)
        return last_

    def vector(self, dve):
        k, v = self.k, self.k.nc.vector
        norm_vector(k, dve, self.n)
        dve.wait_ge(self.w_in, 144)
        dve.wait_ge(self.q_read, 2)
        link(k, dve, v.stream_shuffle(self.q_swap[:, :, :], self.q_raw[:, :, :], [j ^ 8 for j in range(32)]))
        for tile, j in ((self.q_raw, 0), (self.q_swap, 1)):
            view = tile[:, :, :].rearrange("p f (b s) -> p (f b) s", s=S)
            last = v.tensor_tensor(view, view, self.q_rot[:, j:j + 1, :].to_broadcast([P, FC * B, S]), ALU.mult)
        link(k, dve, last)
        link(k, dve, v.tensor_tensor(self.q_raw[:, :, :], self.q_raw[:, :, :], self.q_swap[:, :, :], ALU.add))
        self.separate(k, dve, 0, 0)
        for g in range(8):
            self.swap(k, dve, g, g, g)
        self.vector_loop(k, dve)
        dve.wait_ge(self.late_in, 48)
        finish(k, dve, lambda t: self.bo[:, :], lambda t: k.ps_s[:, t * BANK:t * BANK + D], self.n)


class StageE:

    H, DH = 8, 32

    def __init__(self, k, n):
        self.k, self.n = k, n
        sem = k.sem
        with ExitStack() as st:
            sb = lambda name, shape, dt=F32: k.sb("e_" + name, shape, dt, st)
            self.wqk = sb("wqk", [P, FC, 2 * D])
            self.bqk = sb("bqk", [P, 4])
            self.wvu = sb("wvu", [P, FC, 2 * D])
            self.bvu = sb("bvu", [P, 2 * D])
            self.scale = sb("scale", [P, D])
            self.wo = sb("wo", [P, FC, D])
            self.bo = sb("bo", [P, D])
            self.causal = sb("causal", [P, 1, 1, S])
            self.low = sb("low", [P, 4, T])
            self.high = sb("high", [P, 4, T])
            self.qk = sb("qk", [P, 4, T])
            self.vu = sb("vu", [P, NT, 2 * D])
            self.energy = sb("energy", [P, 2, 4, 2, S])
            self.o = sb("o", [P, NT, D])
            self.sq = sb("sq", [P, D])
            self.ss = sb("ss", [P, NT])
            self.inv = sb("inv", [P, NT])
            self.oT = sb("oT", [P, FC, T])
        self.w_in = sem("e_w_in")
        self.qk_full = sem("e_qk_full")
        self.qk_read = sem("e_qk_read")
        self.low_ready = sem("e_low_ready")
        self.exped = sem("e_exped")
        self.qk_ready = sem("e_qk_ready")
        self.vu_full = sem("e_vu_full")
        self.vu_raw = sem("e_vu_raw")
        self.vu_ready = sem("e_vu_ready")
        self.e_full = sem("e_e_full")
        self.e_ready = sem("e_e_ready")
        self.o_full = sem("e_o_full")
        self.o_ready = sem("e_o_ready")
        self.ss_done = sem("e_ss_done")
        self.rooted = sem("e_rooted")
        self.gated = sem("e_gated")
        self.turned = sem("e_turned")
        self.oT_done = sem("e_oT_done")

    def sync(self, sp):
        k, a = self.k, self.k.a
        sp.wait_ge(k.x_done, self.n)
        for name, tile in (("wqk", self.wqk), ("bqk", self.bqk), ("wvu", self.wvu), ("wo", self.wo),
                           ("causal", self.causal)):
            sp.dma_start(tile[...], a["e_" + name]).then_inc(self.w_in, 16)
        for name, tile in (("bvu", self.bvu), ("scale", self.scale), ("bo", self.bo)):
            sp.dma_start(tile[:, :], a["e_" + name].partition_broadcast(P)).then_inc(self.w_in, 16)

    def gpsimd(self, pool):
        norm_pool(self.k, pool, self.n)

    def tensor(self, pe):
        k, nc = self.k, self.k.nc
        norm_tensor(k, pe, self.n)
        wait_norm(k, pe, self.n)
        pe.wait_ge(self.w_in, 128)
        for m in range(4):
            for f in range(FC):
                last = nc.tensor.matmul(k.ps_s[:, m * BANK:(m + 1) * BANK], self.wqk[:, f, m * P:(m + 1) * P],
                                        k.xnT[:, f, :], start=(f == 0), stop=(f == FC - 1))
            last.then_inc(self.qk_full, 1)
        banks = (k.ps_m, k.ps_o)
        for t in range(NT):
            if t >= 2:
                pe.wait_ge(self.vu_raw, t - 1)
            for f in range(FC):
                last = nc.tensor.matmul(banks[t % 2][:, :], k.xnT[:, f, t * P:(t + 1) * P], self.wvu[:, f, :],
                                        start=(f == 0), stop=(f == FC - 1))
            last.then_inc(self.vu_full, 1)
        pe.wait_ge(self.qk_ready, 4)

        def energies(t):
            for par in range(2):
                tok = slice(t * P + par * S, t * P + (par + 1) * S)
                for h in range(8):
                    q, at = h % 4, (2 * t + h // 4) * S
                    rows = slice(32 * q, 32 * q + 32)
                    last = nc.tensor.matmul(k.ps_s[64 * par:64 * par + 64, q * BANK + at:q * BANK + at + S],
                                            self.qk[rows, 2 + h // 4, tok], self.qk[rows, h // 4, tok],
                                            start=True, stop=True)
            last.then_inc(self.e_full, 1)

        pe.wait_ge(self.vu_raw, NT)
        for t in range(NT):
            energies(t)
        for t in range(NT):
            pe.wait_ge(self.e_ready, t + 1)
            pe.wait_ge(self.vu_ready, t + 1)
            if t >= 2:
                pe.wait_ge(self.o_ready, t - 1)
            for par in range(2):
                rows = slice(64 * par, 64 * par + 64)
                for h in range(8):
                    last = nc.tensor.matmul(banks[t % 2][rows, h * 32:(h + 1) * 32], self.energy[rows, t % 2, h % 4, h // 4, :],
                                            self.vu[rows, t, h * 32:(h + 1) * 32], start=True, stop=True)
            last.then_inc(self.o_full, 1)
        for f in range(FC):
            for t in range(NT):
                if f == 0:
                    pe.wait_ge(self.gated, t + 1)
                last = nc.tensor.transpose(k.ps_t[:, f, t * P:(t + 1) * P], self.o[:, t, f * P:(f + 1) * P], k.ident[:, :])
            last.then_inc(self.turned, 1)
        pe.wait_ge(self.oT_done, 2)
        for t in range(NT):
            for f in range(FC):
                last = nc.tensor.matmul(k.ps_s[:, t * BANK:t * BANK + D], self.oT[:, f, t * P:(t + 1) * P],
                                        self.wo[:, f, :], start=(f == 0), stop=(f == FC - 1))
            last.then_inc(k.y_full, 1)

    def scalar(self, act):
        k, nc = self.k, self.k.nc
        norm_scalar(k, act, self.n)
        for m in range(4):
            act.wait_ge(self.low_ready, m + 1)
            nc.scalar.activation(self.low[:, m, :], self.low[:, m, :], ACT.Exp).then_inc(self.exped, 1)
        for t in range(NT):
            act.wait_ge(self.vu_raw, t + 1)
            nc.scalar.activation(self.vu[:, t, :], self.vu[:, t, :], ACT.Silu).then_inc(self.vu_ready, 1)
        for t in range(NT):
            act.wait_ge(self.o_ready, t + 1)
            if t:
                act.wait_ge(self.ss_done, t)
            nc.scalar.activation(self.sq[:, :], self.o[:, t, :], ACT.Square, accum_out=self.ss[:, t:t + 1])\
                .then_inc(self.ss_done, 1)
        act.wait_ge(self.ss_done, NT)
        nc.scalar.activation(self.ss[:, :], self.ss[:, :], ACT.Sqrt, scale=1.0 / D).then_inc(self.rooted, 1)
        for f in range(FC):
            act.wait_ge(self.turned, f + 1)
            nc.scalar.activation(self.oT[:, f, :], k.ps_t[:, f, :], ACT.Copy).then_inc(self.oT_done, 1)

    def vector(self, dve):
        k, v = self.k, self.k.nc.vector
        norm_vector(k, dve, self.n)
        dve.wait_ge(self.w_in, 128)
        banks = (k.ps_m, k.ps_o)
        for m in range(4):
            dve.wait_ge(self.qk_full, m + 1)
            bank = k.ps_s[:, m * BANK:(m + 1) * BANK]
            v.tensor_scalar(self.low[:, m, :], bank, self.bqk[:, m:m + 1], 0.0, ALU.add, ALU.min).then_inc(self.low_ready, 1)
            last = v.tensor_scalar(self.high[:, m, :], bank, self.bqk[:, m:m + 1], 0.0, ALU.add, ALU.max)
        link(k, dve, last)
        for m in range(4):
            dve.wait_ge(self.exped, m + 1)
            v.scalar_tensor_tensor(self.qk[:, m, :], self.low[:, m, :], -1.0, self.high[:, m, :], ALU.add, ALU.add)\
                .then_inc(self.qk_ready, 1)
        for t in range(NT):
            dve.wait_ge(self.vu_full, t + 1)
            v.tensor_tensor(self.vu[:, t, :], banks[t % 2][:, :], self.bvu[:, :], ALU.add).then_inc(self.vu_raw, 1)
        for t in range(NT):
            dve.wait_ge(self.e_full, NT)
            if t >= 2:
                dve.wait_ge(self.o_full, t - 1)
            v.tensor_tensor(self.energy[:, t % 2, :, :, :],
                            k.ps_s[:, :].rearrange("p (q t c s) -> p q t c s", q=4, t=NT, c=2)[:, :, t, :, :],
                            self.causal[:, :, :, :].to_broadcast([P, 4, 2, S]), ALU.mult).then_inc(self.e_ready, 1)
            dve.wait_ge(self.o_full, t + 1)
            v.tensor_copy(self.o[:, t, :], banks[t % 2][:, 0:D]).then_inc(self.o_ready, 1)
        dve.wait_ge(self.rooted, 1)
        link(k, dve, v.tensor_scalar(self.ss[:, :], self.ss[:, :], 1e-8, None, ALU.add))
        link(k, dve, v.reciprocal(self.inv[:, :], self.ss[:, :]))
        dve.wait_ge(self.vu_ready, NT)
        for t in range(NT):
            link(k, dve, v.scalar_tensor_tensor(self.o[:, t, :], self.o[:, t, :], self.inv[:, t:t + 1], self.scale[:, :],
                                                ALU.mult, ALU.mult))
            v.tensor_tensor(self.o[:, t, :], self.o[:, t, :], self.vu[:, t, D:2 * D], ALU.mult).then_inc(self.gated, 1)
        finish(k, dve, lambda t: self.bo[:, :], lambda t: k.ps_s[:, t * BANK:t * BANK + D], self.n)


class StageF(Experts):

    HC, LAG, RING, LOADS = 6, 1, 2, 4
    ROUTED = 7
    I = 704

    def __init__(self, k, n):
        self.k, self.n = k, n
        with ExitStack() as st:
            sb = lambda name, shape, dt=F32: k.sb("f_" + name, shape, dt, st)
            self.experts_memory(k, sb, "f_")
            self.wr = sb("wr", [P, FC, 8])
            self.rb = sb("rb", [P, 1, 7])
            self.wg = sb("wg", [P, 2, FC, self.I])
            self.wu = sb("wu", [P, 2, FC, self.I])
            self.wd = sb("wd", [P, 2, 6, D])
            self.sg = sb("sg", [P, 2, T])
            self.su = sb("su", [P, 2, T])
            self.gated = k.sem("f_gated")

    def rows(self, c):
        return P if c < 5 else self.I - 5 * P

    def load(self, sp, e, p):
        a = self.k.a
        for src, dst in (("f_wg", self.wg), ("f_wu", self.wu)):
            at = a[src][e] if isinstance(e, int) else a[src][ds(e, 1)].rearrange("a p f m -> (a p) f m")
            sp.dma_start(dst[:, p, :, :], at).then_inc(self.e_in[p], 16)
        d = a["f_wd"][e] if isinstance(e, int) else a["f_wd"][ds(e, 1)].rearrange("a i d -> (a i) d")
        sp.dma_start(self.wd[:, p, 0:5, :], d[0:5 * P, :].rearrange("(c p) d -> p c d", p=P)).then_inc(self.e_in[p], 16)
        sp.dma_start(self.wd[0:self.rows(5), p, 5, :], d[5 * P:self.I, :]).then_inc(self.e_in[p], 16)

    def sync(self, sp):
        k, a = self.k, self.k.a
        sp.wait_ge(k.x_done, self.n)
        sp.dma_start(self.wr[:, :, 0:7], a["f_wr"]).then_inc(self.router_in, 16)
        sp.dma_start(self.rb[:, 0, :], a["f_rb"].partition_broadcast(P)).then_inc(self.router_in, 16)
        self.sync_experts(k, sp)

    def tensor(self, pe):
        k, nc = self.k, self.k.nc
        norm_tensor(k, pe, self.n)
        wait_norm(k, pe, self.n)
        pe.wait_ge(self.router_in, 32)
        for t in range(NT):
            for f in range(FC):
                last = nc.tensor.matmul(k.ps_m[:, t * 8:t * 8 + 7], k.xnT[:, f, t * P:(t + 1) * P], self.wr[:, f, 0:7],
                                        start=(f == 0), stop=(f == FC - 1))
        last.then_inc(self.logits_full, 1)
        self.spread(k, pe)
        self.tensor_experts(k, pe, False)

    def pe_first(self, k, pe, e, c, r):
        rows = self.rows(c)
        for j, w in enumerate((self.wg, self.wu)):
            for f in range(FC):
                last = k.nc.tensor.matmul(k.ps_s[0:rows, (2 * r + j) * BANK:(2 * r + j + 1) * BANK],
                                          w[:, e, f, c * P:c * P + rows], k.xnT[:, f, :],
                                          start=(f == 0), stop=(f == FC - 1))
        return last

    def second_operands(self, e, c, f, h):
        rows = self.rows(c)
        return self.wd[0:rows, e, c, f * P:(f + 1) * P], self.hid[0:rows, h, :]

    def scalar(self, act):
        k, nc = self.k, self.k.nc
        norm_scalar(k, act, self.n)
        act.wait_ge(self.gapped, self.R + 1)
        nc.scalar.activation(self.second[:, :], self.gap[:, :], ACT.Exp).then_inc(self.second_done, 1)
        self.act_spread(k, act)
        self.scalar_experts(k, act)

    def act_unit(self, k, act, e, c, r):
        rows = self.rows(c)
        return k.nc.scalar.activation(self.sg[0:rows, r, :], k.ps_s[0:rows, 2 * r * BANK:(2 * r + 1) * BANK], ACT.Silu)

    def dve_unit(self, k, dve, e, c, u, n):
        rows, r = self.rows(c), u % 2
        w = self.wide[0:rows, e, :] if isinstance(e, int) else self.wide[0:rows, ds(e, 1), :].rearrange("p a t -> p (a t)")
        k.nc.vector.tensor_tensor(self.su[0:rows, r, :], self.sg[0:rows, r, :],
                                  k.ps_s[0:rows, (2 * r + 1) * BANK:(2 * r + 2) * BANK], ALU.mult).then_inc(self.gated, 1)
        stand(k, dve, self.gated, n + 1)
        return k.nc.vector.tensor_tensor(self.hid[0:rows, u % 4, :], self.su[0:rows, r, :], w, ALU.mult)

    def vector(self, dve):
        k = self.k
        norm_vector(k, dve, self.n)
        dve.wait_ge(self.router_in, 32)
        self.choose(k, dve, self.rb[:, :, :])
        self.vector_experts(k, dve)
        finish(k, dve, None, lambda t: k.ps_s[:, t * BANK:t * BANK + D], self.n)


def finish(k, dve, bias, y, n):
    for t in range(NT):
        if bias is not None:
            link(k, dve, k.nc.vector.tensor_tensor(k.x[:, t, :], k.x[:, t, :], bias(t), ALU.add))
        dve.wait_ge(k.y_full, NT * n + t + 1)
        link(k, dve, k.nc.vector.tensor_tensor(k.x[:, t, :], k.x[:, t, :], y(t), ALU.add))
    dve.nop().then_inc(k.x_done, 1)


def rotary(length):
    import numpy as np
    f = np.float32
    inv_freq = f(1.0) / np.power(f(10000.0), np.arange(0, 16, 2, dtype=f) / f(16))
    angle = np.outer(f(10.0) * (np.arange(length, dtype=f) / f(length)), inv_freq).astype(f)
    cos, sin = np.cos(angle).T, np.sin(angle).T
    rows = np.stack([np.concatenate([cos, cos]), np.concatenate([-sin, sin])], axis=1)
    return np.ascontiguousarray(np.tile(rows, (8, 1, 1)).astype(f))


def head_rows():
    import numpy as np
    return np.where(np.arange(P)[:, None] // 16 == np.arange(8)[None], StageD.SCALE, 0.0).astype(np.float32)


def layouts(inp):
    import numpy as np
    g = {n: np.asarray(v) for n, v in inp.items()}
    chunk = lambda w: np.ascontiguousarray(w.reshape(-1, P, w.shape[-1]).transpose(1, 0, 2))
    o = {"x": g["x"], "ctx_1024": g["ctx_1024"]}
    o["ctxT"] = np.ascontiguousarray(g["ctx_1024"].transpose(0, 2, 1).reshape(B, FC, P, M).transpose(0, 2, 1, 3))
    o["a_wq"] = chunk(g["L0_xattn_Wq"])
    o["a_wkT"] = np.ascontiguousarray(g["L0_xattn_Wk"].T.reshape(8, 64, D).transpose(1, 0, 2))
    o["a_wv"] = chunk(g["L0_xattn_Wv"])
    o["a_wo"] = chunk(g["L0_xattn_Wo"])
    o["a_bo"] = g["L0_xattn_bo"]
    head = lambda w: w.reshape(w.shape[:-1] + (16, 16))
    c = g["L0_attn_ctrl_W"]
    cb = g["L0_attn_ctrl_b"][None]

    def interleave(w):
        q, kk, v, dec, bet, gate = np.split(w, [256, 512, 768, 784, 800], axis=-1)
        return np.concatenate([np.concatenate([head(q), head(kk), head(v), bet[..., None], dec[..., None]], -1)
                               .reshape(len(w), 800), gate], -1)
    o["b_ctl"] = chunk(interleave(c))
    o["b_ctl_b"] = interleave(cb)[0]
    halves = lambda w: np.concatenate([w[..., 0::2], w[..., 1::2]], -1)
    o["b_cin"] = chunk(halves(g["L0_attn_cond_in_W"]))
    dw = halves(g["L0_attn_delta_W"].T).T
    q, kk, v, bet = np.split(dw, [256, 512, 768], axis=-1)
    o["b_delta"] = np.ascontiguousarray(np.concatenate([head(q), head(kk), head(v), bet[..., None]], -1))
    r = g["L0_attn_qkv_ramp_logit"]
    o["b_ramp"] = np.ascontiguousarray(np.concatenate(
        [head(r[0]), head(r[1]), head(r[2]), g["L0_attn_beta_ramp_logit"][:, None]], -1))
    o["b_theta"] = g["L0_attn_rot_theta"][:, None]
    o["b_norm_w"] = np.ascontiguousarray(g["L0_attn_cond_norm_w"].reshape(64, 2))
    cw = np.stack([g["L0_attn_q_conv_w"], g["L0_attn_k_conv_w"], g["L0_attn_v_conv_w"]])
    cw = cw.reshape(3, 16, 16, 4).transpose(1, 3, 0, 2).reshape(16, 4, 48)
    o["b_conv_w"] = np.ascontiguousarray(np.concatenate([cw] * B))
    o["b_o_w"] = g["L0_attn_out_norm_w"]
    o["b_wo"] = chunk(g["L0_attn_out_proj_W"].T)
    o["b_bo"] = g["L0_attn_out_proj_b"]
    o["c_rw1"] = chunk(g["L0_ffn_rw1"])
    o["c_rb1"] = np.ascontiguousarray(g["L0_ffn_rb1"].reshape(FC, P).T)
    o["c_rw2"] = chunk(g["L0_ffn_rw2"])
    o["c_rb2"] = g["L0_ffn_rb2"]
    o["c_b1"] = np.ascontiguousarray(g["L0_ffn_eb1"].reshape(8, 4, P).transpose(2, 0, 1))
    o["c_b2"] = g["L0_ffn_eb2"]
    o["c_w1"] = np.ascontiguousarray(g["L0_ffn_ew1"].reshape(8, FC, P, 512).transpose(0, 2, 1, 3))
    o["c_w2"] = np.ascontiguousarray(g["L0_ffn_ew2"].reshape(8, 4, P, D).transpose(0, 2, 1, 3))
    o["f_wr"] = chunk(g["L1_ffn_wr"].T)
    o["f_rb"] = g["L1_ffn_rb"]
    for n, m in (("g", "g"), ("u", "u")):
        w = np.concatenate([g["L1_ffn_r" + m], g["L1_ffn_s" + m][None]])
        o["f_w" + n] = np.ascontiguousarray(w.transpose(0, 2, 1).reshape(8, FC, P, 704).transpose(0, 2, 1, 3))
    w = np.concatenate([g["L1_ffn_rd"], g["L1_ffn_sd"][None]])
    o["f_wd"] = np.ascontiguousarray(w.transpose(0, 2, 1))
    wt = lambda n: chunk(g[n].T)
    col = lambda v: np.ascontiguousarray(v.reshape(-1, P).T)
    o["d_wq"], o["d_wk"], o["d_wv"] = wt("L1_xattn_Wq"), wt("L1_xattn_Wk"), wt("L1_xattn_Wv")
    o["d_bq"], o["d_bk"] = col(g["L1_xattn_bq"]), col(g["L1_xattn_bk"])
    pair = lambda w: w.reshape((8, 2, 16) + w.shape[1:])
    o["d_wo"] = np.ascontiguousarray(pair(g["L1_xattn_Wo"].T).transpose(0, 2, 1, 3).reshape(P, 2, D))
    o["d_bv"] = np.ascontiguousarray(pair(g["L1_xattn_bv"]).transpose(0, 2, 1).reshape(P, 2))
    o["d_bo"] = g["L1_xattn_bo"]
    o["d_fold"] = np.tile(np.eye(32, dtype=np.float32), (4, 1))
    o["d_q_rot"], o["d_k_rot"], o["d_head_of"] = rotary(S), rotary(M), head_rows()
    e = lambda n, m: chunk(np.concatenate([g["L1_attn_" + n], g["L1_attn_" + m]]).T)
    o["e_wqk"], o["e_wvu"], o["e_wo"] = e("Wq", "Wk"), e("Wv", "Wu"), wt("L1_attn_Wo")
    o["e_bqk"] = col(np.concatenate([g["L1_attn_bq"], g["L1_attn_bk"]]))
    o["e_bvu"] = np.concatenate([g["L1_attn_bv"], g["L1_attn_bu"]])
    o["e_scale"], o["e_bo"] = g["L1_attn_scale"], g["L1_attn_bo"]
    o["e_causal"] = np.ascontiguousarray(np.tile(np.triu(np.ones((S, S), np.float32)), (2, 1)).reshape(P, 1, 1, S))
    return o


def kernel(**inputs):
    import numpy as np
    import concourse.bacc as bacc
    from concourse.bass_utils import run_bass_kernel_spmd as run

    nc = bacc.Bacc("TRN2", target_bir_lowering=False, num_devices=1)
    arrays = {n + "_dram": np.ascontiguousarray(v) for n, v in layouts(inputs).items()}
    aps = {n[:-5]: nc.dram_tensor(n, v.shape, mybir.dt.from_np(v.dtype), kind="ExternalInput").ap()
           for n, v in arrays.items()}
    out = nc.dram_tensor("out_dram", (B, S, D), F32, kind="ExternalOutput").ap()
    build(nc, aps, out)
    r = run(nc, [arrays], core_ids=[0])
    return r.results[0]["out_dram"]
```

```python
from contextlib import ExitStack

import concourse.bass as bass
from concourse import mybir

F32 = mybir.dt.float32
F32R = mybir.dt.float32r
U32 = mybir.dt.uint32
ALU = mybir.AluOpType
ACT = mybir.ActivationFunctionType
AX = mybir.AxisListType
ds = bass.ds

P = 128
B = 8
S = 64
D = 256
T = B * S
NT = T // P
FC = D // P
M = 1601
MP = M + M % 2
MC = -(-M // P)
ML = M - (MC - 1) * P
BANK = 512
KB = [(k, min(BANK, M - k)) for k in range(0, M, BANK)]
QUADS = [list(range(q, min(q + 4, MC))) for q in range(0, MC, 4)]
EPS_LN = 1e-5


class Count:

    def __init__(self, sem):
        self.sem, self.base, self.k = sem, 0, 0

    def restart(self, base):
        self.base, self.k = base, 0

    def up(self, instruction):
        instruction.then_inc(self.sem, 1)
        self.k += 1

    def now(self, back=0):
        return self.base + (self.k - back)


def keys(c):
    return P if c < MC - 1 else ML


class Kit:
    pass


def build(nc, a, out):
    k = Kit()
    k.nc, k.a, k.out = nc, a, out
    with ExitStack() as ctx:
        k.sem = lambda name: ctx.enter_context(nc.semaphore(name))
        k.sb = lambda name, shape, dt=F32, where=ctx: where.enter_context(nc.sbuf_tensor(name, shape, dt))
        k.ps_s = ctx.enter_context(nc.psum_tensor("ps_s", [P, 4 * BANK], F32))
        k.ps_t = ctx.enter_context(nc.psum_tensor("ps_t", [P, 2, BANK], F32))
        k.ps_o = ctx.enter_context(nc.psum_tensor("ps_o", [P, BANK], F32))
        k.ps_m = ctx.enter_context(nc.psum_tensor("ps_m", [P, BANK], F32))
        k.x = k.sb("x", [P, NT, D])
        k.xn = k.sb("xn", [P, NT, D])
        k.xnT = k.sb("xnT", [P, FC, T])
        k.ident = k.sb("ident", [P, P])
        k.stats = k.sb("stats", [P, NT, 6])
        k.mean_var = k.sb("mean_var", [P, NT, 2])
        k.var_eps = k.sb("var_eps", [P, NT])
        k.rstd = k.sb("rstd", [P, NT])
        k.minus_half = k.sb("minus_half", [P, 2 * NT])
        k.x_in = k.sem("x_in")
        k.out_sent = k.sem("out_sent")
        k.consts = k.sem("consts")
        k.dve_order = k.sem("dve_order")
        k.ln_var = k.sem("ln_var")
        k.ln_rstd = k.sem("ln_rstd")
        k.ln_xn = k.sem("ln_xn")
        k.ln_turned = k.sem("ln_turned")
        k.ln_xT_act = k.sem("ln_xT_act")
        k.ln_xT_dve = k.sem("ln_xT_dve")
        k.passed = k.sem("passed")
        k.y_full = k.sem("y_full")
        k.x_done = k.sem("x_done")
        k.order = Count(k.dve_order)

        k.shared, k.rounds, k.units = {}, 0, 0
        parts = [StageA, StageB, StageC, StageD, StageE, StageF]
        parts = [p(k, n) for n, p in enumerate(parts)]
        block = ctx.enter_context(nc.Block())

        @block.sync
        def _(sp):
            sp.dma_start(k.x[:, :, :], a["x"].rearrange("(t b) s d -> (b s) t d", t=NT)).then_inc(k.x_in, 16)
            for p in parts:
                p.sync(sp)
            sp.wait_ge(k.x_done, len(parts))
            sp.dma_start(out.rearrange("(t b) s d -> (b s) t d", t=NT), k.x[:, :, :]).then_inc(k.out_sent, 16)
            sp.wait_ge(k.out_sent, 16)

        @block.gpsimd
        def _(pool):
            nc.gpsimd.memset(k.ident[:, :], 0.0).then_inc(k.consts, 1)
            nc.gpsimd.memset(k.minus_half[:, :], -0.5).then_inc(k.consts, 1)
            pool.wait_ge(k.consts, 2)
            nc.gpsimd.affine_select(out=k.ident[:, :], in_=k.ident[:, :], compare_op=ALU.not_equal, fill=1.0,
                                    base=0, pattern=[[-1, P]], channel_multiplier=1).then_inc(k.consts, 1)
            for p in parts:
                p.gpsimd(pool)

        @block.scalar
        def _(act):
            for p in parts:
                p.scalar(act)

        @block.vector
        def _(dve):
            dve.wait_ge(k.x_in, 16)
            for p in parts:
                p.vector(dve)

        @block.tensor
        def _(pe):
            pe.wait_ge(k.consts, 3)
            for p in parts:
                p.tensor(pe)


def link(k, dve, instruction):
    k.order.up(instruction)
    dve.wait_ge(k.dve_order, k.order.now())


def stand(k, eng, sem, value):
    eng.wait_ge(sem, value)
    if not isinstance(value, int):
        eng.nop().then_inc(k.passed, 1)


def norm_vector(k, dve, n):
    nc = k.nc
    for t in range(NT):
        last = nc.vector.bn_stats(k.stats[:, t, :], k.x[:, t, :])
    link(k, dve, last)
    for t in range(NT):
        last = nc.vector.bn_aggr(k.mean_var[:, t, :], k.stats[:, t, :])
    link(k, dve, last)
    nc.vector.tensor_scalar(k.var_eps[:, :], k.mean_var[:, :, 1], EPS_LN, None, ALU.add).then_inc(k.ln_var, 1)
    dve.wait_ge(k.ln_rstd, n + 1)
    for t in range(NT):
        nc.vector.tensor_scalar(k.xn[:, t, :], k.x[:, t, :], k.mean_var[:, t, 0:1], k.rstd[:, t:t + 1],
                                ALU.subtract, ALU.mult).then_inc(k.ln_xn, 1)
    dve.wait_ge(k.ln_turned, 2 * n + 2)
    nc.vector.tensor_copy(k.xnT[:, 1, :], k.ps_t[:, 1, :]).then_inc(k.ln_xT_dve, 1)


def norm_pool(k, pool, n):
    pool.wait_ge(k.ln_var, n + 1)
    k.nc.gpsimd.tensor_tensor(k.rstd[:, :], k.var_eps[:, :], k.minus_half[:, 0:NT], ALU.pow).then_inc(k.ln_rstd, 1)


def norm_tensor(k, pe, n):
    for f in range(FC):
        for t in range(NT):
            if f == 0:
                pe.wait_ge(k.ln_xn, NT * n + t + 1)
            last = k.nc.tensor.transpose(k.ps_t[:, f, t * P:(t + 1) * P], k.xn[:, t, f * P:(f + 1) * P], k.ident[:, :])
        last.then_inc(k.ln_turned, 1)


def norm_scalar(k, act, n):
    act.wait_ge(k.ln_turned, 2 * n + 1)
    k.nc.scalar.activation(k.xnT[:, 0, :], k.ps_t[:, 0, :], ACT.Copy).then_inc(k.ln_xT_act, 1)


def wait_norm(k, eng, n):
    eng.wait_ge(k.ln_xT_act, n + 1)
    eng.wait_ge(k.ln_xT_dve, n + 1)


class Attention:

    G = None
    WIDTH = None
    FOLDED = False

    def attention_memory(self, k, st):
        name = self.name
        self.p = k.sb(name + "p", [P, M], F32, st)
        self.pT = k.sb(name + "pT", [P, MC, P], F32, st)
        self.neg_max = k.sb(name + "neg_max", [P, 2], F32, st)
        self.sums = k.sb(name + "sums", [P, 2], F32, st)
        self.inv = k.sb(name + "inv", [P, 2], F32, st)
        sem = k.sem
        self.scored = sem(name + "scored")
        self.maxed = sem(name + "maxed")
        self.exped = sem(name + "exped")
        self.turned = sem(name + "turned")
        self.moved_dve = sem(name + "moved_dve")
        self.moved_act = sem(name + "moved_act")
        self.valued = sem(name + "valued")
        self.inverted = sem(name + "inverted")
        self.scaled = sem(name + "scaled")
        self.misc_full = sem(name + "misc_full")
        self.misc_read = sem(name + "misc_read")

    def bodies(self, eng, body):
        body(0, True, False)
        with eng.Fori(1, B // 2 - 1) as i:
            body(i, False, False)
        body(B // 2 - 1, False, True)

    def dve_extra(self, k, dve, i, s, first, last):
        pass

    def act_extra(self, k, act, i, s, first, last):
        pass

    def pe_turn(self, k, pe, n, s, q):
        if q >= 2:
            pe.wait_ge(self.moved_act if q % 2 else self.moved_dve, 2 * n + 1)
        elif not (isinstance(n, int) and n == 0):
            pe.wait_ge(self.moved_act if q % 2 else self.moved_dve, 2 * n)
        for j, c in enumerate(QUADS[q]):
            last = k.nc.tensor.transpose(k.ps_t[0:keys(c), q % 2, j * P:(j + 1) * P],
                                         self.p[:, c * P:c * P + keys(c)], k.ident[:, :])
        last.then_inc(self.turned, 1)

    def pe_value(self, k, pe, n, s, q):
        pe.wait_ge(self.moved_act if q % 2 else self.moved_dve, 2 * n + 1 + q // 2)
        for c in QUADS[q]:
            last = k.nc.tensor.matmul(k.ps_o[:, 0:self.WIDTH], self.pT[0:keys(c), c, :],
                                      self.values(s, c), start=(c == 0), stop=(c == MC - 1))
        return last

    def tensor_loop(self, k, pe):
        G = self.G
        misc = Count(self.misc_full)

        def fill(*what):
            if not (isinstance(misc.base, int) and misc.now() == 0):
                stand(k, pe, self.misc_read, misc.now())
            misc.up(self.pe_misc(k, pe, *what))

        self.pe_before(k, pe, fill)
        pre = misc.k
        self.pe_scores(k, pe, 0, 0, KB).then_inc(self.scored, 1)

        def body(i, first, last):
            if not first:
                misc.restart(self.first_fills + self.fills * (i - 1))
            for s in range(2 * G):
                n = 2 * G * i + s
                end = last and s == 2 * G - 1
                pe.wait_ge(self.exped, n + 1)
                self.pe_turn(k, pe, n, s, 0)
                self.pe_turn(k, pe, n, s, 1)
                if self.FOLDED and not (first and s == 0):
                    self.pe_fold(k, pe, n - 1)
                if not end:
                    s1 = (s + 1) % (2 * G)
                    i1 = i if s1 else i + 1
                    self.pe_ready(k, pe, i1, s1, misc)
                    self.pe_scores(k, pe, i1, s1, KB[0:2])
                self.pe_turn(k, pe, n, s, 2)
                self.pe_turn(k, pe, n, s, 3)
                if not end:
                    self.pe_scores(k, pe, i1, s1, KB[2:]).then_inc(self.scored, 1)
                for what in self.fills_before(s, first, last):
                    fill(i, *what)
                if not (first and s == 0):
                    pe.wait_ge(self.scaled, n)
                for q in range(3):
                    self.pe_value(k, pe, n, s, q)
                self.pe_value(k, pe, n, s, 3).then_inc(self.parted if self.FOLDED else self.valued, 1)
                for what in self.fills_after(s, first, last):
                    fill(i, *what)
            if first:
                assert misc.k == self.first_fills, misc.k
            elif not last:
                assert misc.k == self.fills, misc.k

        self.bodies(pe, body)
        misc.restart(self.first_fills + self.fills * (B // 2 - 2) + misc.k)
        self.pe_after(k, pe, fill, misc)

    def vector_loop(self, k, dve):
        G = self.G

        def maximum(n, s):
            dve.wait_ge(self.scored, n + 1)
            k.nc.vector.tensor_reduce(self.neg_max[:, s % 2:s % 2 + 1], k.ps_s[:, 0:M], AX.X, ALU.max,
                                      negate=True).then_inc(self.maxed, 1)

        def move(n, q):
            dve.wait_ge(self.turned, 4 * n + q + 1)
            w, c = len(QUADS[q]), QUADS[q][0]
            k.nc.vector.tensor_copy(self.pT[:, c:c + w, :], k.ps_t[:, q % 2, 0:w * P]
                                    .rearrange("p (c r) -> p c r", r=P)).then_inc(self.moved_dve, 1)

        def scale_folded(n, s):
            dve.wait_ge(self.inverted, n + 1)
            dve.wait_ge(self.valued, n + 1)
            self.dve_scale(k, dve, s % (2 * G)).then_inc(self.scaled, 1)

        maximum(0, 0)

        def body(i, first, last):
            for s in range(2 * G):
                n = 2 * G * i + s
                move(n, 0)
                if self.FOLDED and not (first and s == 0):
                    scale_folded(n - 1, s - 1)
                move(n, 2)
                if not (last and s == 2 * G - 1):
                    maximum(n + 1, s + 1)
                dve.wait_ge(self.exped, n + 1)
                k.nc.vector.reciprocal(self.inv[:, s % 2:s % 2 + 1], self.sums[:, s % 2:s % 2 + 1])\
                    .then_inc(self.inverted, 1)
                if self.FOLDED:
                    dve.wait_ge(self.parted, n + 1)
                    self.dve_unfold(k, dve)
                    if last and s == 2 * G - 1:
                        scale_folded(n, s)
                else:
                    dve.wait_ge(self.inverted, n + 1)
                    dve.wait_ge(self.valued, n + 1)
                    self.dve_scale(k, dve, s).then_inc(self.scaled, 1)
                self.dve_extra(k, dve, i, s, first, last)

        self.bodies(dve, body)

    def scalar_loop(self, k, act):
        G = self.G
        misc = Count(self.misc_read)

        def read(*what):
            act.wait_ge(self.misc_full, misc.now() + 1)
            misc.up(self.act_misc(k, act, *what))

        def exponential(n, s):
            act.wait_ge(self.maxed, n + 1)
            k.nc.scalar.activation(self.p[:, :], k.ps_s[:, 0:M], ACT.Exp, bias=self.neg_max[:, s % 2:s % 2 + 1],
                                   accum_out=self.sums[:, s % 2:s % 2 + 1]).then_inc(self.exped, 1)

        def move(n, q):
            act.wait_ge(self.turned, 4 * n + q + 1)
            w, c = len(QUADS[q]), QUADS[q][0]
            r = keys(c)
            k.nc.scalar.activation(self.pT[0:r, c:c + w, :], k.ps_t[0:r, q % 2, 0:w * P]
                                   .rearrange("p (c r) -> p c r", r=P), ACT.Copy).then_inc(self.moved_act, 1)

        self.act_before(k, act, read)
        exponential(0, 0)

        def body(i, first, last):
            if not first:
                misc.restart(self.first_fills + self.fills * (i - 1))
            for s in range(2 * G):
                n = 2 * G * i + s
                move(n, 1)
                move(n, 3)
                for what in self.fills_before(s, first, last):
                    read(i, *what)
                if not (last and s == 2 * G - 1):
                    exponential(n + 1, s + 1)
                self.act_extra(k, act, i, s, first, last)
                for what in self.fills_after(s, first, last):
                    read(i, *what)

        self.bodies(act, body)
        misc.restart(self.first_fills + self.fills * (B // 2 - 2) + misc.k)
        self.act_after(k, act, read)


class StageA(Attention):

    name = "a_"
    H, DH = 8, 64
    G = 4
    WIDTH = D

    def __init__(self, k, n):
        self.n, self.k = n, k
        sem = k.sem
        with ExitStack() as st:
            sb = lambda name, shape, dt=F32: k.sb("a_" + name, shape, dt, st)
            self.wq = sb("wq", [P, FC, 512])
            self.wkT = sb("wkT", [P, 8, D])
            self.wv = sb("wv", [P, FC, 512])
            self.wo = sb("wo", [P, 4, D])
            self.bo = sb("bo", [P, D])
            self.qT = sb("qT", [P, 8, T])
            self.ctx = sb("ctx", [P, 2, MC, D])
            self.ctxT = sb("ctxT", [P, FC, MP])
            self.ctxT_hi = sb("ctxT_hi", [P, 2, FC, MP], F32R)
            self.ctxT_lo = sb("ctxT_lo", [P, 2, FC, MP], F32R)
            self.qk = sb("qk", [P, FC, 8 * S])
            self.qk_hi = sb("qk_hi", [P, 2, FC, 8 * S], F32R)
            self.qk_lo = sb("qk_lo", [P, 2, FC, 8 * S], F32R)
            self.mixed = sb("mixed", [P, 2, D])
            self.mixedT = sb("mixedT", [P, 2, FC, 8 * S])
            self.oT = sb("oT", [P, 4, T])
            self.attention_memory(k, st)
            self.w_in = sem("a_w_in")
            self.late_in = sem("a_late_in")
            self.ctx_in = [sem("a_ctx_in0"), sem("a_ctx_in1")]
            self.ctxT_in = sem("a_ctxT_in")
            self.padded = sem("a_padded")
            self.ctxT_high = sem("a_ctxT_high")
            self.ctxT_low = sem("a_ctxT_low")
            self.qk_high = sem("a_qk_high")
            self.qk_low = sem("a_qk_low")
            self.q_full = sem("a_q_full")
            self.q_read = sem("a_q_read")
        self.first_fills = 2 + 8 - 1 + 1 + 4
        self.fills = 8 + 2 + 4

    def pe_ready(self, k, pe, i, s1, misc):
        if s1 % 4 == 0:
            b = 2 * i + s1 // 4
            stand(k, pe, self.qk_low, FC * b + FC)
            stand(k, pe, self.ctxT_low, FC * b + FC)

    def fills_before(self, s, first, last):
        return [] if first and s == 0 else [("turn", (s - 1) % 8)]

    def fills_after(self, s, first, last):
        g = s % 4
        out = []
        if g == 0 and not (first and s == 0):
            out.append(("out", (s - 1) % 8 // 4))
        if g < FC and not (last and s >= 4):
            out.append(("qk", 1 - s // 4, g, 1 + s // 4))
        return out

    def values(self, s, c):
        return self.ctx[0:keys(c), s // 4, c, :]

    def sync(self, sp):
        k, a = self.k, self.k.a
        sp.dma_start(self.wq[:, :, :], a["a_wq"]).then_inc(self.w_in, 16)
        sp.dma_start(self.wkT[:, :, :], a["a_wkT"]).then_inc(self.w_in, 16)

        def load(b, p):
            at = b if isinstance(b, int) else ds(b, 1)
            tT, t = a["ctxT"], a["ctx_1024"]
            srcT = tT[b] if isinstance(b, int) else tT[ds(b, 1)].rearrange("a p f m -> (a p) f m")
            src = t[b] if isinstance(b, int) else t[ds(b, 1)].rearrange("a m d -> (a m) d")
            if not (isinstance(b, int) and b == 0):
                sp.wait_ge(self.ctxT_low, FC * b)
            sp.dma_start(self.ctxT[:, :, 0:M], srcT).then_inc(self.ctxT_in, 16)
            if not (isinstance(b, int) and b < 2):
                sp.wait_ge(self.valued, 4 * (b - 2) + 4)
            sp.dma_start(self.ctx[:, p, 0:MC - 1, :],
                         src[0:(MC - 1) * P, :].rearrange("(c p) d -> p c d", p=P)).then_inc(self.ctx_in[p], 16)
            sp.dma_start(self.ctx[0:ML, p, MC - 1, :], src[(MC - 1) * P:M, :]).then_inc(self.ctx_in[p], 16)

        load(0, 0)
        load(1, 1)
        sp.dma_start(self.wv[:, :, :], a["a_wv"]).then_inc(self.late_in, 16)
        sp.dma_start(self.wo[:, :, :], a["a_wo"]).then_inc(self.late_in, 16)
        sp.dma_start(self.bo[:, :], a["a_bo"].partition_broadcast(P)).then_inc(self.late_in, 16)
        with sp.Fori(1, B // 2) as i:
            load(2 * i, 0)
            load(2 * i + 1, 1)

    def split_ctxT(self, k, pool, b, p):
        for f in range(FC):
            stand(k, pool, self.ctxT_high, FC * b + (f + 1))
            k.nc.gpsimd.tensor_tensor(self.ctxT_lo[:, p, f, :], self.ctxT[:, f, :], self.ctxT_hi[:, p, f, :].bitcast(F32),
                                      ALU.subtract).then_inc(self.ctxT_low, 1)

    def split_qk(self, k, pool, b, p, f, read):
        stand(k, pool, self.misc_read, read)
        k.nc.gpsimd.tensor_copy(self.qk_hi[:, p, f, :], self.qk[:, f, :]).then_inc(self.qk_high, 1)
        stand(k, pool, self.qk_high, FC * b + (f + 1))
        k.nc.gpsimd.tensor_tensor(self.qk_lo[:, p, f, :], self.qk[:, f, :], self.qk_hi[:, p, f, :].bitcast(F32),
                                  ALU.subtract).then_inc(self.qk_low, 1)

    def act_extra(self, k, act, i, s, first, last):
        f = s % 4
        if f < FC and not (last and s >= 4):
            self.high_ctxT(k, act, 2 * i + 1 + s // 4, 1 - s // 4, f)

    def high_ctxT(self, k, act, b, p, f):
        if f == 0:
            stand(k, act, self.ctxT_in, 16 * b + 16)
        k.nc.scalar.activation(self.ctxT_hi[:, p, f, :], self.ctxT[:, f, :], ACT.Copy).then_inc(self.ctxT_high, 1)

    def gpsimd(self, pool):
        k = self.k
        norm_pool(k, pool, self.n)
        k.nc.gpsimd.memset(self.ctxT[:, :, M:MP], 0.0).then_inc(self.padded, 1)
        pool.wait_ge(self.padded, 1)
        k.nc.gpsimd.memset(self.qT[64:P, :, :], 0.0).then_inc(self.padded, 1)
        self.split_ctxT(k, pool, 0, 0)
        for f in range(FC):
            self.split_qk(k, pool, 0, 0, f, f + 1)

        def body(i, first, last):
            reads = FC if first else self.first_fills + self.fills * (i - 1)
            seen = 0
            for s in range(8):
                for what in self.fills_before(s, first, last) + self.fills_after(s, first, last):
                    seen += 1
                    if what[0] == "qk":
                        _, p, f, ahead = what
                        self.split_qk(k, pool, 2 * i + ahead, p, f, reads + seen)
                if s % 4 == 1 and not (last and s >= 4):
                    self.split_ctxT(k, pool, 2 * i + 1 + s // 4, 1 - s // 4)

        self.bodies(pool, body)

    def tensor(self, pe):
        norm_tensor(self.k, pe, self.n)
        self.tensor_loop(self.k, pe)

    def pe_before(self, k, pe, fill):
        nc = k.nc
        wait_norm(k, pe, self.n)
        pe.wait_ge(self.w_in, 32)
        for m in range(4):
            for f in range(FC):
                last = nc.tensor.matmul(k.ps_s[:, m * BANK:(m + 1) * BANK], self.wq[:, f, m * P:(m + 1) * P],
                                        k.xnT[:, f, :], start=(f == 0), stop=(f == FC - 1))
            last.then_inc(self.q_full, 1)
        pe.wait_ge(self.q_read, 8)
        fill(0, "qk", 0, 0, 0)
        fill(0, "qk", 0, 1, 0)
        pe.wait_ge(self.qk_low, FC)
        pe.wait_ge(self.ctxT_low, FC)

    def pe_scores(self, k, pe, i, s, blocks):
        p, g = s // 4, s % 4
        rows = slice(g * P, (g + 1) * P)
        for c, w in blocks:
            w += w % 2
            for f in range(FC):
                for q, ctx in ((self.qk_hi, self.ctxT_hi), (self.qk_hi, self.ctxT_lo), (self.qk_lo, self.ctxT_hi)):
                    last = k.nc.tensor.matmul(k.ps_s[:, c:c + w], q[:, p, f, rows], ctx[:, p, f, c:c + w],
                                              start=(f == 0 and ctx is self.ctxT_hi and q is self.qk_hi),
                                              stop=(f == FC - 1 and q is self.qk_lo))
        return last

    def pe_value(self, k, pe, n, s, q):
        if s % 4 == 0 and q == 0:
            pe.wait_ge(self.ctx_in[s // 4], 32 * (self.pe_i + 1))
        return Attention.pe_value(self, k, pe, n, s, q)

    def pe_misc(self, k, pe, i, kind, *which):
        nc = k.nc
        if kind == "turn":
            s = which[0]
            n = 8 * i + s if s < 7 else 8 * i - 1
            pe.wait_ge(self.scaled, n + 1)
            for f in range(FC):
                last = nc.tensor.transpose(k.ps_m[:, f * P:(f + 1) * P], self.mixed[:, s % 2, f * P:(f + 1) * P],
                                           k.ident[:, :])
        elif kind == "out":
            p = which[0]
            if isinstance(i, int) and i == 0:
                pe.wait_ge(self.late_in, 48)
            for h in range(8):
                for f in range(FC):
                    last = nc.tensor.matmul(k.ps_m[64 * (h % 2):64 * (h % 2) + 64, h // 2 * S:(h // 2 + 1) * S],
                                            self.wv[:, f, h * 64:(h + 1) * 64],
                                            self.mixedT[:, p, f, h * S:(h + 1) * S],
                                            start=(f == 0), stop=(f == FC - 1))
        else:
            p, f, ahead = which
            b = 2 * i + ahead
            for h in range(8):
                rhs = self.qT[:, h, b * S:(b + 1) * S] if isinstance(b, int) else self.qT[:, h, ds(b * S, S)]
                last = nc.tensor.matmul(k.ps_m[:, h * S:(h + 1) * S], self.wkT[:, h, f * P:(f + 1) * P], rhs,
                                        start=True, stop=True)
        return last

    def bodies(self, eng, body):
        def noted(i, first, last):
            self.pe_i = i
            body(i, first, last)
        Attention.bodies(self, eng, noted)

    def pe_after(self, k, pe, fill, misc):
        nc = k.nc
        misc_last = B // 2
        fill(misc_last, "turn", 7)
        fill(misc_last, "out", 1)
        pe.wait_ge(self.misc_read, misc.now())
        pe.wait_ge(self.late_in, 48)
        for t in range(NT):
            for c in range(4):
                last = nc.tensor.matmul(k.ps_s[:, t * BANK:t * BANK + D], self.oT[:, c, t * P:(t + 1) * P],
                                        self.wo[:, c, :], start=(c == 0), stop=(c == 3))
            last.then_inc(k.y_full, 1)

    def scalar(self, act):
        norm_scalar(self.k, act, self.n)
        self.scalar_loop(self.k, act)

    def act_before(self, k, act, read):
        act.wait_ge(self.padded, 2)
        for f in range(FC):
            self.high_ctxT(k, act, 0, 0, f)
        for h in range(8):
            act.wait_ge(self.q_full, h // 2 + 1)
            odd = 64 * (h % 2)
            k.nc.scalar.activation(self.qT[0:64, h, :], k.ps_s[odd:odd + 64, h // 2 * BANK:(h // 2 + 1) * BANK],
                                   ACT.Copy).then_inc(self.q_read, 1)
        read(0, "qk", 0, 0, 0)
        read(0, "qk", 0, 1, 0)

    def act_misc(self, k, act, i, kind, *which):
        nc = k.nc
        if kind == "turn":
            s = which[0]
            return nc.scalar.activation(self.mixedT[:, s // 4, :, s % 4 * P:(s % 4 + 1) * P],
                                        k.ps_m[:, 0:FC * P].rearrange("p (f r) -> p f r", r=P), ACT.Copy)
        if kind == "out":
            b = 2 * i + which[0] if which[0] == 0 else 2 * i - 1
            at = slice(b * S, (b + 1) * S) if isinstance(b, int) else ds(b * S, S)
            return nc.scalar.activation(self.oT[:, :, at], k.ps_m[:, 0:4 * S].rearrange("p (c s) -> p c s", s=S), ACT.Copy)
        p, f, _ = which
        return nc.scalar.activation(self.qk[:, f, :], k.ps_m[:, :], ACT.Copy, scale=self.DH ** -0.5)

    def act_after(self, k, act, read):
        read(B // 2, "turn", 7)
        read(B // 2, "out", 1)

    def dve_scale(self, k, dve, s):
        return k.nc.vector.tensor_scalar(self.mixed[:, s % 2, :], k.ps_o[:, 0:D], self.inv[:, s % 2:s % 2 + 1], None,
                                         ALU.mult)

    def vector(self, dve):
        k = self.k
        norm_vector(k, dve, self.n)
        self.vector_loop(k, dve)
        dve.wait_ge(self.late_in, 48)
        finish(k, dve, lambda t: self.bo[:, :], lambda t: k.ps_s[:, t * BANK:t * BANK + D], self.n)


class StageB:

    H, DH = 16, 16
    RUN = 50
    W = H * RUN + D
    RING = 8

    def __init__(self, k, n):
        self.k, self.n = k, n
        sem = k.sem
        with ExitStack() as st:
            sb = lambda name, shape, dt=F32: k.sb("b_" + name, shape, dt, st)
            self.cin = sb("cin", [P, FC, P])
            self.ctl = sb("ctl", [P, FC, self.W])
            self.ctl_b = sb("ctl_b", [P, self.W])
            self.delta = sb("delta", [P, 16, self.RUN])
            self.ramp = sb("ramp", [P, 16, self.RUN - 1])
            self.theta = sb("theta", [64, 1])
            self.turn_work = sb("turn_work", [64, 8])
            self.cos_sin = sb("cos_sin", [64, 6, 3])
            self.norm_w = sb("norm_w", [64, 2])
            self.state = sb("state", [64, 2, 2, T])
            self.part = sb("part", [64, 2, T])
            self.rms = sb("rms", [P, NT])
            self.rms_inv = sb("rms_inv", [P, NT])
            self.ones = sb("ones", [64, 1])
            self.spread = sb("spread", [64, T])
            self.condT = sb("condT", [P, T])
            self.mix = sb("mix", [P, NT, self.W])
            self.rows = sb("rows", [P, 3 + S, self.RUN])
            self.conv_w = sb("conv_w", [P, 4, 48])
            self.conv = sb("conv", [P, S, 48])
            self.prod = sb("prod", [P, S, 48])
            self.act = sb("act", [P, S, 48])
            self.gates = sb("gates", [P, S, 2])
            self.neg_gb = sb("neg_gb", [P, S])
            self.ssq = sb("ssq", [P, 2, S])
            self.ssq_inv = sb("ssq_inv", [P, 2, S])
            self.kv = sb("kv", [P, S, 2, 16])
            self.qn = sb("qn", [P, S, 16])
            self.hist = sb("hist", [P, self.RING, 16, 16])
            self.tmp = sb("tmp", [P, 16, 16])
            self.outer = sb("outer", [P, 16, 16])
            self.past = sb("past", [P, 16])
            self.begun = sb("begun", [P, 16])
            self.coef = sb("coef", [P, S, 2])
            self.u = sb("u", [P, 16])
            self.qs = sb("qs", [P, self.RING, 16, 16])
            self.o = sb("o", [P, S, 16])
            self.o_sq = sb("o_sq", [P, S, 16])
            self.o_w = sb("o_w", [P, 16])
            self.o_dims = sb("o_dims", [P, 16, S])
            self.o_tok = sb("o_tok", [P, NT, D])
            self.gate = sb("gate", [P, NT, D])
            self.oT = sb("oT", [P, FC, T])
            self.wo = sb("wo", [P, FC, D])
            self.bo = sb("bo", [P, D])
        self.mix_dram = k.nc.dram_tensor("b_mix_dram", (T, 800), F32, kind="Internal").ap()
        self.w_in = sem("b_w_in")
        self.small_in = sem("b_small_in")
        self.cleared = sem("b_cleared")
        self.ramped = sem("b_ramped")
        self.delta_ready = sem("b_delta_ready")
        self.angle = sem("b_angle")
        self.sines = sem("b_sines")
        self.cosines = sem("b_cosines")
        self.p_full = sem("b_p_full")
        self.p_read = sem("b_p_read")
        self.squared = sem("b_squared")
        self.ms_full = sem("b_ms_full")
        self.ms_eps = sem("b_ms_eps")
        self.ms_inv = sem("b_ms_inv")
        self.spread_full = sem("b_spread_full")
        self.cond = sem("b_cond")
        self.mix_full = sem("b_mix_full")
        self.mix_ready = sem("b_mix_ready")
        self.mix_sent = sem("b_mix_sent")
        self.rows_in = sem("b_rows_in")
        self.q_prod = sem("b_q_prod")
        self.conved = sem("b_conved")
        self.silued = sem("b_silued")
        self.gated = sem("b_gated")
        self.squares = sem("b_squares")
        self.rooted = sem("b_rooted")
        self.ones_set = sem("b_ones_set")
        self.roots = sem("b_roots")
        self.ready = sem("b_ready")
        self.state_done = sem("b_state_done")
        self.qs_done = sem("b_qs_done")
        self.qs_read = sem("b_qs_read")
        self.step = sem("b_step")
        self.o_ready = sem("b_o_ready")
        self.o_ms = sem("b_o_ms")
        self.o_root = sem("b_o_root")
        self.o_normed = sem("b_o_normed")
        self.o_turned = sem("b_o_turned")
        self.o_shifted = sem("b_o_shifted")
        self.gate_silu = sem("b_gate_silu")
        self.gated_out = sem("b_gated_out")
        self.turned_o = sem("b_turned_o")
        self.oT_act = sem("b_oT_act")

    def sync(self, sp):
        k, a = self.k, self.k.a
        sp.wait_ge(k.x_done, self.n)
        for name, tile in (("theta", self.theta), ("norm_w", self.norm_w), ("conv_w", self.conv_w)):
            sp.dma_start(tile[...], a["b_" + name]).then_inc(self.small_in, 16)
        sp.dma_start(self.o_w[:, :], a["b_o_w"].partition_broadcast(P)).then_inc(self.small_in, 16)
        sp.dma_start(self.ramp[:, :, :], a["b_ramp"].partition_broadcast(P)).then_inc(self.small_in, 16)
        sp.dma_start(self.cin[:, :, :], a["b_cin"]).then_inc(self.w_in, 16)
        sp.wait_ge(self.cleared, 1)
        sp.dma_start(self.delta[:, :, 0:self.RUN - 1], a["b_delta"]).then_inc(self.w_in, 16)
        sp.dma_start(self.ctl[:, :, :], a["b_ctl"]).then_inc(self.w_in, 16)
        sp.dma_start(self.ctl_b[:, :], a["b_ctl_b"].partition_broadcast(P)).then_inc(self.w_in, 16)
        sp.dma_start(self.wo[:, :, :], a["b_wo"]).then_inc(self.w_in, 16)
        sp.dma_start(self.bo[:, :], a["b_bo"].partition_broadcast(P)).then_inc(self.w_in, 16)
        sp.wait_ge(self.cleared, 2)
        for t in range(NT):
            sp.wait_ge(self.mix_ready, t + 1)
            sp.dma_start(self.mix_dram[t * P:(t + 1) * P, :], self.mix[:, t, 0:800]).then_inc(self.mix_sent, 16)
            sp.wait_ge(self.mix_sent, 16 * (t + 1))
            for b in (2 * t, 2 * t + 1):
                sp.dma_start(self.rows[16 * b:16 * b + 16, 3:3 + S, :],
                             self.mix_dram[b * S:(b + 1) * S, :].rearrange("s (h c) -> h s c", h=16))\
                    .then_inc(self.rows_in, 16)

    def gpsimd(self, pool):
        k, nc = self.k, self.k.nc
        pool.wait_ge(k.x_done, self.n)
        nc.gpsimd.memset(self.delta[:, :, :], 0.0).then_inc(self.cleared, 1)
        nc.gpsimd.memset(self.ones[:, :], 1.0).then_inc(self.ones_set, 1)
        nc.gpsimd.memset(self.rows[:, 0:3, :], 0.0).then_inc(self.cleared, 1)
        norm_pool(k, pool, self.n)
        pool.wait_ge(self.ramped, 1)
        pool.wait_ge(self.w_in, 96)
        nc.gpsimd.tensor_tensor(self.delta[:, :, 0:self.RUN - 1], self.delta[:, :, 0:self.RUN - 1], self.ramp[:, :, :],
                                ALU.mult).then_inc(self.delta_ready, 1)
        pool.wait_ge(self.ms_eps, 1)
        nc.gpsimd.tensor_tensor(self.rms_inv[:, :], self.rms[:, :], k.minus_half[:, 0:NT], ALU.pow)\
            .then_inc(self.ms_inv, 1)
        pool.wait_ge(self.rows_in, 16 * B)
        pool.wait_ge(self.small_in, 80)
        order = 0
        for j in range(4):
            dst = self.conv if j == 0 else self.prod
            nc.gpsimd.tensor_tensor(dst[:, :, 0:16], self.rows[:, j:j + S, 0:16],
                                    self.conv_w[:, j:j + 1, 0:16].to_broadcast([P, S, 16]), ALU.mult)\
                .then_inc(self.q_prod, 1)
            order += 1
            pool.wait_ge(self.q_prod, order)
            if j:
                nc.gpsimd.tensor_tensor(self.conv[:, :, 0:16], self.conv[:, :, 0:16], self.prod[:, :, 0:16], ALU.add)\
                    .then_inc(self.q_prod, 1)
                order += 1
                pool.wait_ge(self.q_prod, order)
        pool.wait_ge(self.ready, 1)
        H = self.RING // 2

        def products(i, start, end):
            for j in range(self.RING):
                stand(k, pool, self.state_done, i * self.RING + (j + 1))
                if j % H == 0 and not start:
                    stand(k, pool, self.qs_read, 2 * i + (j // H - 1))
                q = self.qn[:, ds(i * self.RING + j, 1), :].to_broadcast([P, 16, 16])
                nc.gpsimd.tensor_tensor(self.qs[:, j, :, :], self.hist[:, j, :, :], q, ALU.mult).then_inc(self.qs_done, 1)

        self.rounds(pool, products)

    def rounds(self, eng, body):
        body(0, True, False)
        with eng.Fori(1, S // self.RING - 1) as i:
            body(i, False, False)
        body(S // self.RING - 1, False, True)

    def o_tokens(self, par, odd, tile=None):
        tile = self.o_tok if tile is None else tile
        return tile[64 * par:64 * par + 64, :, :].rearrange("p t (h j e) -> p t h j e", h=16, e=2)[:, :, :, :, odd]

    def o_psum(self, par, odd):
        view = self.k.ps_s[64 * odd:64 * odd + 64, 0:8 * P].rearrange("p (j t a h) -> p a t h j", j=8, t=NT, a=2)
        return view[:, par, :, :, :]

    def tensor(self, pe):
        k, nc = self.k, self.k.nc
        norm_tensor(k, pe, self.n)
        wait_norm(k, pe, self.n)
        pe.wait_ge(self.w_in, 96)
        for c in range(2):
            for f in range(FC):
                last = nc.tensor.matmul(k.ps_s[0:64, c * BANK:(c + 1) * BANK], self.cin[:, f, c * 64:(c + 1) * 64],
                                        k.xnT[:, f, :], start=(f == 0), stop=(f == FC - 1))
            last.then_inc(self.p_full, 1)
        pe.wait_ge(self.squared, 1)
        pe.wait_ge(self.ones_set, 1)
        for t in range(NT):
            for c in range(2):
                last = nc.tensor.matmul(k.ps_m[:, t:t + 1], self.part[:, c, t * P:(t + 1) * P], self.ones[:, :],
                                        start=(c == 0), stop=(c == 1))
        last.then_inc(self.ms_full, 1)
        pe.wait_ge(self.ms_inv, 1)
        for t in range(NT):
            last = nc.tensor.matmul(k.ps_o[0:64, t * P:(t + 1) * P], self.rms_inv[:, t:t + 1].to_broadcast([P, 64]),
                                    k.ident[:, :], start=True, stop=True)
        last.then_inc(self.spread_full, 1)
        pe.wait_ge(self.cond, 2)
        pe.wait_ge(self.delta_ready, 1)
        dw = self.delta[:, :, :].rearrange("p h c -> p (h c)")
        for t in range(NT):
            if t:
                pe.wait_ge(self.mix_ready, t)
            tok = slice(t * P, (t + 1) * P)
            for lo in range(0, self.W, BANK):
                hi = min(lo + BANK, self.W)
                nc.tensor.matmul(k.ps_s[:, lo:hi], k.xnT[:, 0, tok], self.ctl[:, 0, lo:hi], start=True, stop=False)
                if lo < 800:
                    top = min(hi, 800)
                    nc.tensor.matmul(k.ps_s[:, lo:top], self.condT[:, tok], dw[:, lo:top], start=False, stop=False)
                last = nc.tensor.matmul(k.ps_s[:, lo:hi], k.xnT[:, 1, tok], self.ctl[:, 1, lo:hi], start=False, stop=True)
            last.then_inc(self.mix_full, 1)
        pe.wait_ge(self.o_normed, 1)
        turned = self.o_dims[:, :, :].rearrange("p d s -> p (d s)")
        for j in range(8):
            last = nc.tensor.transpose(k.ps_s[:, j * P:(j + 1) * P], turned[:, j * P:(j + 1) * P], k.ident[:, :])
        last.then_inc(self.o_turned, 1)
        pe.wait_ge(self.gated_out, 4)
        for f in range(FC):
            for t in range(NT):
                last = nc.tensor.transpose(k.ps_t[:, f, t * P:(t + 1) * P], self.o_tok[:, t, f * P:(f + 1) * P],
                                           k.ident[:, :])
            last.then_inc(self.turned_o, 1)
        pe.wait_ge(self.oT_act, 2)
        for t in range(NT):
            for f in range(FC):
                last = nc.tensor.matmul(k.ps_s[:, t * BANK:t * BANK + D], self.oT[:, f, t * P:(t + 1) * P],
                                        self.wo[:, f, :], start=(f == 0), stop=(f == FC - 1))
            last.then_inc(k.y_full, 1)

    def scalar(self, act):
        k, nc = self.k, self.k.nc
        act.wait_ge(self.small_in, 80)
        nc.scalar.activation(self.ramp[:, :, :], self.ramp[:, :, :], ACT.Sigmoid).then_inc(self.ramped, 1)
        norm_scalar(k, act, self.n)
        act.wait_ge(self.angle, 1)
        nc.scalar.activation(self.turn_work[:, 2:3], self.turn_work[:, 1:2], ACT.Sin).then_inc(self.sines, 1)
        nc.scalar.activation(self.turn_work[:, 3:4], self.turn_work[:, 1:2], ACT.Sin, scale=0.5).then_inc(self.sines, 1)
        for c in range(2):
            act.wait_ge(self.p_full, c + 1)
            nc.scalar.activation(self.state[:, 0, c, :], k.ps_s[0:64, c * BANK:(c + 1) * BANK], ACT.Copy)\
                .then_inc(self.p_read, 1)
        act.wait_ge(self.spread_full, 1)
        nc.scalar.activation(self.spread[:, :], k.ps_o[0:64, :], ACT.Copy).then_inc(self.cosines, 1)
        act.wait_ge(self.rows_in, 16 * B)
        nc.scalar.activation(self.gates[:, :, :], self.rows[:, 3:3 + S, 48:50], ACT.Sigmoid).then_inc(self.gated, 1)
        act.wait_ge(self.mix_ready, NT)
        for t in range(NT):
            nc.scalar.activation(self.gate[:, t, :], self.mix[:, t, 800:self.W], ACT.Silu).then_inc(self.gate_silu, 1)
        act.wait_ge(self.q_prod, 7)
        nc.scalar.activation(self.act[:, :, 0:16], self.conv[:, :, 0:16], ACT.Silu).then_inc(self.silued, 1)
        act.wait_ge(self.silued, 1)
        nc.scalar.activation(self.prod[:, :, 0:16], self.act[:, :, 0:16], ACT.Square).then_inc(self.squares, 1)
        act.wait_ge(self.conved, 1)
        nc.scalar.activation(self.act[:, :, 16:48], self.conv[:, :, 16:48], ACT.Silu).then_inc(self.silued, 1)
        act.wait_ge(self.silued, 2)
        nc.scalar.activation(self.prod[:, :, 16:32], self.act[:, :, 16:32], ACT.Square).then_inc(self.squares, 1)
        act.wait_ge(self.rooted, 1)
        nc.scalar.activation(self.ssq[:, :, :], self.ssq[:, :, :], ACT.Sqrt).then_inc(self.roots, 1)
        act.wait_ge(self.o_ms, 1)
        nc.scalar.activation(self.ssq[:, 0, :], self.ssq[:, 0, :], ACT.Sqrt).then_inc(self.o_root, 1)
        act.wait_ge(self.o_turned, 1)
        nc.scalar.activation(self.o_tokens(0, 1), self.o_psum(0, 1), ACT.Copy).then_inc(self.o_shifted, 1)
        act.wait_ge(self.gated_out, 1)
        nc.scalar.activation(self.o_tokens(1, 0), self.o_psum(1, 0), ACT.Copy).then_inc(self.o_shifted, 1)
        for f in range(FC):
            act.wait_ge(self.turned_o, f + 1)
            nc.scalar.activation(self.oT[:, f, :], k.ps_t[:, f, :], ACT.Copy).then_inc(self.oT_act, 1)

    def vector(self, dve):
        k, nc = self.k, self.k.nc
        v = nc.vector
        chain = lambda ins: link(k, dve, ins)
        norm_vector(k, dve, self.n)
        dve.wait_ge(self.small_in, 80)
        w = self.turn_work
        TWO_PI_HI, TWO_PI_LO, MAGIC = 6.28125, 0.0019353071795864769, 12582912.0
        chain(v.tensor_scalar(w[:, 0:1], self.theta[:, :], 0.15915494309189535, MAGIC, ALU.mult, ALU.add))
        chain(v.tensor_scalar(w[:, 0:1], w[:, 0:1], MAGIC, None, ALU.subtract))
        chain(v.scalar_tensor_tensor(w[:, 1:2], w[:, 0:1], -TWO_PI_HI, self.theta[:, :], ALU.mult, ALU.add))
        chain(v.scalar_tensor_tensor(w[:, 1:2], w[:, 0:1], -TWO_PI_LO, w[:, 1:2], ALU.mult, ALU.add))
        v.tensor_scalar(w[:, 1:2], w[:, 1:2], 3.1415925, -3.1415925, ALU.min, ALU.max).then_inc(self.angle, 1)
        dve.wait_ge(self.sines, 2)
        cs = self.cos_sin
        v.tensor_copy(cs[:, 0, 1:2], w[:, 2:3])
        chain(v.tensor_tensor(w[:, 4:5], w[:, 3:4], w[:, 3:4], ALU.mult))
        chain(v.tensor_scalar(cs[:, 0, 0:1], w[:, 4:5], -2.0, 1.0, ALU.mult, ALU.add))
        for j in range(1, 6):
            c, s_ = cs[:, j - 1, 0:1], cs[:, j - 1, 1:2]
            chain(v.tensor_tensor(w[:, 5:6], s_, s_, ALU.mult))
            v.tensor_scalar(cs[:, j, 0:1], w[:, 5:6], -2.0, 1.0, ALU.mult, ALU.add)
            chain(v.tensor_scalar(cs[:, j, 1:2], s_, c, 2.0, ALU.mult, ALU.mult))
        chain(v.tensor_scalar(cs[:, :, 2], cs[:, :, 1], -1.0, None, ALU.mult))
        dve.wait_ge(self.p_read, 2)
        part = self.part[:, :, :].rearrange("p c (b s) -> p c b s", s=S)
        for j in range(6):
            d = 1 << j
            old = self.state[:, j % 2, :, :].rearrange("p c (b s) -> p c b s", s=S)
            new = self.state[:, 1 - j % 2, :, :].rearrange("p c (b s) -> p c b s", s=S)
            c, s_, ms = (cs[:, j, q:q + 1] for q in range(3))
            for q in range(2):
                v.scalar_tensor_tensor(part[:, q, :, d:S], old[:, q, :, 0:S - d], c, old[:, q, :, d:S], ALU.mult, ALU.add)
            chain(v.tensor_copy(self.state[:, 1 - j % 2, :, :].rearrange("p c (b s) -> p (c b) s", s=S)[:, :, 0:d],
                                self.state[:, j % 2, :, :].rearrange("p c (b s) -> p (c b) s", s=S)[:, :, 0:d]))
            v.scalar_tensor_tensor(new[:, 0, :, d:S], old[:, 1, :, 0:S - d], ms, part[:, 0, :, d:S], ALU.mult, ALU.add)
            chain(v.scalar_tensor_tensor(new[:, 1, :, d:S], old[:, 0, :, 0:S - d], s_, part[:, 1, :, d:S],
                                         ALU.mult, ALU.add))
        st = self.state[:, 0, :, :]
        v.tensor_tensor(self.part[:, :, :], st, st, ALU.mult).then_inc(self.squared, 1)
        dve.wait_ge(self.ms_full, 1)
        v.tensor_scalar(self.rms[:, :], k.ps_m[:, 0:NT], 1.0 / P, 1e-6, ALU.mult, ALU.add).then_inc(self.ms_eps, 1)
        dve.wait_ge(self.cosines, 1)
        for q in range(2):
            v.scalar_tensor_tensor(self.condT[64 * q:64 * q + 64, :], self.state[:, 0, q, :], self.norm_w[:, q:q + 1],
                                   self.spread[:, :], ALU.mult, ALU.mult).then_inc(self.cond, 1)
        for t in range(NT):
            dve.wait_ge(self.mix_full, t + 1)
            v.tensor_tensor(self.mix[:, t, :], k.ps_s[:, 0:self.W], self.ctl_b[:, :], ALU.add).then_inc(self.mix_ready, 1)
        dve.wait_ge(self.rows_in, 16 * B)
        for j in range(4):
            dst = self.conv if j == 0 else self.prod
            chain(v.tensor_tensor(dst[:, :, 16:48], self.rows[:, j:j + S, 16:48],
                                  self.conv_w[:, j:j + 1, 16:48].to_broadcast([P, S, 32]), ALU.mult))
            if j:
                last = v.tensor_tensor(self.conv[:, :, 16:48], self.conv[:, :, 16:48], self.prod[:, :, 16:48], ALU.add)
                if j < 3:
                    chain(last)
        last.then_inc(self.conved, 1)
        for q in range(2):
            dve.wait_ge(self.squares, q + 1)
            last = v.tensor_reduce(self.ssq[:, q, :], self.prod[:, :, 16 * q:16 * q + 16], AX.X, ALU.add)
        chain(last)
        v.tensor_scalar(self.ssq[:, :, :], self.ssq[:, :, :], 1e-6, None, ALU.add).then_inc(self.rooted, 1)
        dve.wait_ge(self.gated, 1)
        beta, g = self.gates[:, :, 0], self.gates[:, :, 1]
        v.scalar_tensor_tensor(self.neg_gb[:, :], beta, -1.0, g, ALU.mult, ALU.mult)
        v.tensor_tensor(self.kv[:, :, 0, :], self.act[:, :, 32:48],
                        self.gates[:, :, 0:1].to_broadcast([P, S, 16]), ALU.mult)
        dve.wait_ge(self.roots, 1)
        chain(v.reciprocal(self.ssq_inv[:, :, :], self.ssq[:, :, :]))
        v.memset(self.tmp[:, :, :], 0.0)
        v.memset(self.hist[:, self.RING - 1, :, :], 0.0)
        inv = self.ssq_inv[:, :, :]
        v.tensor_tensor(self.kv[:, :, 1, :], self.act[:, :, 16:32],
                        inv[:, 1, :].rearrange("p (s o) -> p s o", o=1).to_broadcast([P, S, 16]), ALU.mult)
        last = v.tensor_tensor(self.qn[:, :, :], self.act[:, :, 0:16],
                               inv[:, 0, :].rearrange("p (s o) -> p s o", o=1).to_broadcast([P, S, 16]), ALU.mult)
        chain(last)
        v.nop().then_inc(self.ready, 1)
        last = v.tensor_tensor(self.prod[:, 1:S, 0:16], self.kv[:, 1:S, 1, :], self.kv[:, 0:S - 1, 1, :], ALU.mult)
        v.memset(self.past[:, :], 0.0)
        v.memset(self.u[:, :], 0.0)
        v.memset(self.coef[:, 0:1, :], 0.0)
        v.tensor_tensor(self.coef[:, 1:S, 0], self.neg_gb[:, 1:S], self.gates[:, 0:S - 1, 1], ALU.mult)
        chain(last)
        chain(v.tensor_reduce(self.ssq[:, 0, 1:S], self.prod[:, 1:S, 0:16], AX.X, ALU.add))
        chain(v.tensor_tensor(self.coef[:, 1:S, 1], self.neg_gb[:, 1:S], self.ssq[:, 0, 1:S], ALU.mult))
        R, H = self.RING, self.RING // 2
        col = lambda tile, at: tile[:, ds(at, 1)] if not isinstance(at, int) else tile[:, at:at + 1]

        def keys_at(t):
            return self.kv[:, ds(t, 1), 1, :].to_broadcast([P, 16, 16])

        def outputs(half):
            stand(k, dve, self.qs_done, half * H + H)
            lo = H * (half % 2) if isinstance(half, int) else H * self.half_slot
            v.tensor_reduce(self.o[:, ds(half * H, H), :].rearrange("p s d -> p (s d)"),
                            self.qs[:, lo:lo + H, :, :].rearrange("p s v k -> p (s v) k"), AX.X, ALU.add)\
                .then_inc(self.qs_read, 1)

        def recur(i, start, end):
            for j in range(R):
                t = i * R + j
                prev = self.hist[:, (j - 1) % R, :, :]
                done = 5 * R * i + 5 * j
                if not (start and j == 0):
                    stand(k, dve, self.step, done)
                v.scalar_tensor_tensor(self.begun[:, :], self.past[:, :], self.coef[:, ds(t, 1), 0],
                                       self.kv[:, ds(t, 1), 0, :].rearrange("p a d -> p (a d)"), ALU.mult, ALU.add)\
                    .then_inc(self.step, 1)
                if not (start and j == 0):
                    stand(k, dve, self.state_done, t)
                ahead = not (end and j == R - 1)
                if ahead:
                    v.tensor_tensor(self.tmp[:, :, :], prev, keys_at(t + 1), ALU.mult).then_inc(self.step, 1)
                stand(k, dve, self.step, done + 1)
                v.scalar_tensor_tensor(self.u[:, :], self.u[:, :], self.coef[:, ds(t, 1), 1], self.begun[:, :],
                                       ALU.mult, ALU.add).then_inc(self.step, 1)
                stand(k, dve, self.step, done + 2 + ahead)
                v.tensor_tensor(self.outer[:, :, :], self.u[:, :].rearrange("p (v o) -> p v o", o=1)
                                .to_broadcast([P, 16, 16]), keys_at(t), ALU.mult).then_inc(self.step, 1)
                if ahead:
                    v.tensor_reduce(self.past[:, :], self.tmp[:, :, :], AX.X, ALU.add).then_inc(self.step, 1)
                stand(k, dve, self.step, done + 3 + ahead)
                v.scalar_tensor_tensor(self.hist[:, j, :, :], prev, self.gates[:, ds(t, 1), 1], self.outer[:, :, :],
                                       ALU.mult, ALU.add).then_inc(self.state_done, 1)
                if j % H == 1 and not (start and j < H):
                    self.half_slot = 1 - j // H
                    outputs(2 * i + j // H - 1)

        self.rounds(dve, recur)
        outputs(S // H - 1)
        dve.wait_ge(self.qs_read, S // H)
        chain(v.tensor_tensor(self.o_sq[:, :, :], self.o[:, :, :], self.o[:, :, :], ALU.mult))
        chain(v.tensor_reduce(self.ssq[:, 0, :], self.o_sq[:, :, :], AX.X, ALU.add))
        v.tensor_scalar(self.ssq[:, 0, :], self.ssq[:, 0, :], 1.0 / 16, 1e-6, ALU.mult, ALU.add).then_inc(self.o_ms, 1)
        dve.wait_ge(self.o_root, 1)
        chain(v.reciprocal(self.ssq_inv[:, 0, :], self.ssq[:, 0, :]))
        chain(v.tensor_tensor(self.o[:, :, :], self.o[:, :, :],
                              inv[:, 0, :].rearrange("p (s o) -> p s o", o=1).to_broadcast([P, S, 16]), ALU.mult))
        v.tensor_tensor(self.o_dims[:, :, :].rearrange("p d s -> p s d"), self.o[:, :, :],
                        self.o_w[:, :].rearrange("p (o d) -> p o d", o=1).to_broadcast([P, S, 16]), ALU.mult)\
            .then_inc(self.o_normed, 1)
        dve.wait_ge(self.gate_silu, NT)
        dve.wait_ge(self.o_turned, 1)
        v.tensor_tensor(self.o_tokens(0, 0), self.o_psum(0, 0), self.o_tokens(0, 0, self.gate), ALU.mult)\
            .then_inc(self.gated_out, 1)
        dve.wait_ge(self.o_shifted, 1)
        v.tensor_tensor(self.o_tokens(1, 1), self.o_psum(1, 1), self.o_tokens(1, 1, self.gate), ALU.mult)\
            .then_inc(self.gated_out, 1)
        v.tensor_tensor(self.o_tokens(0, 1), self.o_tokens(0, 1), self.o_tokens(0, 1, self.gate), ALU.mult)\
            .then_inc(self.gated_out, 1)
        dve.wait_ge(self.o_shifted, 2)
        v.tensor_tensor(self.o_tokens(1, 0), self.o_tokens(1, 0), self.o_tokens(1, 0, self.gate), ALU.mult)\
            .then_inc(self.gated_out, 1)
        finish(k, dve, lambda t: self.bo[:, :], lambda t: k.ps_s[:, t * BANK:t * BANK + D], self.n)


class Experts:

    E = 8
    HC = None
    LAG = None
    RING = None
    WIDE = None

    def experts_memory(self, k, sb, name):
        sem = k.sem
        self.logits = sb("logits", [P, NT, 8])
        self.top = sb("top", [P, NT, 8])
        self.top_i = sb("top_i", [P, NT, 8], U32)
        self.top_f = sb("top_f", [P, NT, 8])
        self.gap = sb("gap", [P, NT])
        self.second = sb("second", [P, NT])
        self.total = sb("total", [P, NT])
        self.p1 = sb("p1", [P, NT])
        self.p2 = sb("p2", [P, NT])
        self.index_i = sb("index_i", [P, 8], U32)
        self.index = sb("index", [P, 8])
        self.pick = sb("pick", [P, NT, 8])
        self.w = sb("w", [P, NT, 8])
        self.wT = sb("wT", [P, T])
        self.wide = sb("wide", [P, 8, T])
        self.PIECES = self.HC // 2
        self.PW = self.WIDE // self.PIECES
        self.raw = sb("raw", [P, 2, self.WIDE])
        self.w_hi = sb("w_hi", [P, 2, self.WIDE], F32R)
        self.w_lo = sb("w_lo", [P, 2, self.WIDE], F32R)
        self.x_hi = sb("x_hi", [P, FC, T], F32R)
        self.x_lo = sb("x_lo", [P, FC, T], F32R)
        self.hid = sb("hid", [P, 4, T])
        self.hid_hi = sb("hid_hi", [P, 4, T], F32R)
        self.hid_lo = sb("hid_lo", [P, 4, T], F32R)
        self.yT = sb("yT", [P, FC, T])
        self.R, self.U, self.low_before = k.rounds, k.units, k.units // 2
        k.rounds, k.units = k.rounds + 1, k.units + self.E * self.HC
        self.router_in = sem(name + "router_in")

        def shared(n):
            if n not in k.shared:
                k.shared[n] = sem("experts_" + n)
            return k.shared[n]

        self.w_counted = shared("w_counted")
        self.logits_full = shared("logits_full")
        self.gapped = shared("gapped")
        self.second_done = shared("second_done")
        self.w_ready = shared("w_ready")
        self.wT_full = shared("wT_full")
        self.wT_done = shared("wT_done")
        self.wide_full = shared("wide_full")
        self.wide_done = shared("wide_done")
        self.hid_full = shared("hid_full")
        self.hid_act = shared("hid_act")
        self.hid_parts = shared("hid_parts")
        self.hid_done = shared("hid_done")
        self.high = shared("high")
        self.low = shared("low")
        self.x_high = shared("x_high")
        self.x_split = shared("x_split")
        self.y_unit = shared("y_unit")
        self.yT_act = shared("yT_act")
        self.yT_dve = shared("yT_dve")
        self.e_in = [sem(name + "e_in0"), sem(name + "e_in1")]

    def bodies(self, eng, body):
        body(0, True, False)
        with eng.Fori(1, self.E // 2 - 1) as i:
            body(i, False, False)
        body(self.E // 2 - 1, False, True)

    def load(self, sp, e, p):
        src = self.k.a[self.WEIGHTS]
        at = src[e] if isinstance(e, int) else src[ds(e, 1)].rearrange("a p m -> (a p) m")
        sp.dma_start(self.raw[:, p, :], at).then_inc(self.e_in[p], 16)

    def sync_experts(self, k, sp):
        for e in range(2):
            self.load(sp, e, e)
        with sp.Fori(1, self.E // 2) as i:
            for p in range(2):
                sp.wait_ge(self.low, self.low_before + self.PIECES * (2 * (i - 1) + p + 1))
                self.load(sp, 2 * i + p, p)

    def gpsimd(self, pool):
        k = self.k
        pool.wait_ge(k.x_done, self.n)
        k.nc.gpsimd.memset(self.wT[:, :], 0.0).then_inc(self.w_counted, 1)
        k.nc.gpsimd.iota(self.index_i[:, :], pattern=[[1, 8]], base=0, channel_multiplier=0).then_inc(self.w_counted, 1)
        norm_pool(k, pool, self.n)

        def body(i, start, end):
            for u in range(2 * self.HC):
                e, c = u // self.HC, u % self.HC
                if c < self.PIECES and not (end and e == 1):
                    self.split_low(k, pool, 2 * i + e + 1, 1 - e, c)

        for c in range(self.PIECES):
            self.split_low(k, pool, 0, 0, c)
        self.bodies(pool, body)

    def split_x(self, k, dve):
        wait_norm(k, dve, self.n)
        k.nc.vector.tensor_copy(self.x_hi[:, :, :], k.xnT[:, :, :]).then_inc(self.x_high, 1)
        dve.wait_ge(self.x_high, self.R + 1)
        k.nc.vector.tensor_tensor(self.x_lo[:, :, :], k.xnT[:, :, :], self.x_hi[:, :, :].bitcast(F32), ALU.subtract)\
            .then_inc(self.x_split, 1)

    def weights_of(self, e):
        return self.wide[:, e, :] if isinstance(e, int) else self.wide[:, ds(e, 1), :].rearrange("p a t -> p (a t)")

    def split_high(self, k, act, e, p, c):
        at = slice(c * self.PW, (c + 1) * self.PW)
        k.nc.scalar.activation(self.w_hi[:, p, at], self.raw[:, p, at], ACT.Copy).then_inc(self.high, 1)

    def split_low(self, k, pool, e, p, c):
        at = slice(c * self.PW, (c + 1) * self.PW)
        stand(k, pool, self.high, self.low_before + self.PIECES * e + c + 1)
        k.nc.gpsimd.tensor_tensor(self.w_lo[:, p, at], self.raw[:, p, at], self.w_hi[:, p, at].bitcast(F32), ALU.subtract)\
            .then_inc(self.low, 1)

    def choose(self, k, dve, bias):
        v = k.nc.vector
        chain = lambda ins: link(k, dve, ins)
        dve.wait_ge(self.w_counted, 2 * (self.R + 1))
        v.tensor_copy(self.index[:, :], self.index_i[:, :])
        dve.wait_ge(self.logits_full, self.R + 1)
        E = self.ROUTED
        if E < 8:
            v.memset(self.logits[:, :, E:8], -3.0e38)
        chain(v.tensor_tensor(self.logits[:, :, 0:E], k.ps_m[:, 0:NT * 8].rearrange("p (t e) -> p t e", e=8)[:, :, 0:E],
                              bias.to_broadcast([P, NT, E]), ALU.add))
        for t in range(NT):
            last = v.max(self.top[:, t, :], self.logits[:, t, :])
        chain(last)
        for t in range(NT):
            v.max_index(self.top_i[:, t, :], self.top[:, t, :], self.logits[:, t, :])
        v.tensor_tensor(self.gap[:, :], self.top[:, :, 1], self.top[:, :, 0], ALU.subtract).then_inc(self.gapped, 1)
        chain(v.tensor_copy(self.index[:, :], self.index_i[:, :]))
        dve.wait_ge(self.second_done, self.R + 1)
        chain(v.tensor_copy(self.top_f[:, :, :], self.top_i[:, :, :]))
        chain(v.tensor_scalar(self.total[:, :], self.second[:, :], 1.0, None, ALU.add))
        chain(v.reciprocal(self.p1[:, :], self.total[:, :]))
        chain(v.tensor_tensor(self.p2[:, :], self.second[:, :], self.p1[:, :], ALU.mult))
        for t in range(NT):
            v.tensor_scalar(self.w[:, t, :], self.index[:, :], self.top_f[:, t, 0:1], self.p1[:, t:t + 1],
                            ALU.is_equal, ALU.mult)
            last = v.tensor_scalar(self.pick[:, t, :], self.index[:, :], self.top_f[:, t, 1:2], self.p2[:, t:t + 1],
                                   ALU.is_equal, ALU.mult)
        chain(last)
        last = v.tensor_tensor(self.w[:, :, :], self.w[:, :, :], self.pick[:, :, :], ALU.add)
        if E < 8:
            chain(last)
            last = v.memset(self.w[:, :, E:8], 1.0)
        last.then_inc(self.w_ready, 1)
        dve.wait_ge(self.wT_full, self.R + 1)
        v.tensor_copy(self.wT[0:8, :], k.ps_o[0:8, :]).then_inc(self.wT_done, 1)

    def spread(self, k, pe):
        nc = k.nc
        pe.wait_ge(self.w_ready, self.R + 1)
        for t in range(NT):
            last = nc.tensor.matmul(k.ps_o[0:8, t * P:(t + 1) * P], self.w[:, t, :], k.ident[:, :], start=True, stop=True)
        last.then_inc(self.wT_full, 1)
        pe.wait_ge(self.wT_done, self.R + 1)
        for e in range(self.E):
            if e >= 2:
                pe.wait_ge(self.wide_done, self.E * self.R + e - 1)
            nc.tensor.matmul(k.ps_t[:, e % 2, :], k.ident[:, e:e + 1].to_broadcast([P, P]), self.wT[:, :],
                             start=True, stop=True).then_inc(self.wide_full, 1)
        pe.wait_ge(self.wide_done, self.E * (self.R + 1))

    def act_spread(self, k, act):
        for e in range(self.E):
            act.wait_ge(self.wide_full, self.E * self.R + e + 1)
            k.nc.scalar.activation(self.wide[:, e, :], k.ps_t[:, e % 2, :], ACT.Copy).then_inc(self.wide_done, 1)

    def tensor_begin(self, k, pe):
        pe.wait_ge(self.x_split, self.R + 1)
        for u in range(self.LAG):
            self.first_unit(k, pe, 0, u)

    def first_unit(self, k, pe, i, u):
        HC = self.HC
        e, c = u // HC % 2, u % HC
        if c == 0:
            stand(k, pe, self.low, self.low_before + self.PIECES * (2 * (i + u // (2 * HC)) + e + 1))
        n = 2 * HC * i + u
        if not (isinstance(n, int) and n < self.RING):
            stand(k, pe, self.hid_done, n + (self.U - self.RING + 1))
        self.pe_first(k, pe, e, c, u % self.RING).then_inc(self.hid_full, 1)

    def tensor_experts(self, k, pe, begun):
        HC, L = self.HC, self.LAG

        def body(i, start, end):
            for u in range(2 * HC):
                if not (end and u + L >= 2 * HC):
                    self.first_unit(k, pe, i, u + L)
                stand(k, pe, self.hid_done, 2 * HC * i + (self.U + u + 1))
                e, c = u // HC, u % HC
                for f in range(FC):
                    at = self.second_column(c, f)
                    last = self.three(k, k.ps_t[:, f, :], e, at, self.hid_hi[:, u % 4, :], self.hid_lo[:, u % 4, :],
                                      start and u == 0 and not begun, end and u == 2 * HC - 1)
                last.then_inc(self.y_unit, 1)

        self.bodies(pe, body)
        pe.wait_ge(self.yT_act, self.R + 1)
        pe.wait_ge(self.yT_dve, self.R + 1)
        for t in range(NT):
            for f in range(FC):
                last = k.nc.tensor.transpose(k.ps_s[:, t * BANK + f * P:t * BANK + (f + 1) * P],
                                             self.yT[:, f, t * P:(t + 1) * P], k.ident[:, :])
            last.then_inc(k.y_full, 1)

    def three(self, k, out, e, at, high, low, start, stop):
        mm = k.nc.tensor.matmul
        mm(out, self.w_hi[:, e, at:at + P], high, start=start, stop=False)
        mm(out, self.w_hi[:, e, at:at + P], low, start=False, stop=False)
        return mm(out, self.w_lo[:, e, at:at + P], high, start=False, stop=stop)

    def scalar_experts(self, k, act):
        HC = self.HC

        def body(i, start, end):
            for u in range(2 * HC):
                e, c = u // HC, u % HC
                stand(k, act, self.hid_full, 2 * HC * i + (self.U + u + 1))
                self.act_unit(k, act, 2 * i + e, c, u % self.RING).then_inc(self.hid_act, 1)
                if c < self.PIECES and not (end and e == 1):
                    if c == 0:
                        stand(k, act, self.e_in[1 - e], 16 * (i + e + 1))
                        if not (start and e == 0):
                            stand(k, act, self.y_unit, 2 * HC * i + (self.U + HC * e))
                    self.split_high(k, act, 2 * i + e + 1, 1 - e, c)

        self.bodies(act, body)
        act.wait_ge(self.y_unit, self.U + self.E * HC)
        k.nc.scalar.activation(self.yT[:, 0, :], k.ps_t[:, 0, :], ACT.Copy).then_inc(self.yT_act, 1)

    def vector_experts(self, k, dve):
        HC = self.HC

        def body(i, start, end):
            for u in range(2 * HC):
                n = 2 * HC * i + u
                stand(k, dve, self.hid_act, n + (self.U + 1))
                self.dve_unit(k, dve, u, n)
                v = k.nc.vector
                for dst in (self.hid[:, u % 4, :], self.hid_hi[:, u % 4, :]):
                    v.tensor_tensor(dst, self.unweighted(u), self.weights_of(2 * i + u // HC), ALU.mult)\
                        .then_inc(self.hid_parts, 1)
                stand(k, dve, self.hid_parts, 2 * (n + (self.U + 1)))
                v.tensor_tensor(self.hid_lo[:, u % 4, :], self.hid[:, u % 4, :], self.hid_hi[:, u % 4, :].bitcast(F32),
                                ALU.subtract).then_inc(self.hid_done, 1)

        self.bodies(dve, body)
        dve.wait_ge(self.y_unit, self.U + self.E * HC)
        k.nc.vector.tensor_copy(self.yT[:, 1, :], k.ps_t[:, 1, :]).then_inc(self.yT_dve, 1)


class StageC(Experts):

    HC, LAG, RING = 4, 2, 4
    WEIGHTS, WIDE = "c_w", FC * 512 + 4 * D
    ROUTED = 8

    def __init__(self, k, n):
        self.k, self.n = k, n
        with ExitStack() as st:
            sb = lambda name, shape, dt=F32: k.sb("c_" + name, shape, dt, st)
            self.experts_memory(k, sb, "c_")
            self.rw1 = sb("rw1", [P, FC, D])
            self.rb1 = sb("rb1", [P, FC])
            self.rw2 = sb("rw2", [P, FC, 8])
            self.rb2 = sb("rb2", [P, 1, 8])
            self.b1 = sb("b1", [P, 8, 4])
            self.b2 = sb("b2", [8, D])
            self.rh = sb("rh", [P, FC, T])
            self.sg = sb("sg", [P, 4, T])
            self.rh_full = k.sem("c_rh_full")
            self.rh_done = k.sem("c_rh_done")

    def sync(self, sp):
        k, a = self.k, self.k.a
        sp.wait_ge(k.x_done, self.n)
        for name, tile in (("rw1", self.rw1), ("rb1", self.rb1), ("rw2", self.rw2), ("b1", self.b1), ("b2", self.b2)):
            sp.dma_start(tile[...], a["c_" + name]).then_inc(self.router_in, 16)
        sp.dma_start(self.rb2[:, 0, :], a["c_rb2"].partition_broadcast(P)).then_inc(self.router_in, 16)
        self.sync_experts(k, sp)

    def tensor(self, pe):
        k, nc = self.k, self.k.nc
        norm_tensor(k, pe, self.n)
        wait_norm(k, pe, self.n)
        pe.wait_ge(self.router_in, 96)
        for m in range(FC):
            for f in range(FC):
                last = nc.tensor.matmul(k.ps_s[:, m * BANK:(m + 1) * BANK], self.rw1[:, f, m * P:(m + 1) * P],
                                        k.xnT[:, f, :], start=(f == 0), stop=(f == FC - 1))
            last.then_inc(self.rh_full, 1)
        pe.wait_ge(self.rh_done, 2)
        for t in range(NT):
            for f in range(FC):
                last = nc.tensor.matmul(k.ps_m[:, t * 8:(t + 1) * 8], self.rh[:, f, t * P:(t + 1) * P], self.rw2[:, f, :],
                                        start=(f == 0), stop=(f == FC - 1))
        last.then_inc(self.logits_full, 1)
        self.tensor_begin(k, pe)
        self.spread(k, pe)
        for f in range(FC):
            nc.tensor.matmul(k.ps_t[:, f, :], self.b2[:, f * P:(f + 1) * P], self.wT[0:8, :], start=True, stop=False)
        self.tensor_experts(k, pe, True)

    def pe_first(self, k, pe, e, c, r):
        for f in range(FC):
            last = self.three(k, k.ps_s[:, r * BANK:(r + 1) * BANK], e, f * 512 + c * P, self.x_hi[:, f, :],
                              self.x_lo[:, f, :], f == 0, f == FC - 1)
        return last

    def second_column(self, c, f):
        return FC * 512 + c * D + f * P

    def unweighted(self, u):
        return self.sg[:, u % 4, :]

    def scalar(self, act):
        k, nc = self.k, self.k.nc
        norm_scalar(k, act, self.n)
        act.wait_ge(self.router_in, 96)
        for m in range(FC):
            act.wait_ge(self.rh_full, m + 1)
            nc.scalar.activation(self.rh[:, m, :], k.ps_s[:, m * BANK:(m + 1) * BANK], ACT.Silu,
                                 bias=self.rb1[:, m:m + 1]).then_inc(self.rh_done, 1)
        act.wait_ge(self.e_in[0], 16)
        for c in range(self.PIECES):
            self.split_high(k, act, 0, 0, c)
        act.wait_ge(self.gapped, self.R + 1)
        nc.scalar.activation(self.second[:, :], self.gap[:, :], ACT.Exp).then_inc(self.second_done, 1)
        self.act_spread(k, act)
        self.scalar_experts(k, act)

    def act_unit(self, k, act, e, c, r):
        b = self.b1[:, e, c:c + 1] if isinstance(e, int) else self.b1[:, ds(e, 1), c]
        return k.nc.scalar.activation(self.sg[:, r, :], k.ps_s[:, r * BANK:(r + 1) * BANK], ACT.Silu, bias=b)

    def dve_unit(self, k, dve, u, n):
        pass

    def vector(self, dve):
        k = self.k
        norm_vector(k, dve, self.n)
        self.split_x(k, dve)
        dve.wait_ge(self.router_in, 96)
        self.choose(k, dve, self.rb2[:, :, :])
        self.vector_experts(k, dve)
        finish(k, dve, lambda t: k.xn[:, t, :], lambda t: k.ps_s[:, t * BANK:t * BANK + D], self.n)


class StageD(Attention):

    name = "d_"
    G = 8
    FOLDED = True
    SCALE = 0.25
    FIRST_FILLS = [("k", 0)] + [f for g in range(7) for f in (("k", g + 1), ("v", g))]
    STACKED = 16 * 12

    def __init__(self, k, n):
        self.n, self.k = n, k
        sem = k.sem
        with ExitStack() as st:
            sb = lambda name, shape, dt=F32: k.sb("d_" + name, shape, dt, st)
            self.wq = sb("wq", [P, FC, D])
            self.wk = sb("wk", [P, FC, D])
            self.wv = sb("wv", [P, FC, D])
            self.wo = sb("wo", [P, 2, D])
            self.bq = sb("bq", [P, FC])
            self.bk = sb("bk", [P, FC])
            self.bv = sb("bv", [P, 2])
            self.bo = sb("bo", [P, D])
            self.k_rot = sb("k_rot", [P, 2, M])
            self.q_rot = sb("q_rot", [P, 2, S])
            self.head_of = sb("head_of", [P, 2, S])
            self.ctxT = sb("ctxT", [P, 2, FC, M])
            self.k_split = sb("k_split", [P, 2, MP], F32R)
            self.k_stack = sb("k_stack", [3 * 32, 8, MP], F32R)
            self.v = sb("v", [P, 2, MC, D])
            self.k_raw = sb("k_raw", [P, 2, BANK])
            self.k_swap = sb("k_swap", [P, 2, BANK])
            self.q_raw = sb("q_raw", [P, FC, T])
            self.q_hi = sb("q_hi", [P, FC, T], F32R)
            self.q_lo = sb("q_lo", [P, FC, T], F32R)
            self.q_stack = sb("q_stack", [3 * 32, 2, FC, 4, 2, S], F32R)
            self.o = sb("o", [P, 2, 8, 16])
            self.oT = sb("oT", [P, 2, T])
            self.parts = sb("parts", [P, P])
            self.fold = sb("fold", [P, 32])
            self.attention_memory(k, st)
        self.parted = sem("d_parted")
        self.unfolded = sem("d_unfolded")
        self.w_in = sem("d_w_in")
        self.late_in = sem("d_late_in")
        self.q_full = sem("d_q_full")
        self.q_read = sem("d_q_read")
        self.qm_ready = sem("d_qm_ready")
        self.k_swapped = sem("d_k_swapped")
        self.k_part = sem("d_k_part")
        self.k_roped = sem("d_k_roped")
        self.ctxT_in = [sem("d_ctxT_in0"), sem("d_ctxT_in1")]
        self.stacked = [sem("d_stacked0"), sem("d_stacked1")]
        self.padded = sem("d_padded")
        self.first_fills = 15 + 15 + 16
        self.fills = 32

    def fills_before(self, s, first, last):
        g = s % 8
        if g == 0:
            return [] if first and s == 0 else [("o", 1 - s // 8)]
        return [] if last and s >= 8 else [("k", 1 - s // 8, g, 1 + s // 8)]

    def fills_after(self, s, first, last):
        g = s % 8
        if last and s >= 8:
            return []
        return [("k", 1 - s // 8, 0, 1 + s // 8)] if g == 0 else [("v", 1 - s // 8, g - 1, 1 + s // 8)]

    def values(self, s, c):
        g = s % 8
        return self.v[0:keys(c), s // 8, c, g * 32:(g + 1) * 32]

    def pe_value(self, k, pe, n, s, q):
        pe.wait_ge(self.moved_act if q % 2 else self.moved_dve, 2 * n + 1 + q // 2)
        for j, c in enumerate(QUADS[q]):
            last = k.nc.tensor.matmul(k.ps_o[32 * j:32 * j + 32, 0:P], self.values(s, c), self.pT[0:keys(c), c, :],
                                      start=(c < 4), stop=(c + 4 >= MC))
        return last

    def pe_fold(self, k, pe, n):
        stand(k, pe, self.unfolded, n + 1)
        k.nc.tensor.matmul(k.ps_o[:, P:P + 32], self.parts[:, :], self.fold[:, :], start=True, stop=True)\
            .then_inc(self.valued, 1)

    def dve_unfold(self, k, dve):
        k.nc.vector.tensor_copy(self.parts[:, :], k.ps_o[:, 0:P]).then_inc(self.unfolded, 1)

    def sync(self, sp):
        k, a = self.k, self.k.a
        sp.wait_ge(k.x_done, self.n)

        def load(b, p):
            srcT = a["ctxT"][b] if isinstance(b, int) else a["ctxT"][ds(b, 1)].rearrange("a p f m -> (a p) f m")
            if not (isinstance(b, int) and b < 2):
                sp.wait_ge(self.scored, 8 * (b - 2) + 2)
            sp.dma_start(self.ctxT[:, p, :, :], srcT).then_inc(self.ctxT_in[p], 16)

        for name, tile in (("wq", self.wq), ("bq", self.bq), ("q_rot", self.q_rot), ("head_of", self.head_of),
                           ("fold", self.fold),
                           ("wk", self.wk), ("bk", self.bk), ("wv", self.wv)):
            sp.dma_start(tile[...], a["d_" + name]).then_inc(self.w_in, 16)
        load(0, 0)
        sp.dma_start(self.k_rot[:, :, :], a["d_k_rot"]).then_inc(self.w_in, 16)
        load(1, 1)
        sp.dma_start(self.wo[:, :, :], a["d_wo"]).then_inc(self.late_in, 16)
        sp.dma_start(self.bv[:, :], a["d_bv"]).then_inc(self.late_in, 16)
        sp.dma_start(self.bo[:, :], a["d_bo"].partition_broadcast(P)).then_inc(self.late_in, 16)

        def stack(b, m):
            if not (isinstance(b, int) and b == 0):
                stand(k, sp, self.scored, 8 * (b - 1) + (4 * m + 4))
            stand(k, sp, self.k_roped, 8 * b + (4 * m + 4))
            for j in range(4):
                for r, part in enumerate((0, 0, 1)):
                    sp.dma_start(self.k_stack[32 * r:32 * r + 32, 4 * m + j, :].bitcast(F32),
                                 self.k_split[32 * j:32 * j + 32, part, :].bitcast(F32))\
                        .then_inc(self.stacked[m], 16)

        stack(0, 0)
        stack(0, 1)
        with sp.Fori(0, B // 2 - 1) as i:
            for p in range(2):
                load(2 * i + 2 + p, p)
                stack(2 * i + 1 + p, 0)
                stack(2 * i + 1 + p, 1)
        stack(B - 1, 0)
        stack(B - 1, 1)

    def gpsimd(self, pool):
        k = self.k
        norm_pool(k, pool, self.n)
        if MP > M:
            pool.wait_ge(k.x_done, self.n)
            k.nc.gpsimd.memset(self.k_split[:, :, M:MP].bitcast(F32), 0.0).then_inc(self.padded, 1)
            pool.wait_ge(self.padded, 1)
        pool.wait_ge(self.w_in, 144)
        part = Count(self.k_part)

        def rope(r, g):
            c, w = KB[g % 4]
            raw, swap = self.k_raw[:, g % 2, 0:w], self.k_swap[:, g % 2, 0:w]
            stand(k, pool, self.k_swapped, r + 1)
            part.up(k.nc.gpsimd.tensor_tensor(raw, raw, self.k_rot[:, 0, c:c + w], ALU.mult))
            part.up(k.nc.gpsimd.tensor_tensor(swap, swap, self.k_rot[:, 1, c:c + w], ALU.mult))
            stand(k, pool, self.k_part, part.now())
            if g % 4 == 0 and not (isinstance(r, int) and r == 0):
                stand(k, pool, self.stacked[1 - g // 4], (r + 4) // 8 * self.STACKED if isinstance(r, int) else
                      self.batch * self.STACKED + (self.STACKED if g else 0))
            part.up(k.nc.gpsimd.tensor_tensor(self.k_split[:, 0, c:c + w], raw, swap, ALU.add))
            part.up(k.nc.gpsimd.tensor_tensor(raw, raw, swap, ALU.add))
            stand(k, pool, self.k_part, part.now())
            return k.nc.gpsimd.tensor_tensor(self.k_split[:, 1, c:c + w], raw, self.k_split[:, 0, c:c + w].bitcast(F32),
                                             ALU.subtract)

        for g in range(8):
            rope(g, g).then_inc(self.k_roped, 1)
        with pool.Fori(1, B) as b:
            self.batch = b
            part.restart(32 * b)
            for g in range(8):
                rope(8 * b + g, g).then_inc(self.k_roped, 1)

    def tensor(self, pe):
        norm_tensor(self.k, pe, self.n)
        self.tensor_loop(self.k, pe)

    def pe_before(self, k, pe, fill):
        nc = k.nc
        wait_norm(k, pe, self.n)
        pe.wait_ge(self.w_in, 144)
        for m in range(FC):
            for f in range(FC):
                last = nc.tensor.matmul(k.ps_s[:, m * BANK:(m + 1) * BANK], self.wq[:, f, m * P:(m + 1) * P],
                                        k.xnT[:, f, :], start=(f == 0), stop=(f == FC - 1))
            last.then_inc(self.q_full, 1)
        for kind, g in self.FIRST_FILLS:
            fill(0, kind, 0, g, 0)
        pe.wait_ge(self.q_read, 2)
        pe.wait_ge(self.misc_read, 15)
        pe.wait_ge(self.qm_ready, 4)
        pe.wait_ge(self.stacked[0], self.STACKED)

    def pe_ready(self, k, pe, i, s1, misc):
        b = 2 * i + s1 // 8
        if s1 % 8 == 0:
            stand(k, pe, self.qm_ready, 4 * b + 4)
            stand(k, pe, self.stacked[0], self.STACKED * b + self.STACKED)
        elif s1 % 8 == 4:
            stand(k, pe, self.stacked[1], self.STACKED * b + self.STACKED)

    def pe_scores(self, k, pe, i, s, blocks):
        q = self.q_stack[:, s // 8, s % 8 // 4, s % 4, :, :].rearrange("p a s -> p (a s)")
        for c, w in blocks:
            w += w % 2
            last = k.nc.tensor.matmul(k.ps_s[:, c:c + w], q, self.k_stack[:, s % 8, c:c + w], start=True, stop=True)
        return last

    def pe_misc(self, k, pe, i, kind, *which):
        nc = k.nc
        if kind == "o":
            p = which[0]
            stand(k, pe, self.scaled, 16 * i + (8 if p == 0 else 0))
            return nc.tensor.transpose(k.ps_m[:, 0:P], self.o[:, p, :, :].rearrange("p j d -> p (j d)"), k.ident[:, :])
        p, g, ahead = which
        if kind == "k":
            if g == 0:
                stand(k, pe, self.ctxT_in[p], 16 * (i + ahead // 2 + 1))
            c, w = KB[g % 4]
            m = g // 4
            for f in range(FC):
                last = nc.tensor.matmul(k.ps_m[:, 0:w], self.wk[:, f, m * P:(m + 1) * P], self.ctxT[:, p, f, c:c + w],
                                        start=(f == 0), stop=(f == FC - 1))
            return last
        for j, c in enumerate(range(2 * g, min(2 * g + 2, MC))):
            for f in range(FC):
                last = nc.tensor.matmul(k.ps_m[0:keys(c), j * D:(j + 1) * D], self.ctxT[:, p, f, c * P:c * P + keys(c)],
                                        self.wv[:, f, :], start=(f == 0), stop=(f == FC - 1))
        return last

    def pe_after(self, k, pe, fill, misc):
        nc = k.nc
        self.pe_fold(k, pe, self.G * B - 1)
        fill(B // 2, "o", 1)
        pe.wait_ge(self.misc_read, misc.now())
        pe.wait_ge(self.late_in, 48)
        for t in range(NT):
            for p in range(2):
                last = nc.tensor.matmul(k.ps_s[:, t * BANK:t * BANK + D], self.oT[:, p, t * P:(t + 1) * P],
                                        self.wo[:, p, :], start=(p == 0), stop=(p == 1))
            last.then_inc(k.y_full, 1)

    def scalar(self, act):
        norm_scalar(self.k, act, self.n)
        self.scalar_loop(self.k, act)

    def act_before(self, k, act, read):
        act.wait_ge(self.w_in, 144)
        for m in range(FC):
            act.wait_ge(self.q_full, m + 1)
            k.nc.scalar.activation(self.q_raw[:, m, :], k.ps_s[:, m * BANK:(m + 1) * BANK], ACT.Identity,
                                   bias=self.bq[:, m:m + 1]).then_inc(self.q_read, 1)
        for kind, g in self.FIRST_FILLS:
            read(0, kind, 0, g, 0)

    def act_misc(self, k, act, i, kind, *which):
        nc = k.nc
        if kind == "o":
            b = 2 * i if which[0] == 0 else 2 * i - 1
            if isinstance(i, int):
                act.wait_ge(self.late_in, 48)
            for par in range(2):
                dst = self.oT[:, par, b * S:(b + 1) * S] if isinstance(b, int) else self.oT[:, par, ds(b * S, S)]
                last = nc.scalar.activation(dst, k.ps_m[:, par * S:(par + 1) * S], ACT.Identity,
                                            bias=self.bv[:, par:par + 1])
            return last
        p, g, ahead = which
        if kind == "k":
            c, w = KB[g % 4]
            r = 16 * i + 8 * ahead + g
            if not (isinstance(r, int) and r < 2):
                stand(k, act, self.k_roped, r - 1)
            return nc.scalar.activation(self.k_raw[:, g % 2, 0:w], k.ps_m[:, 0:w], ACT.Identity,
                                        bias=self.bk[:, g // 4:g // 4 + 1])
        n = min(2, MC - 2 * g)
        r = keys(2 * g)
        return nc.scalar.activation(self.v[0:r, p, 2 * g:2 * g + n, :],
                                    k.ps_m[0:r, 0:n * D].rearrange("p (c d) -> p c d", d=D), ACT.Copy)

    def act_after(self, k, act, read):
        read(B // 2, "o", 1)

    def swap(self, k, dve, r, g, index):
        c, w = KB[g % 4]
        stand(k, dve, self.misc_read, index + 1)
        if not (isinstance(r, int) and r < 2):
            stand(k, dve, self.k_roped, r - 1)
        k.nc.vector.stream_shuffle(self.k_swap[:, g % 2, 0:w], self.k_raw[:, g % 2, 0:w], [j ^ 8 for j in range(32)])\
            .then_inc(self.k_swapped, 1)

    def separate(self, k, dve, b, p, j):
        at = slice(b * S, (b + 1) * S) if isinstance(b, int) else ds(b * S, S)
        rows = slice(32 * j, 32 * j + 32)
        for r, q in enumerate((self.q_hi, self.q_lo, self.q_hi)):
            for f in range(FC):
                last = k.nc.vector.tensor_tensor(
                    self.q_stack[32 * r:32 * r + 32, p, f, j, :, :],
                    q[rows, f:f + 1, at].bitcast(F32).to_broadcast([32, 2, S]), self.head_of[rows, :, :], ALU.mult)
        last.then_inc(self.qm_ready, 1)

    def dve_extra(self, k, dve, i, s, first, last):
        if last and s >= 8:
            return
        g, ahead = s % 8, 1 + s // 8
        if g < 4:
            self.separate(k, dve, 2 * i + ahead, 1 - s // 8, g)
        b16 = 32 * i + 16 * (s // 8)
        self.swap(k, dve, 16 * i + 8 * ahead + g, g, b16 + (15 if g == 0 else 14 + 2 * g))

    def dve_scale(self, k, dve, s):
        p, j = s // 8, s % 8
        for par in range(2):
            rows = slice(64 * par, 64 * par + 64)
            last_ = k.nc.vector.tensor_scalar(self.o[rows, p, j, :], k.ps_o[rows, P + 16 * par:P + 16 * par + 16],
                                              self.inv[rows, s % 2:s % 2 + 1], None, ALU.mult)
        return last_

    def vector(self, dve):
        k, v = self.k, self.k.nc.vector
        norm_vector(k, dve, self.n)
        dve.wait_ge(self.w_in, 144)
        def swap(g):
            self.swap(k, dve, g, g, self.FIRST_FILLS.index(("k", g)))

        swap(0)
        swap(1)
        dve.wait_ge(self.q_read, 2)
        swapped = k.xn[:, :, :].rearrange("p t d -> p (t d)")
        raw = self.q_raw[:, :, :].rearrange("p f t -> p (f t)")
        link(k, dve, v.stream_shuffle(swapped, raw, [j ^ 8 for j in range(32)]))
        for tile, j in ((raw, 0), (swapped, 1)):
            view = tile.rearrange("p (b s) -> p b s", s=S)
            last = v.tensor_tensor(view, view, self.q_rot[:, j:j + 1, :].to_broadcast([P, FC * B, S]), ALU.mult)
        link(k, dve, last)
        swap(2)
        link(k, dve, v.tensor_tensor(raw, raw, swapped, ALU.add))
        link(k, dve, v.tensor_copy(self.q_hi[:, :, :], self.q_raw[:, :, :]))
        link(k, dve, v.tensor_tensor(self.q_lo[:, :, :], self.q_raw[:, :, :], self.q_hi[:, :, :].bitcast(F32), ALU.subtract))
        swap(3)
        for j in range(4):
            self.separate(k, dve, 0, 0, j)
            swap(4 + j)
        self.vector_loop(k, dve)
        dve.wait_ge(self.late_in, 48)
        finish(k, dve, lambda t: self.bo[:, :], lambda t: k.ps_s[:, t * BANK:t * BANK + D], self.n)


class StageE:

    H, DH = 8, 32

    def __init__(self, k, n):
        self.k, self.n = k, n
        sem = k.sem
        with ExitStack() as st:
            sb = lambda name, shape, dt=F32: k.sb("e_" + name, shape, dt, st)
            self.wqk = sb("wqk", [P, FC, 2 * D])
            self.bqk = sb("bqk", [P, 4])
            self.wvu = sb("wvu", [P, FC, 2 * D])
            self.bvu = sb("bvu", [P, 2 * D])
            self.scale = sb("scale", [P, D])
            self.wo = sb("wo", [P, FC, D])
            self.bo = sb("bo", [P, D])
            self.causal = sb("causal", [P, 1, 1, S])
            self.low = sb("low", [P, 4, T])
            self.high = sb("high", [P, 4, T])
            self.qk = sb("qk", [P, 4, T])
            self.vu = sb("vu", [P, NT, 2 * D])
            self.energy = sb("energy", [P, 2, 4, 2, S])
            self.o = sb("o", [P, NT, D])
            self.sq = sb("sq", [P, D])
            self.ss = sb("ss", [P, NT])
            self.inv = sb("inv", [P, NT])
            self.oT = sb("oT", [P, FC, T])
        self.w_in = sem("e_w_in")
        self.qk_full = sem("e_qk_full")
        self.low_ready = sem("e_low_ready")
        self.exped = sem("e_exped")
        self.qk_ready = sem("e_qk_ready")
        self.vu_full = sem("e_vu_full")
        self.vu_raw = sem("e_vu_raw")
        self.vu_ready = sem("e_vu_ready")
        self.e_full = sem("e_e_full")
        self.e_ready = sem("e_e_ready")
        self.o_full = sem("e_o_full")
        self.o_ready = sem("e_o_ready")
        self.ss_done = sem("e_ss_done")
        self.rooted = sem("e_rooted")
        self.gated = sem("e_gated")
        self.turned = sem("e_turned")
        self.oT_done = sem("e_oT_done")

    def sync(self, sp):
        k, a = self.k, self.k.a
        sp.wait_ge(k.x_done, self.n)
        for name, tile in (("wqk", self.wqk), ("bqk", self.bqk), ("wvu", self.wvu), ("wo", self.wo),
                           ("causal", self.causal)):
            sp.dma_start(tile[...], a["e_" + name]).then_inc(self.w_in, 16)
        for name, tile in (("bvu", self.bvu), ("scale", self.scale), ("bo", self.bo)):
            sp.dma_start(tile[:, :], a["e_" + name].partition_broadcast(P)).then_inc(self.w_in, 16)

    def gpsimd(self, pool):
        norm_pool(self.k, pool, self.n)

    def tensor(self, pe):
        k, nc = self.k, self.k.nc
        norm_tensor(k, pe, self.n)
        wait_norm(k, pe, self.n)
        pe.wait_ge(self.w_in, 128)
        for m in range(4):
            for f in range(FC):
                last = nc.tensor.matmul(k.ps_s[:, m * BANK:(m + 1) * BANK], self.wqk[:, f, m * P:(m + 1) * P],
                                        k.xnT[:, f, :], start=(f == 0), stop=(f == FC - 1))
            last.then_inc(self.qk_full, 1)
        banks = (k.ps_m, k.ps_o)
        for t in range(NT):
            if t >= 2:
                pe.wait_ge(self.vu_raw, t - 1)
            for f in range(FC):
                last = nc.tensor.matmul(banks[t % 2][:, :], k.xnT[:, f, t * P:(t + 1) * P], self.wvu[:, f, :],
                                        start=(f == 0), stop=(f == FC - 1))
            last.then_inc(self.vu_full, 1)
        pe.wait_ge(self.qk_ready, 4)

        def energies(t):
            for par in range(2):
                tok = slice(t * P + par * S, t * P + (par + 1) * S)
                for h in range(8):
                    q, at = h % 4, (2 * t + h // 4) * S
                    rows = slice(32 * q, 32 * q + 32)
                    last = nc.tensor.matmul(k.ps_s[64 * par:64 * par + 64, q * BANK + at:q * BANK + at + S],
                                            self.qk[rows, 2 + h // 4, tok], self.qk[rows, h // 4, tok],
                                            start=True, stop=True)
            last.then_inc(self.e_full, 1)

        pe.wait_ge(self.vu_raw, NT)
        for t in range(NT):
            energies(t)
        for t in range(NT):
            pe.wait_ge(self.e_ready, t + 1)
            pe.wait_ge(self.vu_ready, t + 1)
            if t >= 2:
                pe.wait_ge(self.o_ready, t - 1)
            for par in range(2):
                rows = slice(64 * par, 64 * par + 64)
                for h in range(8):
                    last = nc.tensor.matmul(banks[t % 2][rows, h * 32:(h + 1) * 32], self.energy[rows, t % 2, h % 4, h // 4, :],
                                            self.vu[rows, t, h * 32:(h + 1) * 32], start=True, stop=True)
            last.then_inc(self.o_full, 1)
        for f in range(FC):
            for t in range(NT):
                if f == 0:
                    pe.wait_ge(self.gated, t + 1)
                last = nc.tensor.transpose(k.ps_t[:, f, t * P:(t + 1) * P], self.o[:, t, f * P:(f + 1) * P], k.ident[:, :])
            last.then_inc(self.turned, 1)
        pe.wait_ge(self.oT_done, 2)
        for t in range(NT):
            for f in range(FC):
                last = nc.tensor.matmul(k.ps_s[:, t * BANK:t * BANK + D], self.oT[:, f, t * P:(t + 1) * P],
                                        self.wo[:, f, :], start=(f == 0), stop=(f == FC - 1))
            last.then_inc(k.y_full, 1)

    def scalar(self, act):
        k, nc = self.k, self.k.nc
        norm_scalar(k, act, self.n)
        for m in range(4):
            act.wait_ge(self.low_ready, m + 1)
            nc.scalar.activation(self.low[:, m, :], self.low[:, m, :], ACT.Exp).then_inc(self.exped, 1)
        for t in range(NT):
            act.wait_ge(self.vu_raw, t + 1)
            nc.scalar.activation(self.vu[:, t, :], self.vu[:, t, :], ACT.Silu).then_inc(self.vu_ready, 1)
        for t in range(NT):
            act.wait_ge(self.o_ready, t + 1)
            if t:
                act.wait_ge(self.ss_done, t)
            nc.scalar.activation(self.sq[:, :], self.o[:, t, :], ACT.Square, accum_out=self.ss[:, t:t + 1])\
                .then_inc(self.ss_done, 1)
        act.wait_ge(self.ss_done, NT)
        nc.scalar.activation(self.ss[:, :], self.ss[:, :], ACT.Sqrt, scale=1.0 / D).then_inc(self.rooted, 1)
        for f in range(FC):
            act.wait_ge(self.turned, f + 1)
            nc.scalar.activation(self.oT[:, f, :], k.ps_t[:, f, :], ACT.Copy).then_inc(self.oT_done, 1)

    def vector(self, dve):
        k, v = self.k, self.k.nc.vector
        norm_vector(k, dve, self.n)
        dve.wait_ge(self.w_in, 128)
        banks = (k.ps_m, k.ps_o)
        for m in range(4):
            dve.wait_ge(self.qk_full, m + 1)
            bank = k.ps_s[:, m * BANK:(m + 1) * BANK]
            v.tensor_scalar(self.low[:, m, :], bank, self.bqk[:, m:m + 1], 0.0, ALU.add, ALU.min).then_inc(self.low_ready, 1)
            last = v.tensor_scalar(self.high[:, m, :], bank, self.bqk[:, m:m + 1], 0.0, ALU.add, ALU.max)
        link(k, dve, last)
        for m in range(4):
            dve.wait_ge(self.exped, m + 1)
            v.scalar_tensor_tensor(self.qk[:, m, :], self.low[:, m, :], -1.0, self.high[:, m, :], ALU.add, ALU.add)\
                .then_inc(self.qk_ready, 1)
        for t in range(NT):
            dve.wait_ge(self.vu_full, t + 1)
            v.tensor_tensor(self.vu[:, t, :], banks[t % 2][:, :], self.bvu[:, :], ALU.add).then_inc(self.vu_raw, 1)
        for t in range(NT):
            dve.wait_ge(self.e_full, NT)
            if t >= 2:
                dve.wait_ge(self.o_full, t - 1)
            v.tensor_tensor(self.energy[:, t % 2, :, :, :],
                            k.ps_s[:, :].rearrange("p (q t c s) -> p q t c s", q=4, t=NT, c=2)[:, :, t, :, :],
                            self.causal[:, :, :, :].to_broadcast([P, 4, 2, S]), ALU.mult).then_inc(self.e_ready, 1)
            dve.wait_ge(self.o_full, t + 1)
            v.tensor_copy(self.o[:, t, :], banks[t % 2][:, 0:D]).then_inc(self.o_ready, 1)
        dve.wait_ge(self.rooted, 1)
        link(k, dve, v.tensor_scalar(self.ss[:, :], self.ss[:, :], 1e-8, None, ALU.add))
        link(k, dve, v.reciprocal(self.inv[:, :], self.ss[:, :]))
        dve.wait_ge(self.vu_ready, NT)
        for t in range(NT):
            link(k, dve, v.scalar_tensor_tensor(self.o[:, t, :], self.o[:, t, :], self.inv[:, t:t + 1], self.scale[:, :],
                                                ALU.mult, ALU.mult))
            v.tensor_tensor(self.o[:, t, :], self.o[:, t, :], self.vu[:, t, D:2 * D], ALU.mult).then_inc(self.gated, 1)
        finish(k, dve, lambda t: self.bo[:, :], lambda t: k.ps_s[:, t * BANK:t * BANK + D], self.n)


class StageF(Experts):

    HC, LAG, RING = 6, 1, 2
    ROUTED = 7
    I = HC * P
    WEIGHTS, WIDE = "f_w", 2 * FC * HC * P + HC * D

    def __init__(self, k, n):
        self.k, self.n = k, n
        with ExitStack() as st:
            sb = lambda name, shape, dt=F32: k.sb("f_" + name, shape, dt, st)
            self.experts_memory(k, sb, "f_")
            self.wr = sb("wr", [P, FC, 8])
            self.rb = sb("rb", [P, 1, 7])
            self.sg = sb("sg", [P, 2, T])
            self.su = sb("su", [P, 2, T])
            self.gated = k.sem("f_gated")

    def sync(self, sp):
        k, a = self.k, self.k.a
        sp.wait_ge(k.x_done, self.n)
        sp.dma_start(self.wr[:, :, 0:7], a["f_wr"]).then_inc(self.router_in, 16)
        sp.dma_start(self.rb[:, 0, :], a["f_rb"].partition_broadcast(P)).then_inc(self.router_in, 16)
        self.sync_experts(k, sp)

    def tensor(self, pe):
        k, nc = self.k, self.k.nc
        norm_tensor(k, pe, self.n)
        wait_norm(k, pe, self.n)
        pe.wait_ge(self.router_in, 32)
        for t in range(NT):
            for f in range(FC):
                last = nc.tensor.matmul(k.ps_m[:, t * 8:t * 8 + 7], k.xnT[:, f, t * P:(t + 1) * P], self.wr[:, f, 0:7],
                                        start=(f == 0), stop=(f == FC - 1))
        last.then_inc(self.logits_full, 1)
        self.tensor_begin(k, pe)
        self.spread(k, pe)
        self.tensor_experts(k, pe, False)

    def pe_first(self, k, pe, e, c, r):
        for j in range(2):
            for f in range(FC):
                last = self.three(k, k.ps_s[:, (2 * r + j) * BANK:(2 * r + j + 1) * BANK], e,
                                  (j * FC + f) * self.I + c * P, self.x_hi[:, f, :], self.x_lo[:, f, :],
                                  f == 0, f == FC - 1)
        return last

    def second_column(self, c, f):
        return 2 * FC * self.I + c * D + f * P

    def unweighted(self, u):
        return self.su[:, u % 2, :]

    def scalar(self, act):
        k, nc = self.k, self.k.nc
        norm_scalar(k, act, self.n)
        act.wait_ge(self.e_in[0], 16)
        for c in range(self.PIECES):
            self.split_high(k, act, 0, 0, c)
        act.wait_ge(self.gapped, self.R + 1)
        nc.scalar.activation(self.second[:, :], self.gap[:, :], ACT.Exp).then_inc(self.second_done, 1)
        self.act_spread(k, act)
        self.scalar_experts(k, act)

    def act_unit(self, k, act, e, c, r):
        return k.nc.scalar.activation(self.sg[:, r, :], k.ps_s[:, 2 * r * BANK:(2 * r + 1) * BANK], ACT.Silu)

    def dve_unit(self, k, dve, u, n):
        r = u % 2
        k.nc.vector.tensor_tensor(self.su[:, r, :], self.sg[:, r, :],
                                  k.ps_s[:, (2 * r + 1) * BANK:(2 * r + 2) * BANK], ALU.mult).then_inc(self.gated, 1)
        stand(k, dve, self.gated, n + 1)

    def vector(self, dve):
        k = self.k
        norm_vector(k, dve, self.n)
        self.split_x(k, dve)
        dve.wait_ge(self.router_in, 32)
        self.choose(k, dve, self.rb[:, :, :])
        self.vector_experts(k, dve)
        finish(k, dve, None, lambda t: k.ps_s[:, t * BANK:t * BANK + D], self.n)


def finish(k, dve, bias, y, n):
    for t in range(NT):
        if bias is not None:
            link(k, dve, k.nc.vector.tensor_tensor(k.x[:, t, :], k.x[:, t, :], bias(t), ALU.add))
        dve.wait_ge(k.y_full, NT * n + t + 1)
        link(k, dve, k.nc.vector.tensor_tensor(k.x[:, t, :], k.x[:, t, :], y(t), ALU.add))
    dve.nop().then_inc(k.x_done, 1)


def rotary(length):
    import numpy as np
    f = np.float32
    inv_freq = f(1.0) / np.power(f(10000.0), np.arange(0, 16, 2, dtype=f) / f(16))
    angle = np.outer(f(10.0) * (np.arange(length, dtype=f) / f(length)), inv_freq).astype(f)
    cos, sin = np.cos(angle).T, np.sin(angle).T
    rows = np.stack([np.concatenate([cos, cos]), np.concatenate([-sin, sin])], axis=1)
    return np.ascontiguousarray(np.tile(rows, (8, 1, 1)).astype(f))


def head_rows():
    import numpy as np
    odd = np.arange(P)[:, None] // 16 % 2
    rows = np.where(odd == np.arange(2)[None], StageD.SCALE, 0.0).astype(np.float32)
    return np.repeat(rows[:, :, None], S, axis=2)


def layouts(inp):
    import numpy as np
    g = {n: np.asarray(v) for n, v in inp.items()}
    chunk = lambda w: np.ascontiguousarray(w.reshape(-1, P, w.shape[-1]).transpose(1, 0, 2))
    o = {"x": g["x"], "ctx_1024": g["ctx_1024"]}
    o["ctxT"] = np.ascontiguousarray(g["ctx_1024"].transpose(0, 2, 1).reshape(B, FC, P, M).transpose(0, 2, 1, 3))
    o["a_wq"] = chunk(g["L0_xattn_Wq"])
    wk = g["L0_xattn_Wk"].T.reshape(8, 64, D).transpose(1, 0, 2)
    o["a_wkT"] = np.ascontiguousarray(np.pad(wk, ((0, 64), (0, 0), (0, 0))))
    o["a_wv"] = chunk(g["L0_xattn_Wv"])
    o["a_wo"] = chunk(g["L0_xattn_Wo"])
    o["a_bo"] = g["L0_xattn_bo"]
    head = lambda w: w.reshape(w.shape[:-1] + (16, 16))
    c = g["L0_attn_ctrl_W"]
    cb = g["L0_attn_ctrl_b"][None]

    def interleave(w):
        q, kk, v, dec, bet, gate = np.split(w, [256, 512, 768, 784, 800], axis=-1)
        return np.concatenate([np.concatenate([head(q), head(kk), head(v), bet[..., None], dec[..., None]], -1)
                               .reshape(len(w), 800), gate], -1)
    o["b_ctl"] = chunk(interleave(c))
    o["b_ctl_b"] = interleave(cb)[0]
    halves = lambda w: np.concatenate([w[..., 0::2], w[..., 1::2]], -1)
    o["b_cin"] = chunk(halves(g["L0_attn_cond_in_W"]))
    dw = halves(g["L0_attn_delta_W"].T).T
    q, kk, v, bet = np.split(dw, [256, 512, 768], axis=-1)
    o["b_delta"] = np.ascontiguousarray(np.concatenate([head(q), head(kk), head(v), bet[..., None]], -1))
    r = g["L0_attn_qkv_ramp_logit"]
    o["b_ramp"] = np.ascontiguousarray(np.concatenate(
        [head(r[0]), head(r[1]), head(r[2]), g["L0_attn_beta_ramp_logit"][:, None]], -1))
    o["b_theta"] = g["L0_attn_rot_theta"][:, None]
    o["b_norm_w"] = np.ascontiguousarray(g["L0_attn_cond_norm_w"].reshape(64, 2))
    cw = np.stack([g["L0_attn_q_conv_w"], g["L0_attn_k_conv_w"], g["L0_attn_v_conv_w"]])
    cw = cw.reshape(3, 16, 16, 4).transpose(1, 3, 0, 2).reshape(16, 4, 48)
    o["b_conv_w"] = np.ascontiguousarray(np.concatenate([cw] * B))
    o["b_o_w"] = g["L0_attn_out_norm_w"]
    o["b_wo"] = chunk(g["L0_attn_out_proj_W"].T)
    o["b_bo"] = g["L0_attn_out_proj_b"]
    o["c_rw1"] = chunk(g["L0_ffn_rw1"])
    o["c_rb1"] = np.ascontiguousarray(g["L0_ffn_rb1"].reshape(FC, P).T)
    o["c_rw2"] = chunk(g["L0_ffn_rw2"])
    o["c_rb2"] = g["L0_ffn_rb2"]
    o["c_b1"] = np.ascontiguousarray(g["L0_ffn_eb1"].reshape(8, 4, P).transpose(2, 0, 1))
    o["c_b2"] = g["L0_ffn_eb2"]
    w1 = g["L0_ffn_ew1"].reshape(8, FC, P, 512).transpose(0, 2, 1, 3).reshape(8, P, FC * 512)
    w2 = g["L0_ffn_ew2"].reshape(8, 4, P, D).transpose(0, 2, 1, 3).reshape(8, P, 4 * D)
    o["c_w"] = np.ascontiguousarray(np.concatenate([w1, w2], -1))
    o["f_wr"] = chunk(g["L1_ffn_wr"].T)
    o["f_rb"] = g["L1_ffn_rb"]
    parts = []
    for m in "gu":
        w = np.concatenate([g["L1_ffn_r" + m], g["L1_ffn_s" + m][None]])
        w = np.pad(w, ((0, 0), (0, StageF.I - 704), (0, 0))).transpose(0, 2, 1)
        parts.append(w.reshape(8, FC, P, StageF.I).transpose(0, 2, 1, 3).reshape(8, P, FC * StageF.I))
    w = np.concatenate([g["L1_ffn_rd"], g["L1_ffn_sd"][None]])
    w = np.pad(w, ((0, 0), (0, 0), (0, StageF.I - 704))).transpose(0, 2, 1)
    parts.append(w.reshape(8, StageF.HC, P, D).transpose(0, 2, 1, 3).reshape(8, P, StageF.HC * D))
    o["f_w"] = np.ascontiguousarray(np.concatenate(parts, -1))
    wt = lambda n: chunk(g[n].T)
    col = lambda v: np.ascontiguousarray(v.reshape(-1, P).T)
    o["d_wq"], o["d_wk"], o["d_wv"] = wt("L1_xattn_Wq"), wt("L1_xattn_Wk"), wt("L1_xattn_Wv")
    o["d_bq"], o["d_bk"] = col(g["L1_xattn_bq"]), col(g["L1_xattn_bk"])
    pair = lambda w: w.reshape((8, 2, 16) + w.shape[1:])
    o["d_wo"] = np.ascontiguousarray(pair(g["L1_xattn_Wo"].T).transpose(0, 2, 1, 3).reshape(P, 2, D))
    o["d_bv"] = np.ascontiguousarray(pair(g["L1_xattn_bv"]).transpose(0, 2, 1).reshape(P, 2))
    o["d_bo"] = g["L1_xattn_bo"]
    o["d_fold"] = np.tile(np.eye(32, dtype=np.float32), (4, 1))
    o["d_q_rot"], o["d_k_rot"], o["d_head_of"] = rotary(S), rotary(M), head_rows()
    e = lambda n, m: chunk(np.concatenate([g["L1_attn_" + n], g["L1_attn_" + m]]).T)
    o["e_wqk"], o["e_wvu"], o["e_wo"] = e("Wq", "Wk"), e("Wv", "Wu"), wt("L1_attn_Wo")
    o["e_bqk"] = col(np.concatenate([g["L1_attn_bq"], g["L1_attn_bk"]]))
    o["e_bvu"] = np.concatenate([g["L1_attn_bv"], g["L1_attn_bu"]])
    o["e_scale"], o["e_bo"] = g["L1_attn_scale"], g["L1_attn_bo"]
    o["e_causal"] = np.ascontiguousarray(np.tile(np.triu(np.ones((S, S), np.float32)), (2, 1)).reshape(P, 1, 1, S))
    return o


def kernel(**inputs):
    import numpy as np
    import concourse.bacc as bacc
    from concourse.bass_utils import run_bass_kernel_spmd as run

    nc = bacc.Bacc("TRN2", target_bir_lowering=False, num_devices=1)
    arrays = {n + "_dram": np.ascontiguousarray(v) for n, v in layouts(inputs).items()}
    aps = {n[:-5]: nc.dram_tensor(n, v.shape, mybir.dt.from_np(v.dtype), kind="ExternalInput").ap()
           for n, v in arrays.items()}
    out = nc.dram_tensor("out_dram", (B, S, D), F32, kind="ExternalOutput").ap()
    build(nc, aps, out)
    r = run(nc, [arrays], core_ids=[0])
    return r.results[0]["out_dram"]
```
